# Optimizing a Trainium2 kernel written in Bass

```python
import numpy as np
import jax
import jax.numpy as jnp

def _softmax(x, axis=-1):
    return jax.nn.softmax(x, axis=axis)
def _gelu(x):
    return jax.nn.gelu(x, approximate=True)
def _silu(x):
    return jax.nn.silu(x)
def _sigmoid(x):
    return jax.nn.sigmoid(x)
def _layernorm(x, axis=-1, eps=1e-5):
    m = jnp.mean(x, axis=axis, keepdims=True)
    v = jnp.var(x, axis=axis, keepdims=True)
    return (x - m) / jnp.sqrt(v + eps)
def _scatter_add(tgt, idx, src, axis=0):
    return tgt.at[idx].add(src)
def _segment_sum(src, seg, n):
    return jax.ops.segment_sum(src, seg, n)

kernel_name = 'mk_conv_attn_hybrid_d2_conv_nhwc256_c996b6'

def setup_inputs(seed: int = 0):
    np.random.seed(seed)
    _w = jnp.asarray
    def _rec_inputs():
        import jax
        import jax.numpy as jnp
        _gk = jax.random.key(seed)
        x = -0.0005207 + 1.001 * jax.random.normal(jax.random.fold_in(_gk, 1), (2, 64, 64, 256), jnp.float32)
        return x
    x = _rec_inputs()
    def _L0_conv_setup():
        import jax, jax.numpy as jnp
        import numpy as np
        from jax import lax
        B, H, W, C, G, K = (2, 64, 64, 256, 8, 9)
        CQ = C // 4
        HC = C // G
        PTS = np.array([[-1, -1], [-1, 0], [-1, 1], [0, -1], [0, 0], [0, 1], [1, -1], [1, 0], [1, 1]], np.float32)

        def _dwconv_nhwc(x, w, b):
            ch = x.shape[-1]
            y = lax.conv_general_dilated(x, w, (1, 1), 'SAME', dimension_numbers=('NHWC', 'HWIO', 'NHWC'), feature_group_count=ch)
            return y + b

        def _pconv_nchw(x, w):
            dc = w.shape[0]
            x1 = lax.conv_general_dilated(x[:, :dc], w, (1, 1), 'SAME', dimension_numbers=('NCHW', 'OIHW', 'NCHW'))
            return jnp.concatenate([x1, x[:, dc:]], axis=1)

        def _flow_warp(x, flow):
            N, Cc, Hh, Ww = x.shape
            Kk = flow.shape[1] // 2
            fl = flow.reshape(N, Kk, 2, Hh, Ww).transpose(0, 3, 4, 1, 2)
            gy, gx = jnp.meshgrid(jnp.arange(Hh, dtype=x.dtype), jnp.arange(Ww, dtype=x.dtype), indexing='ij')
            base = jnp.stack([gx, gy], axis=-1)
            coords = base[None, :, :, None, :] + fl
            cx = jnp.clip(coords[..., 0], 0.0, Ww - 1)
            cy = jnp.clip(coords[..., 1], 0.0, Hh - 1)
            x0 = jnp.floor(cx)
            y0 = jnp.floor(cy)
            wx = (cx - x0).reshape(N, 1, -1)
            wy = (cy - y0).reshape(N, 1, -1)
            x0i = x0.astype(jnp.int32)
            y0i = y0.astype(jnp.int32)
            x1i = jnp.minimum(x0i + 1, Ww - 1)
            y1i = jnp.minimum(y0i + 1, Hh - 1)
            xf = x.reshape(N, Cc, Hh * Ww)

            def gather(yi, xi):
                idx = (yi * Ww + xi).reshape(N, -1)
                return jax.vmap(lambda im, ix: im[:, ix])(xf, idx)
            v00 = gather(y0i, x0i)
            v01 = gather(y0i, x1i)
            v10 = gather(y1i, x0i)
            v11 = gather(y1i, x1i)
            out = v00 * (1 - wx) * (1 - wy) + v01 * wx * (1 - wy) + v10 * (1 - wx) * wy + v11 * wx * wy
            return out.reshape(N, Cc, Hh, Ww, Kk).transpose(0, 1, 4, 2, 3)
        key = jax.random.key(seed)
        ks = jax.random.split(key, 13)
        n = lambda i, shp, s: jax.random.normal(ks[i], shp, jnp.float32) * s
        return {'x': jax.random.normal(ks[0], (B, H, W, C), jnp.float32), 'qkv_w': n(1, (C, 3 * C), C ** (-0.5)), 'qkv_b': n(2, (3 * C,), 0.02), 'dw_w': n(3, (3, 3, 1, 3 * C), 1.0 / 3.0), 'dw_b': n(4, (3 * C,), 0.02), 'off_pconv_w': n(5, (G, CQ, CQ, 3, 3), (CQ * 9) ** (-0.5)), 'off_w': n(6, (G, 2 * K, C), 0.1 * C ** (-0.5)), 'off_b': n(7, (G, 2 * K), 0.1), 'mask_pconv_w': n(8, (CQ, CQ, 3, 3), (CQ * 9) ** (-0.5)), 'mask_w': n(9, (K, C), C ** (-0.5)), 'mask_b': n(10, (K,), 0.02), 'proj_w': n(11, (C, C), C ** (-0.5)), 'proj_b': n(12, (C,), 0.02)}
    _L0_conv_all = _L0_conv_setup()
    _L0_conv_in = {k: v for k, v in _L0_conv_all.items() if k in ('qkv_w', 'qkv_b', 'dw_w', 'dw_b', 'off_pconv_w', 'off_w', 'off_b', 'mask_pconv_w', 'mask_w', 'mask_b', 'proj_w', 'proj_b', )}
    del _L0_conv_all

    def _L1_attn_setup():
        import jax, jax.numpy as jnp
        import numpy as np
        from jax import lax
        NUM_HEADS = 8
        HEAD_DIM = 32

        def conv1d_same(x, w, b):
            y = lax.conv_general_dilated(x, w, window_strides=(1,), padding='SAME', dimension_numbers=('NWC', 'WIO', 'NWC'))
            return y + b
        key = jax.random.key(seed)
        ks = jax.random.split(key, 9)
        B, T, C = (8, 2048, 256)
        K = 3
        s = 1.0 / np.sqrt(K * C)
        return {'x': jax.random.normal(ks[0], (B, T, C), dtype=jnp.float32), 'Wq': jax.random.normal(ks[1], (K, C, C), dtype=jnp.float32) * s, 'bq': jnp.zeros((C,), dtype=jnp.float32), 'Wk': jax.random.normal(ks[2], (K, C, C), dtype=jnp.float32) * s, 'bk': jnp.zeros((C,), dtype=jnp.float32), 'Wv': jax.random.normal(ks[3], (K, C, C), dtype=jnp.float32) * s, 'bv': jnp.zeros((C,), dtype=jnp.float32), 'Wo': jax.random.normal(ks[4], (K, C, C), dtype=jnp.float32) * s, 'bo': jnp.zeros((C,), dtype=jnp.float32)}
    _L1_attn_all = _L1_attn_setup()
    _L1_attn_in = {k: v for k, v in _L1_attn_all.items() if k in ('Wq', 'bq', 'Wk', 'bk', 'Wv', 'bv', 'Wo', 'bo', )}
    del _L1_attn_all

    def _L1_ffn_setup():
        import math
        import jax, jax.numpy as jnp
        import numpy as np
        CAPACITY_FACTOR = 1.25
        key = jax.random.key(seed)
        ks = jax.random.split(key, 5)
        B, L, D, F, E = (8, 8192, 256, 1024, 8)
        h = jax.random.normal(ks[0], (B, L, D), dtype=jnp.float32)
        gate_w = jax.random.normal(ks[1], (D, E), dtype=jnp.float32) * 0.02
        gate_b = jnp.zeros((E,), dtype=jnp.float32)
        w1 = jax.random.normal(ks[2], (E, D, F), dtype=jnp.float32) * (1.0 / math.sqrt(D))
        b1 = jnp.zeros((E, F), dtype=jnp.float32)
        w2 = jax.random.normal(ks[3], (E, F, D), dtype=jnp.float32) * (1.0 / math.sqrt(F))
        b2 = jnp.zeros((E, D), dtype=jnp.float32)
        return {'h': h, 'gate_w': gate_w, 'gate_b': gate_b, 'w1': w1, 'b1': b1, 'w2': w2, 'b2': b2}
    _L1_ffn_all = _L1_ffn_setup()
    _L1_ffn_in = {k: v for k, v in _L1_ffn_all.items() if k in ('gate_w', 'gate_b', 'w1', 'b1', 'w2', 'b2', )}
    del _L1_ffn_all

    return {
        "x": x,
        "L0_conv_qkv_w": _L0_conv_in["qkv_w"],
        "L0_conv_qkv_b": _L0_conv_in["qkv_b"],
        "L0_conv_dw_w": _L0_conv_in["dw_w"],
        "L0_conv_dw_b": _L0_conv_in["dw_b"],
        "L0_conv_off_pconv_w": _L0_conv_in["off_pconv_w"],
        "L0_conv_off_w": _L0_conv_in["off_w"],
        "L0_conv_off_b": _L0_conv_in["off_b"],
        "L0_conv_mask_pconv_w": _L0_conv_in["mask_pconv_w"],
        "L0_conv_mask_w": _L0_conv_in["mask_w"],
        "L0_conv_mask_b": _L0_conv_in["mask_b"],
        "L0_conv_proj_w": _L0_conv_in["proj_w"],
        "L0_conv_proj_b": _L0_conv_in["proj_b"],
        "L1_attn_Wq": _L1_attn_in["Wq"],
        "L1_attn_bq": _L1_attn_in["bq"],
        "L1_attn_Wk": _L1_attn_in["Wk"],
        "L1_attn_bk": _L1_attn_in["bk"],
        "L1_attn_Wv": _L1_attn_in["Wv"],
        "L1_attn_bv": _L1_attn_in["bv"],
        "L1_attn_Wo": _L1_attn_in["Wo"],
        "L1_attn_bo": _L1_attn_in["bo"],
        "L1_ffn_gate_w": _L1_ffn_in["gate_w"],
        "L1_ffn_gate_b": _L1_ffn_in["gate_b"],
        "L1_ffn_w1": _L1_ffn_in["w1"],
        "L1_ffn_b1": _L1_ffn_in["b1"],
        "L1_ffn_w2": _L1_ffn_in["w2"],
        "L1_ffn_b2": _L1_ffn_in["b2"],
    }

def reference(x, L0_conv_qkv_w, L0_conv_qkv_b, L0_conv_dw_w, L0_conv_dw_b, L0_conv_off_pconv_w, L0_conv_off_w, L0_conv_off_b, L0_conv_mask_pconv_w, L0_conv_mask_w, L0_conv_mask_b, L0_conv_proj_w, L0_conv_proj_b, L1_attn_Wq, L1_attn_bq, L1_attn_Wk, L1_attn_bk, L1_attn_Wv, L1_attn_bv, L1_attn_Wo, L1_attn_bo, L1_ffn_gate_w, L1_ffn_gate_b, L1_ffn_w1, L1_ffn_b1, L1_ffn_w2, L1_ffn_b2):
    import jax
    import jax.numpy as jnp
    def _L0_conv_ref(x, qkv_w, qkv_b, dw_w, dw_b, off_pconv_w, off_w, off_b, mask_pconv_w, mask_w, mask_b, proj_w, proj_b):
        import jax, jax.numpy as jnp
        import numpy as np
        from jax import lax
        B, H, W, C, G, K = (2, 64, 64, 256, 8, 9)
        CQ = C // 4
        HC = C // G
        PTS = np.array([[-1, -1], [-1, 0], [-1, 1], [0, -1], [0, 0], [0, 1], [1, -1], [1, 0], [1, 1]], np.float32)

        def _dwconv_nhwc(x, w, b):
            ch = x.shape[-1]
            y = lax.conv_general_dilated(x, w, (1, 1), 'SAME', dimension_numbers=('NHWC', 'HWIO', 'NHWC'), feature_group_count=ch)
            return y + b

        def _pconv_nchw(x, w):
            dc = w.shape[0]
            x1 = lax.conv_general_dilated(x[:, :dc], w, (1, 1), 'SAME', dimension_numbers=('NCHW', 'OIHW', 'NCHW'))
            return jnp.concatenate([x1, x[:, dc:]], axis=1)

        def _flow_warp(x, flow):
            N, Cc, Hh, Ww = x.shape
            Kk = flow.shape[1] // 2
            fl = flow.reshape(N, Kk, 2, Hh, Ww).transpose(0, 3, 4, 1, 2)
            gy, gx = jnp.meshgrid(jnp.arange(Hh, dtype=x.dtype), jnp.arange(Ww, dtype=x.dtype), indexing='ij')
            base = jnp.stack([gx, gy], axis=-1)
            coords = base[None, :, :, None, :] + fl
            cx = jnp.clip(coords[..., 0], 0.0, Ww - 1)
            cy = jnp.clip(coords[..., 1], 0.0, Hh - 1)
            x0 = jnp.floor(cx)
            y0 = jnp.floor(cy)
            wx = (cx - x0).reshape(N, 1, -1)
            wy = (cy - y0).reshape(N, 1, -1)
            x0i = x0.astype(jnp.int32)
            y0i = y0.astype(jnp.int32)
            x1i = jnp.minimum(x0i + 1, Ww - 1)
            y1i = jnp.minimum(y0i + 1, Hh - 1)
            xf = x.reshape(N, Cc, Hh * Ww)

            def gather(yi, xi):
                idx = (yi * Ww + xi).reshape(N, -1)
                return jax.vmap(lambda im, ix: im[:, ix])(xf, idx)
            v00 = gather(y0i, x0i)
            v01 = gather(y0i, x1i)
            v10 = gather(y1i, x0i)
            v11 = gather(y1i, x1i)
            out = v00 * (1 - wx) * (1 - wy) + v01 * wx * (1 - wy) + v10 * (1 - wx) * wy + v11 * wx * wy
            return out.reshape(N, Cc, Hh, Ww, Kk).transpose(0, 1, 4, 2, 3)
        Bb, Hh, Ww, Cc = x.shape
        P = Hh * Ww
        scale = HC ** (-0.5)
        qkv = x @ qkv_w + qkv_b
        qkv = _dwconv_nhwc(qkv, dw_w, dw_b)
        q = qkv[..., :Cc]
        k_map = jnp.transpose(qkv[..., Cc:2 * Cc], (0, 3, 1, 2))
        v_map = jnp.transpose(qkv[..., 2 * Cc:], (0, 3, 1, 2))
        q_nchw = jnp.transpose(q, (0, 3, 1, 2))
        xm = _pconv_nchw(q_nchw, mask_pconv_w)
        mask = jnp.einsum('bchw,oc->bohw', xm, mask_w) + mask_b[None, :, None, None]
        base = jnp.asarray(np.stack([(PTS * (2 * g + 1)).reshape(-1) for g in range(G)], axis=0))
        k_list, v_list = ([], [])
        for g in range(G):
            xo = _pconv_nchw(q_nchw, off_pconv_w[g])
            off = jnp.einsum('bchw,oc->bohw', xo, off_w[g]) + off_b[g][None, :, None, None] + base[g][None, :, None, None]
            sl = slice(g * HC, (g + 1) * HC)
            k_list.append(_flow_warp(k_map[:, sl], off) * mask[:, None])
            v_list.append(_flow_warp(v_map[:, sl], off) * mask[:, None])

        def arrange(lst):
            t = jnp.stack(lst, axis=0).transpose(1, 0, 4, 5, 3, 2)
            return t.reshape(Bb, G, P, K, HC)
        k = arrange(k_list)
        v = arrange(v_list)
        qh = q.reshape(Bb, Hh, Ww, G, HC).transpose(0, 3, 1, 2, 4).reshape(Bb, G, P, HC) * scale
        attn = jnp.einsum('bgpc,bgpkc->bgpk', qh, k)
        attn = jax.nn.softmax(attn, axis=-1)
        out = jnp.einsum('bgpk,bgpkc->bgpc', attn, v)
        out = out.transpose(0, 2, 1, 3).reshape(Bb, Hh, Ww, Cc)
        return out @ proj_w + proj_b

    def _L1_attn_ref(x, Wq, bq, Wk, bk, Wv, bv, Wo, bo):
        import jax, jax.numpy as jnp
        import numpy as np
        from jax import lax
        NUM_HEADS = 8
        HEAD_DIM = 32

        def conv1d_same(x, w, b):
            y = lax.conv_general_dilated(x, w, window_strides=(1,), padding='SAME', dimension_numbers=('NWC', 'WIO', 'NWC'))
            return y + b
        B, T, C = x.shape
        q = conv1d_same(x, Wq, bq)
        k = conv1d_same(x, Wk, bk)
        v = conv1d_same(x, Wv, bv)

        def split(t):
            return t.reshape(B, T, NUM_HEADS, HEAD_DIM).transpose(0, 2, 1, 3)
        q, k, v = (split(q), split(k), split(v))
        scale = 1.0 / jnp.sqrt(jnp.float32(HEAD_DIM))
        logits = jnp.einsum('bhqd,bhkd->bhqk', q, k) * scale
        attn = jax.nn.softmax(logits, axis=-1)
        ctx = jnp.einsum('bhqk,bhkd->bhqd', attn, v)
        ctx = ctx.transpose(0, 2, 1, 3).reshape(B, T, C)
        out = x + conv1d_same(ctx, Wo, bo)
        return out

    def _L1_ffn_ref(h, gate_w, gate_b, w1, b1, w2, b2):
        import math
        import jax, jax.numpy as jnp
        import numpy as np
        CAPACITY_FACTOR = 1.25
        B, L, D = h.shape
        E = gate_w.shape[1]
        T = B * L
        C = max(1, math.ceil(CAPACITY_FACTOR * T / E))
        x = h.reshape(T, D)
        logits = x @ gate_w + gate_b
        probs = jax.nn.softmax(logits, axis=-1)
        idx = jnp.argmax(probs, axis=-1)
        prb = jnp.take_along_axis(probs, idx[:, None], axis=1)[:, 0]
        one_hot = jax.nn.one_hot(idx, E, dtype=jnp.float32)
        pos = (jnp.cumsum(one_hot, axis=0) * one_hot).sum(-1).astype(jnp.int32) - 1
        kept = pos < C
        pos_safe = jnp.where(kept, pos, C)
        buf = jnp.zeros((E, C, D), dtype=h.dtype).at[idx, pos_safe].set(x, mode='drop')
        hmid = jax.nn.relu(jnp.einsum('ecd,edf->ecf', buf, w1) + b1[:, None, :])
        ybuf = jnp.einsum('ecf,efd->ecd', hmid, w2) + b2[:, None, :]
        pos_g = jnp.minimum(pos, C - 1)
        y_tok = ybuf[idx, pos_g] * (prb * kept)[:, None]
        y = y_tok.reshape(B, L, D)
        y = jnp.nan_to_num(y, nan=0.0, posinf=10000.0, neginf=-10000.0)
        return y

    def _gn(v, G=32, eps=1e-5):
        B_, H_, W_, C_ = v.shape
        g = v.reshape(B_, H_, W_, G, C_ // G)
        m = jnp.mean(g, axis=(1, 2, 4), keepdims=True)
        s = jnp.var(g, axis=(1, 2, 4), keepdims=True)
        return ((g - m) / jnp.sqrt(s + eps)).reshape(v.shape)

    def _ln_c(v, eps=1e-6):
        m = jnp.mean(v, axis=-1, keepdims=True)
        s = jnp.var(v, axis=-1, keepdims=True)
        return (v - m) / jnp.sqrt(s + eps)

    def _ln_t(v, eps=1e-5):
        m = jnp.mean(v, axis=-1, keepdims=True)
        s = jnp.var(v, axis=-1, keepdims=True)
        return (v - m) / jnp.sqrt(s + eps)

    def _to_tokens(v):
        B_, H_, W_, C_ = v.shape
        return v.reshape(B_, H_ * W_, C_)
    def _from_tokens(t, like):
        return t.reshape(like.shape)

    x = x + _L0_conv_ref(_gn(x), L0_conv_qkv_w, L0_conv_qkv_b, L0_conv_dw_w, L0_conv_dw_b, L0_conv_off_pconv_w, L0_conv_off_w, L0_conv_off_b, L0_conv_mask_pconv_w, L0_conv_mask_w, L0_conv_mask_b, L0_conv_proj_w, L0_conv_proj_b)
    t = _to_tokens(x)
    t = t + _L1_attn_ref(_ln_t(t), L1_attn_Wq, L1_attn_bq, L1_attn_Wk, L1_attn_bk, L1_attn_Wv, L1_attn_bv, L1_attn_Wo, L1_attn_bo)
    t = t + _L1_ffn_ref(_ln_t(t), L1_ffn_gate_w, L1_ffn_gate_b, L1_ffn_w1, L1_ffn_b1, L1_ffn_w2, L1_ffn_b2)
    x = _from_tokens(t, x)
    return x


_drawn_inputs = setup_inputs


def setup_inputs(seed=0):
    import zlib

    import numpy as np

    out = dict(_drawn_inputs(seed))
    spreads = {'L1_attn_bq': (0.0, 2.0),
     'L1_attn_bk': (0.0, 2.0),
     'L1_attn_bv': (0.0, 0.1),
     'L1_attn_bo': (0.0, 0.1),
     'L1_ffn_gate_b': (0.0, 0.1),
     'L1_ffn_b1': (0.0, 0.8),
     'L1_ffn_b2': (0.0, 0.8)}
    factors = {'L0_conv_proj_b': 2.818}
    for name, (base, spread) in spreads.items():
        noise = np.random.default_rng([zlib.crc32(name.encode()), seed]).standard_normal(out[name].shape)
        drawn = base * np.exp(spread * noise) if base else spread * noise
        out[name] = jnp.asarray(drawn.astype(out[name].dtype))
    for name, factor in factors.items():
        out[name] = (out[name] * factor).astype(out[name].dtype)
    return out
```

```python
from contextlib import ExitStack

import concourse.bass as bass
from concourse import mybir

F32 = mybir.dt.float32
F32R = mybir.dt.float32r
U32 = mybir.dt.uint32
ALU = mybir.AluOpType
ACT = mybir.ActivationFunctionType
AX_X = mybir.AxisListType.X

P = 128
B, H, W, C = 2, 64, 64, 256
N = H * W
CH = C // P
TILES = N // P
G, K, HC = 8, 9, C // 8
CQ = C // 4
TAPS = 9
SAMPLES = G * K
OFFS = 2 * SAMPLES + K
PW = W + 2
PADDED = (H + 2) * PW
KVPAD = N + P
KVWIN = P + W + 1
MT = 3 * C // P
CHUNK = 512
CHUNKS = N // CHUNK
HEADS, HD = 8, 32
QB = 1024
QBS = N // QB
BLOCKS = N // P
ROWS = 3 * HD + 2
STEPS_A = HEADS * QBS
P_SLOTS, LAG = 3, 2
E, F, CAP = 8, 4 * C, 5 * B * N // (4 * 8)
ROUND = float(2 ** 23)
HALF = 15
REC = 5 * SAMPLES


class Tally:

    def __init__(self, engine, sem, base=0):
        self.engine, self.sem, self.base, self.n = engine, sem, base, 0

    def inc(self, ins):
        ins.then_inc(self.sem, 1)
        self.n += 1

    def link(self, ins):
        self.inc(ins)
        self.engine.wait_ge(self.sem, self.base + self.n)


class Stage(ExitStack):

    def __init__(self, nc):
        super().__init__()
        self.nc, self.sems = nc, []

    def __exit__(self, *error):
        super().__exit__(*error)
        if error[0] is None:
            self.nc.clear_and_free_semaphores(self.sems)
            self.nc.all_engine_barrier()


class Room:

    def __init__(self, nc, stack, stage):
        self.nc, self.stack, self.stage = nc, stack, stage

    def sb(self, name, shape, dt=F32):
        return self.stack.enter_context(self.nc.sbuf_tensor(f"{self.stage}_{name}", shape, dt))

    def ps(self, name, shape, dt=F32):
        return self.stack.enter_context(self.nc.psum_tensor(f"{self.stage}_{name}", shape, dt))

    def sem(self, name):
        sem = self.nc.alloc_semaphore(name=f"{self.stage}_{name}")
        self.stack.sems.append(sem)
        return sem


def stage_weights(nc, d, s, keep, offset_w):
    with Stage(nc) as stack:
        r = Room(nc, stack, "w")
        pconv = r.sb("pconv", [CQ, G + 1, TAPS, CQ])
        proj_ps = [r.ps(f"ps{i}", [P, 512]) for i in range(2)]
        zeros = r.sb("zeros", [P, E * CAP // P * C // 8])
        loaded, zeroed, made, copied = (r.sem(x) for x in ("loaded", "zeroed", "made", "copied"))
        blank, blanked = r.sem("blank"), r.sem("blanked")
        block = stack.enter_context(nc.Block())

        @block.sync
        def _(sp):
            sp.dma_start(pconv[:, :, :, :], d["pconv"]).then_inc(loaded, 16)
            sp.dma_start(offset_w.off_w[:, :, :], d["off_wT"].rearrange("(h p) n -> p h n", p=P)).then_inc(loaded, 16)
            sp.dma_start(keep.ident[:, :], d["ident"]).then_inc(loaded, 16)
            sp.wait_ge(loaded, 48)
            sp.wait_ge(blank, 1)
            for i in range(8):
                sp.dma_start(s["buf"].rearrange("(i p r) n -> i p (r n)", i=8, p=P)[i], zeros[:, :]).then_inc(blanked, 16)
            sp.wait_ge(blanked, 128)

        @block.gpsimd
        def _(pool):
            pool.memset(offset_w.taps[:, :, :], 0.0).then_inc(zeroed, 1)
            pool.memset(zeros[:, :], 0.0).then_inc(blank, 1)

        @block.tensor
        def _(pe):
            pe.wait_ge(loaded, 48)
            for tap in range(TAPS):
                if tap >= 2:
                    pe.wait_ge(copied, tap - 1)
                for g in range(G + 1):
                    a, b = 2 * K * g, min(2 * K * (g + 1), OFFS)
                    mm = pe.matmul(proj_ps[tap % 2][0:CQ, a:b], pconv[:, g, tap, :], offset_w.off_w[0:CQ, 0, a:b],
                                   start=True, stop=True)
                mm.then_inc(made, 1)

        @block.vector
        def _(dve):
            dve.wait_ge(zeroed, 1)
            for tap in range(TAPS):
                dve.wait_ge(made, tap + 1)
                dve.tensor_copy(offset_w.taps[0:CQ, tap, :], proj_ps[tap % 2][0:CQ, 0:OFFS]).then_inc(copied, 1)
            dve.wait_ge(loaded, 48)
            dve.tensor_copy(offset_w.taps[CQ:P, TAPS // 2, :], offset_w.off_w[CQ:P, 0, :]).then_inc(copied, 1)


def stage_maps(nc, d, s):
    with Stage(nc) as stack:
        r = Room(nc, stack, "m")
        xt = r.sb("xt", [P, CH, N])
        w = r.sb("w", [P, CH, 3 * C])
        wb = r.sb("wb", [P, MT])
        dw = r.sb("dw", [P, MT, TAPS])
        dwb = r.sb("dwb", [P, MT])
        grp = r.sb("grp", [P, P])
        pad = [r.sb(f"pad{i}", [P, H + 2, PW]) for i in range(2)]
        outq = [r.sb(f"outq{i}", [P, H + 2, PW]) for i in range(2)]
        outkv = [r.sb(f"outkv{i}", [P, KVPAD]) for i in range(2)]
        stats = r.sb("stats", [P, CH, CHUNKS, 6])
        mv = r.sb("mv", [P, CH, 2])
        gmean = r.sb("gmean", [P, CH])
        dev = r.sb("dev", [P, CH])
        var = r.sb("var", [P, CH])
        veps = r.sb("veps", [P, CH])
        std = r.sb("std", [P, CH])
        rstd = r.sb("rstd", [P, CH])
        ps_g = r.ps("g", [P, 512])
        ps = [r.ps(f"ps{i}", [P, 512]) for i in range(4)]
        wts, xt_in = r.sem("wts"), r.sem("xt_in")
        chan_mean, chan_var, grp_mean, grp_var = (r.sem(x) for x in ("cm", "cv", "gm", "gv"))
        var_ready, std_ready, xn_ready = r.sem("var"), r.sem("std"), r.sem("xn")
        qkv_ready, pad_full, pad_free, conv_done = r.sem("qkv"), r.sem("padfull"), r.sem("padfree"), r.sem("conv")
        edges = r.sem("edges")
        q_out = [r.sem(f"qout{i}") for i in range(2)]
        kv_out = [r.sem(f"kvout{i}") for i in range(2)]
        chain = r.sem("chain")
        block = stack.enter_context(nc.Block())
        Q_COPIES = (3, 1)
        PER = MT * CHUNKS
        DVE_STEPS = CH * CHUNKS + 7 + MT * (TAPS - 1)

        @block.sync
        def _(sp):
            sp.dma_start(w[:, :, :], d["qkv_w"].rearrange("(h p) n -> p h n", p=P)).then_inc(wts, 16)
            sp.dma_start(wb[:, :], d["qkv_b"]).then_inc(wts, 16)
            sp.dma_start(dw[:, :, :], d["dw_w"]).then_inc(wts, 16)
            sp.dma_start(dwb[:, :], d["dw_b"]).then_inc(wts, 16)
            sp.dma_start(grp[:, :], d["grp"]).then_inc(wts, 16)
            with sp.Fori(0, B) as b:
                sp.wait_ge(qkv_ready, PER * b)
                sp.dma_start(xt[:, :, :], d["xT"][bass.ds(b, 1)].rearrange("a (h p) n -> p (a h) n", p=P)).then_inc(xt_in, 16)
                for m in range(MT):
                    sp.wait_ge(conv_done, MT * b + m + 1)
                    if m < CH:
                        for dx in range(3) if m == 0 else (1,):
                            sp.dma_start(s["dwq"][bass.ds(b, 1), dx if m == 0 else 3]
                                         .rearrange("a p (r c) -> (a p) r c", c=W),
                                         outq[m][:, :, dx:dx + W]).then_inc(q_out[m], 16)
                    else:
                        sp.dma_start(s["dwkv"][bass.ds(b, 1), m - CH].rearrange("a p n -> (a p) n"),
                                     outkv[m % 2][:, :]).then_inc(kv_out[m % 2], 16)
            for i in range(2):
                sp.wait_ge(q_out[i], 16 * Q_COPIES[i] * B)
                sp.wait_ge(kv_out[i], 32 * B)

        @block.gpsimd
        def _(pool):
            for t in pad:
                pool.memset(t[:, :, :], 0.0).then_inc(pad_free, 1)
            for t in outq:
                pool.memset(t[:, :, :], 0.0).then_inc(edges, 1)
            for t in outkv:
                pool.memset(t[:, :], 0.0).then_inc(edges, 1)

        @block.tensor
        def _(pe):
            pe.wait_ge(wts, 80)
            with pe.Fori(0, B) as b:
                pe.wait_ge(chan_mean, b + 1)
                pe.matmul(ps_g[:, 0:CH], grp[:, :], mv[:, :, 0], start=True, stop=True).then_inc(grp_mean, 1)
                pe.wait_ge(chan_var, b + 1)
                pe.matmul(ps_g[:, CH:2 * CH], grp[:, :], var[:, :], start=True, stop=True).then_inc(grp_var, 1)
                pe.wait_ge(xn_ready, b + 1)
                for i in range(PER):
                    m, c = divmod(i, CHUNKS)
                    pe.wait_ge(pad_full, PER * b + max(i - 3, 0))
                    for h in range(CH):
                        mm = pe.matmul(ps[i % 4][:, :], w[:, h, m * P:(m + 1) * P],
                                       xt[:, h, c * CHUNK:(c + 1) * CHUNK], start=(h == 0), stop=(h == CH - 1))
                    mm.then_inc(qkv_ready, 1)

        @block.scalar
        def _(act):
            act.wait_ge(wts, 80)
            with act.Fori(0, B) as b:
                act.wait_ge(var_ready, b + 1)
                act.activation(std[:, :], veps[:, :], ACT.Sqrt).then_inc(std_ready, 1)
                for i in range(PER):
                    m, c = divmod(i, CHUNKS)
                    if c == 0:
                        act.wait_ge(pad_free, MT * b + m + 1)
                    act.wait_ge(qkv_ready, PER * b + i + 1)
                    rows = CHUNK // W
                    act.activation(pad[m % 2][:, 1 + c * rows:1 + (c + 1) * rows, 1:1 + W],
                                   ps[i % 4][:, :].rearrange("p (r c) -> p r c", c=W), ACT.Identity,
                                   bias=wb[:, m:m + 1]).then_inc(pad_full, 1)

        @block.vector
        def _(dve):
            dve.wait_ge(wts, 80)
            dve.wait_ge(edges, 4)
            with dve.Fori(0, B) as b:
                t = Tally(dve, chain, DVE_STEPS * b)
                dve.wait_ge(xt_in, 16 * b + 16)
                for h in range(CH):
                    for c in range(CHUNKS):
                        t.inc(dve.bn_stats(stats[:, h, c, :], xt[:, h, c * CHUNK:(c + 1) * CHUNK]))
                dve.wait_ge(chain, t.base + t.n)
                dve.memset(veps[:, :], 0.0)
                t.inc(dve.bn_aggr(mv[:, 0, :], stats[:, 0, :, :].rearrange("p c s -> p (c s)")))
                dve.bn_aggr(mv[:, 1, :], stats[:, 1, :, :].rearrange("p c s -> p (c s)")).then_inc(chan_mean, 1)
                dve.wait_ge(grp_mean, b + 1)
                t.link(dve.tensor_copy(gmean[:, :], ps_g[:, 0:CH]))
                t.link(dve.tensor_tensor(dev[:, :], mv[:, :, 0], gmean[:, :], ALU.subtract))
                t.link(dve.tensor_tensor(dev[:, :], dev[:, :], dev[:, :], ALU.mult))
                dve.tensor_tensor(var[:, :], dev[:, :], mv[:, :, 1], ALU.add).then_inc(chan_var, 1)
                dve.wait_ge(grp_var, b + 1)
                dve.tensor_scalar(veps[:, :], ps_g[:, CH:2 * CH], 1e-5, None, ALU.add).then_inc(var_ready, 1)
                dve.wait_ge(std_ready, b + 1)
                t.link(dve.reciprocal(rstd[:, :], std[:, :]))
                for h in range(CH):
                    t.inc(dve.tensor_scalar(xt[:, h, :], xt[:, h, :], gmean[:, h:h + 1], rstd[:, h:h + 1],
                                            ALU.subtract, ALU.mult))
                dve.wait_ge(chain, t.base + t.n)
                dve.tensor_copy(dev[:, :], rstd[:, :]).then_inc(xn_ready, 1)
                for m in range(MT):
                    dve.wait_ge(pad_full, PER * b + CHUNKS * (m + 1))
                    if m < CH:
                        dve.wait_ge(q_out[m], 16 * Q_COPIES[m] * b)
                        acc = outq[m][:, 1:1 + H, 1:1 + W]
                    else:
                        dve.wait_ge(kv_out[m % 2], 32 * b + 16 * ((m - CH) // 2))
                        acc = outkv[m % 2][:, 0:N].rearrange("p (r c) -> p r c", c=W)
                    for tap in range(TAPS):
                        dy, dx = divmod(tap, 3)
                        win = pad[m % 2][:, dy:dy + H, dx:dx + W]
                        wt = dw[:, m, tap:tap + 1]
                        if tap == 0:
                            t.link(dve.tensor_scalar(acc, win, wt, dwb[:, m:m + 1], ALU.mult, ALU.add))
                        elif tap < TAPS - 1:
                            t.link(dve.scalar_tensor_tensor(out=acc, in0=win, scalar=wt, in1=acc, op0=ALU.mult, op1=ALU.add))
                        else:
                            dve.scalar_tensor_tensor(out=acc, in0=win, scalar=wt, in1=acc, op0=ALU.mult,
                                                     op1=ALU.add).then_inc(conv_done, 1)
                    dve.wait_ge(conv_done, MT * b + m + 1)
                    dve.tensor_copy(dev[:, 0:1], rstd[:, 0:1]).then_inc(pad_free, 1)
                assert t.n == DVE_STEPS, t.n


def stage_tables(nc, d, s, keep, offset_w):
    with Stage(nc) as stack:
        r = Room(nc, stack, "t")
        qwin = [r.sb(f"qwin{i}", [P, 4, 4 * W]) for i in range(2)]
        kvwin = [r.sb(f"kvwin{i}", [P, 2 * CH, KVWIN]) for i in range(2)]
        qpix = [r.sb(f"qpix{i}", [P, C]) for i in range(2)]
        rows = [r.sb(f"rows{i}", [P, G, 4, 2, HC]) for i in range(2)]
        bias = r.sb("bias", [P, OFFS])
        grid = r.sb("grid", [P, TILES, 2 * SAMPLES])
        gcol = r.sb("gcol", [P, B, SAMPLES])
        off = r.sb("off", [P, TILES, OFFS])
        pos = r.sb("pos", [P, TILES, 2 * SAMPLES])
        low = r.sb("low", [P, TILES, 2 * SAMPLES])
        tmp = r.sb("tmp", [P, TILES, 2 * SAMPLES])
        rec = r.sb("rec", [P, TILES, REC])
        ps_off = [r.ps(f"off{i}", [P, 512]) for i in range(2)]
        ps_q = [r.ps(f"q{i}", [P, 512]) for i in range(2)]
        ps_kv = [r.ps(f"kv{i}", [P, 512]) for i in range(4)]
        consts = r.sem("consts")
        qwin_in = [r.sem(f"qwin_in{i}") for i in range(2)]
        kvwin_in = [r.sem(f"kvwin_in{i}") for i in range(2)]
        off_mm, q_mm, kv_mm = r.sem("off_mm"), r.sem("q_mm"), r.sem("kv_mm")
        off_got, q_got, kv_act, kv_dve = (r.sem(x) for x in ("off_got", "q_got", "kv_act", "kv_dve"))
        q_out = [r.sem(f"q_out{i}") for i in range(2)]
        rows_out = [r.sem(f"rows_out{i}") for i in range(2)]
        chain, rec_ready, rec_out = r.sem("chain"), r.sem("rec_ready"), r.sem("rec_out")
        block = stack.enter_context(nc.Block())
        CONSTS = 48
        HALF = TILES // 2

        @block.sync
        def _(sp):
            sp.dma_start(bias[:, :], d["off_b"].to_broadcast([P, OFFS])).then_inc(consts, 16)
            sp.dma_start(grid[:, :, :], d["grid"]).then_inc(consts, 16)
            sp.dma_start(gcol[:, :, :], d["gcol"]).then_inc(consts, 16)
            def load(b, t, u):
                sp.dma_start(qwin[u][:, :, :], s["dwq"][bass.ds(b, 1), :, :, bass.ds(t * P, 4 * W)]
                             .rearrange("a h p n -> p (a h) n")).then_inc(qwin_in[u], 16)
                sp.dma_start(kvwin[u][:, :, :], s["dwkv"][bass.ds(b, 1), :, :, bass.ds(t * P, KVWIN)]
                             .rearrange("a h p n -> p (a h) n")).then_inc(kvwin_in[u], 16)

            with sp.Fori(0, B) as b:
                sp.wait_ge(kv_mm, 4 * TILES * b)
                for u in range(2):
                    load(b, u, u)
                with sp.Fori(0, HALF - 1) as i:
                    for u in range(2):
                        sp.wait_ge(kv_mm, 4 * (TILES * b + 2 * i + u + 1))
                        load(b, 2 * i + 2 + u, u)
                sp.wait_ge(rec_ready, b + 1)
                sp.dma_start(s["rec"][bass.ds(b, 1)].rearrange("a t p n -> p (a t) n"), rec[:, :, :]).then_inc(rec_out, 16)
            sp.wait_ge(rec_out, 16 * B)

        @block.tensor
        def _(pe):
            with pe.Fori(0, B) as b:
                with pe.Fori(0, HALF) as i:
                    for u in range(2):
                        turn = HALF * b + i
                        pe.wait_ge(qwin_in[u], 16 * turn + 16)
                        pe.wait_ge(off_got, 2 * turn)
                        for tap in range(TAPS):
                            dy, dx = divmod(tap, 3)
                            pe.matmul(ps_off[u][:, 0:OFFS], qwin[u][:, dx, dy * W:dy * W + P], offset_w.taps[:, tap, :],
                                      start=(tap == 0), stop=False)
                        pe.matmul(ps_off[u][:, 0:OFFS], qwin[u][:, 3, W:W + P], offset_w.off_w[:, 1, :],
                                  start=False, stop=True).then_inc(off_mm, 1)
                        pe.wait_ge(q_got, 2 * turn)
                        for h in range(CH):
                            mm = pe.transpose(ps_q[u][:, h * P:(h + 1) * P], qwin[u][:, 1 + 2 * h, W:W + P], keep.ident[:, :])
                        mm.then_inc(q_mm, 1)
                        pe.wait_ge(kvwin_in[u], 16 * turn + 16)
                        for c in range(4):
                            pe.wait_ge(kv_act if c < 2 else kv_dve, 4 * turn + (2 * u if u else 0))
                            at = (c // 2) * W + c % 2
                            for m in range(2 * CH):
                                mm = pe.transpose(ps_kv[c][:, m * P:(m + 1) * P], kvwin[u][:, m, at:at + P], keep.ident[:, :])
                            mm.then_inc(kv_mm, 1)

        def corner(u, c):
            return (rows[u][:, :, c, :, :].rearrange("p g a c -> p a g c"),
                    ps_kv[c][:, :].rearrange("p (a g c) -> p a g c", a=2, g=G))

        @block.scalar
        def _(act):
            with act.Fori(0, B) as b:
                with act.Fori(0, HALF) as i:
                    for u in range(2):
                        turn = HALF * b + i
                        act.wait_ge(q_mm, 2 * turn + u + 1)
                        act.wait_ge(q_out[u], 16 * turn)
                        act.activation(qpix[u][:, :], ps_q[u][:, 0:C], ACT.Copy).then_inc(q_got, 1)
                        act.wait_ge(q_got, 2 * turn + u + 1)
                        act.dma_start(s["qpix"][bass.ds(b, 1), bass.ds(2 * i + u, 1)].rearrange("a t p n -> (a t p) n"),
                                      qpix[u][:, :]).then_inc(q_out[u], 16)
                        act.wait_ge(rows_out[u], 16 * turn)
                        for c in range(2):
                            act.wait_ge(kv_mm, 8 * turn + 4 * u + c + 1)
                            out, src = corner(u, c)
                            act.activation(out, src, ACT.Copy).then_inc(kv_act, 1)
                        act.wait_ge(kv_act, 4 * turn + 2 * u + 2)
                        act.wait_ge(kv_dve, 4 * turn + 2 * u + 2)
                        act.dma_start(s["table"][bass.ds(b, 1), bass.ds(2 * i + u, 1)].rearrange("a t p n -> (a t p) n"),
                                      rows[u][:, :, :, :, :].rearrange("p g c a n -> p (g c a n)")).then_inc(rows_out[u], 16)
            for u in range(2):
                act.wait_ge(q_out[u], 16 * HALF * B)
                act.wait_ge(rows_out[u], 16 * HALF * B)

        @block.vector
        def _(dve):
            dve.wait_ge(consts, CONSTS)
            CALC = 9
            with dve.Fori(0, B) as b:
                with dve.Fori(0, HALF) as i:
                    for u in range(2):
                        turn = HALF * b + i
                        dve.wait_ge(off_mm, 2 * turn + u + 1)
                        dve.tensor_tensor(off[:, bass.ds(2 * i + u, 1), :].rearrange("p a n -> p (a n)"),
                                          ps_off[u][:, 0:OFFS], bias[:, :], ALU.add).then_inc(off_got, 1)
                        dve.wait_ge(rows_out[u], 16 * turn)
                        for c in range(2, 4):
                            dve.wait_ge(kv_mm, 8 * turn + 4 * u + c + 1)
                            out, src = corner(u, c)
                            dve.tensor_copy(out, src).then_inc(kv_dve, 1)
                t = Tally(dve, chain, CALC * b)
                dve.wait_ge(off_got, TILES * b + TILES)
                dve.wait_ge(rec_out, 16 * b)
                t.link(dve.tensor_tensor(pos[:, :, :], off[:, :, 0:2 * SAMPLES], grid[:, :, :], ALU.add))
                t.link(dve.tensor_scalar(pos[:, :, :], pos[:, :, :], 0.0, float(W - 1), ALU.max, ALU.min))
                t.link(dve.tensor_scalar(low[:, :, :], pos[:, :, :], ROUND, -ROUND, ALU.add, ALU.add))
                t.link(dve.tensor_tensor(tmp[:, :, :], low[:, :, :], pos[:, :, :], ALU.is_gt))
                t.link(dve.tensor_tensor(low[:, :, :], low[:, :, :], tmp[:, :, :], ALU.subtract))
                t.link(dve.tensor_tensor(pos[:, :, :], pos[:, :, :], low[:, :, :], ALU.subtract))
                xy = low[:, :, :].rearrange("p t (k c) -> p (t k) c", c=2)
                pix = tmp[:, :, 0:SAMPLES]
                wx = pos[:, :, :].rearrange("p t (g k c) -> p t g k c", g=G, c=2)
                mask = off[:, :, 2 * SAMPLES:OFFS].unsqueeze(2).to_broadcast([P, TILES, G, K])
                xw = rec[:, :, SAMPLES:3 * SAMPLES].rearrange("p t (g k c) -> p t g k c", g=G, c=2)
                yw = rec[:, :, 3 * SAMPLES:5 * SAMPLES].rearrange("p t (k c) -> p t k c", c=2)
                wy = pos[:, :, :].rearrange("p t (k c) -> p t k c", c=2)
                low2 = low[:, :, :].rearrange("p t (k c) -> p t k c", c=2)
                t.link(dve.scalar_tensor_tensor(out=pix, in0=low2[:, :, :, 1], scalar=float(W), in1=low2[:, :, :, 0],
                                                op0=ALU.mult, op1=ALU.add))
                dve.scalar_tensor_tensor(out=rec[:, :, 0:SAMPLES].bitcast(U32), in0=pix, scalar=float(G),
                                         in1=gcol[:, bass.ds(b, 1), :].to_broadcast([P, TILES, SAMPLES]),
                                         op0=ALU.mult, op1=ALU.add)
                t.link(dve.tensor_tensor(xw[:, :, :, :, 1], wx[:, :, :, :, 0], mask, ALU.mult))
                dve.tensor_tensor(xw[:, :, :, :, 0], mask, xw[:, :, :, :, 1], ALU.subtract)
                dve.tensor_copy(yw[:, :, :, 1], wy[:, :, :, 1])
                t.link(dve.tensor_scalar(yw[:, :, :, 0], wy[:, :, :, 1], -1.0, 1.0, ALU.mult, ALU.add))
                dve.tensor_copy(tmp[:, 0, 0:1], pos[:, 0, 0:1]).then_inc(rec_ready, 1)
                assert t.n == CALC, t.n


class Sampling:

    def __init__(self, nc, stack, d, s, keep, b):
        r = Room(nc, stack, f"s{b}")
        self.nc, self.d, self.s, self.keep, self.b = nc, d, s, keep, b
        self.rec = [r.sb(f"rec{i}", [P, REC]) for i in range(2)]
        self.q = [r.sb(f"q{i}", [P, C]) for i in range(2)]
        self.x = [r.sb(f"x{i}", [P, C]) for i in range(2)]
        self.x1 = [r.sb(f"x1{i}", [P, C]) for i in range(2)]
        self.slot = [r.sb(f"slot{g}", [P, K, 4, 2, HC]) for g in range(G)]
        self.vals = [r.sb(f"vals{i}", [P, 4 * K, P]) for i in range(2)]
        self.proj_w = r.sb("proj_w", [P, CH, C])
        self.proj_b = r.sb("proj_b", [P, C])
        self.outT = r.sb("outT", [P, CH, P])
        self.dots = [r.sb(f"dots{i}", [P, 4, K, 4]) for i in range(2)]
        self.corner = [r.sb(f"corner{i}", [P, 4 * K, 2, 2]) for i in range(2)]
        self.logit = [r.sb(f"logit{i}", [P, 4, K]) for i in range(2)]
        self.top = [r.sb(f"top{i}", [P, 4]) for i in range(2)]
        self.prob = [r.sb(f"prob{i}", [P, 4, K]) for i in range(2)]
        self.total = [r.sb(f"total{i}", [P, 4]) for i in range(2)]
        self.share = [r.sb(f"share{i}", [P, 4]) for i in range(2)]
        self.const_in = r.sem("const_in")
        self.slots_free = r.sem("slots_free")
        self.gathered = [r.sem(f"gathered{g}") for g in range(G)]
        self.values_made = r.sem("values_made")
        self.values_summed = r.sem("values_summed")
        self.logits_made = r.sem("logits_made")
        self.probs_made = r.sem("probs_made")
        self.outT_made = r.sem("outT_made")
        self.projected = r.sem("projected")
        self.x1_made = r.sem("x1_made")
        self.x1_out = [r.sem(f"x1_out{i}") for i in range(2)]
        self.chain = r.sem("chain")
        self.tile_in = [r.sem(f"tile_in{i}") for i in range(2)]
        self.x_in = [r.sem(f"x_in{i}") for i in range(2)]
        self.biased = r.sem("biased")
        self.STEPS = 2 + 2 * G + 2 * 7

    def ps_in_one_bank(self, r):
        ps = r.ps("sums", [P, 512])
        self.ps_sum = [ps[:, i * P:(i + 1) * P] for i in range(2)]
        self.ps_proj = ps[:, C:2 * C]

    def load_constants(self, sp):
        sp.dma_start(self.proj_w[:, :, :], self.d["proj_w"].rearrange("(h p) n -> p h n", p=P)).then_inc(self.const_in, 16)
        sp.dma_start(self.proj_b[:, :], self.d["proj_b"].to_broadcast([P, C])).then_inc(self.const_in, 16)

    def load_tile(self, sp, n, u):
        b = self.b
        flat = "a p n -> (a p) n"
        sp.dma_start(self.rec[u][:, :], self.s["rec"][b, bass.ds(n, 1)].rearrange(flat)).then_inc(self.tile_in[u], 16)
        sp.dma_start(self.q[u][:, :], self.s["qpix"][b, bass.ds(n, 1)].rearrange(flat)).then_inc(self.tile_in[u], 16)

    def load_x(self, sp, n, u):
        sp.dma_start(self.x[u][:, :], self.d["x"][self.b].rearrange("(t p) n -> t p n", p=P)[bass.ds(n, 1)]
                     .rearrange("a p n -> (a p) n"))\
            .then_inc(self.x_in[u], 16)

    def reload(self, sp, n, u):
        sp.wait_ge(self.values_made, G * n + G + 5)
        self.load_tile(sp, n + 2, u)

    def store_tile(self, sp, n, u):
        sp.wait_ge(self.x1_made, n + 1)
        sp.dma_start(self.s["x1"][self.b, bass.ds(n, 1)].rearrange("a p n -> (a p) n"), self.x1[u][:, :])\
            .then_inc(self.x1_out[u], 16)

    def wait_stores(self, sp):
        for u in range(2):
            sp.wait_ge(self.x1_out[u], 16 * TILES // 2)

    def gather(self, pool, n, turn, u, g):
        if g == 0:
            pool.wait_ge(self.tile_in[u], 32 * turn + 32)
        pool.wait_ge(self.values_made, G * n + g + 1)
        pool.sem_inc(self.slots_free, 1)
        for k in range(K):
            pool.indirect_dma_start(
                out=self.slot[g][:, k, :, :, :].rearrange("p c a n -> p (c a n)"), out_offset=None,
                in_=self.s["table"].rearrange("b t p (g n) -> (b t p g) n", g=G),
                in_offset=bass.IndirectOffsetOnAxis(ap=self.rec[u][:, g * K + k:g * K + k + 1].bitcast(U32), axis=0),
            ).then_inc(self.gathered[g], 16)

    def begin(self, dve):
        dve.wait_ge(self.const_in, 32)
        dve.sem_inc(self.values_made, G)

    def tally(self, dve, n):
        return Tally(dve, self.chain, self.STEPS * n)

    def tile_start(self, dve, t, n, turn, u):
        dve.wait_ge(self.tile_in[u], 32 * turn + 32)
        for i in range(2):
            w = self.rec[u][:, SAMPLES + i * SAMPLES:SAMPLES + (i + 1) * SAMPLES].rearrange("p (k x) -> p k x", x=2)
            v = self.rec[u][:, (3 + i) * SAMPLES:(4 + i) * SAMPLES].rearrange("p (k y) -> p k y", y=2)
            t.inc(dve.tensor_tensor(self.corner[i][:, :, :, :], v.unsqueeze(3).to_broadcast([P, 4 * K, 2, 2]),
                                    w.unsqueeze(2).to_broadcast([P, 4 * K, 2, 2]), ALU.mult))

    def q_times_k(self, dve, t, n, u, g):
        dve.wait_ge(self.gathered[g], 16 * K * n + 16 * K)
        k = self.slot[g][:, :, :, 0, :].rearrange("p k c n -> p (k c) n")
        q = self.q[u][:, g * HC:(g + 1) * HC].unsqueeze(1).to_broadcast([P, 4 * K, HC])
        t.inc(dve.tensor_tensor(k, k, q, ALU.mult))

    def scores(self, dve, t, n, g):
        k = self.slot[g][:, :, :, 0, :].rearrange("p k c n -> p (k c) n")
        dve.wait_ge(self.chain, t.base + t.n)
        t.inc(dve.tensor_reduce(self.dots[g // 4][:, g % 4, :, :].rearrange("p k c -> p (k c)"), k, AX_X, ALU.add))

    def logits(self, dve, t, n, i):
        dots = self.dots[i][:, :, :, :].rearrange("p g k c -> p (g k) c")
        dve.wait_ge(self.chain, t.base + t.n)
        t.link(dve.tensor_tensor(dots, dots, self.corner[i][:, :, :, :].rearrange("p k y x -> p k (y x)"), ALU.mult))
        t.link(dve.tensor_reduce(self.logit[i][:, :, :].rearrange("p g k -> p (g k)"), dots, AX_X, ALU.add))
        t.link(dve.tensor_reduce(self.top[i][:, :], self.logit[i][:, :, :], AX_X, ALU.max))
        dve.tensor_tensor(self.logit[i][:, :, :], self.logit[i][:, :, :],
                          self.top[i][:, :].unsqueeze(2).to_broadcast([P, 4, K]), ALU.subtract).then_inc(self.logits_made, 1)

    def weights(self, dve, t, n, i):
        dve.wait_ge(self.probs_made, 2 * n + i + 1)
        t.link(dve.tensor_reduce(self.total[i][:, :], self.prob[i][:, :, :], AX_X, ALU.add))
        t.link(dve.reciprocal(self.share[i][:, :], self.total[i][:, :]))
        t.link(dve.tensor_tensor(self.prob[i][:, :, :], self.prob[i][:, :, :],
                                 self.share[i][:, :].unsqueeze(2).to_broadcast([P, 4, K]), ALU.mult))
        c = self.corner[i][:, :, :, :].rearrange("p k y x -> p k (y x)")
        p = self.prob[i][:, :, :].rearrange("p g k -> p (g k)").unsqueeze(2).to_broadcast([P, 4 * K, 4])
        t.link(dve.tensor_tensor(c, c, p, ALU.mult))

    def piece(self, dve, t, n, turn, u, slot):
        i, m = divmod(slot, HALF)
        if i > 1:
            return
        if slot == 0:
            self.tile_start(dve, t, n, turn, u)
        if m < 8 and m % 2 == 0:
            self.q_times_k(dve, t, n, u, 4 * i + m // 2)
        elif m < 8:
            self.scores(dve, t, n, 4 * i + m // 2)
        elif m == 8:
            self.logits(dve, t, n, i)
        elif m == 10:
            self.weights(dve, t, n, i)
        elif m > 10:
            self.values(dve, n, 4 * i + m - 11)

    def values(self, dve, n, g):
        i, j = divmod(g, 4)
        if j == 0:
            dve.wait_ge(self.values_summed, 2 * n + i)
        v = self.slot[g][:, :, :, 1, :].rearrange("p k c n -> p (k c) n")
        w = self.corner[i][:, j * K:(j + 1) * K, :, :].rearrange("p k y x -> p (k y x)").unsqueeze(2)
        dve.tensor_tensor(self.vals[i][:, :, j * HC:(j + 1) * HC], v, w.to_broadcast([P, 4 * K, HC]), ALU.mult)\
            .then_inc(self.values_made, 1)

    def add_residual(self, dve, n, turn, u):
        dve.wait_ge(self.x_in[u], 16 * turn + 16)
        dve.tensor_tensor(self.x[u][:, :], self.x[u][:, :], self.proj_b[:, :], ALU.add).then_inc(self.biased, 1)
        dve.wait_ge(self.biased, n + 1)
        dve.wait_ge(self.projected, n + 1)
        dve.wait_ge(self.x1_out[u], 16 * turn)
        dve.tensor_tensor(self.x1[u][:, :], self.ps_proj, self.x[u][:, :], ALU.add).then_inc(self.x1_made, 1)

    def exps(self, act, n, i):
        act.wait_ge(self.logits_made, 2 * n + i + 1)
        act.activation(self.prob[i][:, :, :], self.logit[i][:, :, :], ACT.Exp, scale=float(HC) ** -0.5)\
            .then_inc(self.probs_made, 1)

    def copy_out(self, act, n, i):
        act.wait_ge(self.values_summed, 2 * n + i + 2)
        if i == 0:
            act.wait_ge(self.projected, n)
        act.activation(self.outT[:, i, :], self.ps_sum[i], ACT.Copy).then_inc(self.outT_made, 1)

    def pe_begin(self, pe):
        pe.wait_ge(self.const_in, 32)
        pe.sem_inc(self.values_summed, 1)

    def sum_values(self, pe, n, i, part, parts):
        if part == 0:
            pe.wait_ge(self.values_made, G * n + 4 * i + 4 + G)
            if i == 0:
                pe.wait_ge(self.x1_made, n)
            else:
                pe.wait_ge(self.outT_made, 2 * n + 1)
        step = 4 * K // parts
        for j in range(part * step, (part + 1) * step):
            mm = pe.matmul(self.ps_sum[i], self.vals[i][:, j, :], self.keep.ident[:, :],
                           start=(j == 0), stop=(j == 4 * K - 1))
        if part == parts - 1:
            mm.then_inc(self.values_summed, 1)

    def project(self, pe, n):
        pe.wait_ge(self.outT_made, 2 * n + 2)
        for i in range(CH):
            mm = pe.matmul(self.ps_proj, self.outT[:, i, :], self.proj_w[:, i, :], start=(i == 0), stop=(i == CH - 1))
        mm.then_inc(self.projected, 1)


def stage_sample(nc, d, s, keep, b):
    with Stage(nc) as stack:
        sa = Sampling(nc, stack, d, s, keep, b)
        r = Room(nc, stack, f"sp{b}")
        sa.ps_in_one_bank(r)
        block = stack.enter_context(nc.Block())
        PAIRS = TILES // 2

        @block.sync
        def _(sp):
            sa.load_constants(sp)
            for u in range(2):
                sa.load_tile(sp, u, u)
                sa.load_x(sp, u, u)
            with sp.Fori(0, PAIRS - 1) as i:
                for u in range(2):
                    n = 2 * i + u
                    sa.reload(sp, n, u)
                    sa.store_tile(sp, n, u)
                    sa.load_x(sp, n + 2, u)
            for u in range(2):
                sa.store_tile(sp, TILES - 2 + u, u)
            sa.wait_stores(sp)

        @block.gpsimd
        def _(pool):
            with pool.Fori(0, PAIRS) as i:
                for u in range(2):
                    for g in range(G):
                        sa.gather(pool, 2 * i + u, i, u, g)

        @block.vector
        def _(dve):
            sa.begin(dve)
            with dve.Fori(0, PAIRS) as i:
                for u in range(2):
                    n = 2 * i + u
                    t = sa.tally(dve, n)
                    for slot in range(2 * HALF):
                        sa.piece(dve, t, n, i, u, slot)
                    sa.add_residual(dve, n, i, u)
                    assert t.n == sa.STEPS, t.n

        @block.scalar
        def _(act):
            with act.Fori(0, PAIRS) as i:
                for u in range(2):
                    n = 2 * i + u
                    for half in range(2):
                        sa.exps(act, n, half)
                        sa.copy_out(act, n, half)

        @block.tensor
        def _(pe):
            sa.pe_begin(pe)
            with pe.Fori(0, PAIRS) as i:
                for u in range(2):
                    n = 2 * i + u
                    for half in range(2):
                        sa.sum_values(pe, n, half, 0, 1)
                    sa.project(pe, n)


def stage_project(nc, d, s, keep, b):
    with Stage(nc) as stack:
        r = Room(nc, stack, f"p{b}")
        x = r.sb("x", [P, TILES, C])
        hT = r.sb("hT", [P, CH, N + 2])
        w = r.sb("w", [P, 3, 3, CH, C])
        wb = r.sb("wb", [P, 3, CH])
        bo = r.sb("bo", [P, C])
        h = [r.sb(f"h{i}", [P, C]) for i in range(2)]
        hi = [r.sb(f"hi{i}", [P, QB], F32R) for i in range(2)]
        lo = [r.sb(f"lo{i}", [P, QB], F32R) for i in range(2)]
        vT = [r.sb(f"vT{i}", [P, QB]) for i in range(2)]
        va = [r.sb(f"va{i}", [P, 4, QB // P, 2 * HD]) for i in range(2)]
        norm = Norm(r, TILES)
        ps_c = [r.ps(f"c{i}", [P, QB]) for i in range(2)]
        ps_h = [r.ps(f"ps_h{i}", [P, 512]) for i in range(2)]
        ps_v = [r.ps(f"ps_v{i}", [P, 512]) for i in range(2)]
        consts, x_in, edges = r.sem("consts"), r.sem("x_in"), r.sem("edges")
        h_made, hT_mm, hT_made, base_made, base_out = (r.sem(n) for n in ("hm", "hTmm", "hTm", "bm", "bo"))
        conv_mm, act_got, lo_made, vT_mm, va_made = (r.sem(n) for n in ("cmm", "ag", "lm", "vmm", "vam"))
        parts_out = [r.sem(f"parts_out{i}") for i in range(2)]
        va_out = [r.sem(f"va_out{i}") for i in range(2)]
        block = stack.enter_context(nc.Block())
        names = ("Wq", "Wk", "Wv")
        STEPS = 6

        @block.sync
        def _(sp):
            sp.dma_start(x[:, :, :], s["x1"][b].rearrange("t p n -> p t n")).then_inc(x_in, 16)
            for i, name in enumerate(names):
                for tap in range(3):
                    sp.dma_start(w[:, i, tap, :, :], d[name][tap].rearrange("(h p) n -> p h n", p=P)).then_inc(consts, 16)
            sp.dma_start(wb[:, :, :], d["bqkv"]).then_inc(consts, 16)
            sp.dma_start(bo[:, :], d["bo"].to_broadcast([P, C])).then_inc(consts, 16)
            sp.wait_ge(base_made, TILES)
            sp.dma_start(s["base"][b].rearrange("t p n -> p t n"), x[:, :, :]).then_inc(base_out, 16)
            with sp.Fori(0, QBS) as c:
                for k in range(4):
                    sp.wait_ge(lo_made, 4 * c + k + 1)
                    u, m = k % 2, k % 2
                    if k < 2:
                        dst = s["q"][b].rearrange("(h q) r n -> h q r n", q=QBS)[4 * m:4 * m + 4, bass.ds(c, 1)]\
                            .rearrange("h q r n -> (h q) r n")
                        order = (hi, hi, lo)
                    else:
                        dst = s["k"][b, 4 * m:4 * m + 4, :, bass.ds(c * QB, QB)]
                        order = (hi, lo, hi)
                    for j, part in enumerate(order):
                        sp.dma_start(dst[:, j * HD:(j + 1) * HD, :], part[u][:, :].bitcast(F32)).then_inc(parts_out[u], 16)
                for m in range(CH):
                    sp.wait_ge(va_made, 4 * c + 2 * m + 2)
                    sp.dma_start(s["v"][b, 4 * m:4 * m + 4, :, bass.ds(c * QB // P * 2 * HD, QB // P * 2 * HD)]
                                 .rearrange("h p n -> p h n"), va[m][:, :, :, :].rearrange("p h k n -> p h (k n)"))\
                        .then_inc(va_out[m], 16)
            sp.wait_ge(base_out, 16)
            for u in range(2):
                sp.wait_ge(parts_out[u], 96 * QBS)
                sp.wait_ge(va_out[u], 16 * QBS)

        @block.gpsimd
        def _(pool):
            pool.memset(hT[:, :, 0:1], 0.0).then_inc(edges, 1)
            pool.memset(hT[:, :, N + 1:N + 2], 0.0).then_inc(edges, 1)
            for t in va:
                pool.memset(t[:, :, :, :], 1.0).then_inc(edges, 1)

        @block.tensor
        def _(pe):
            pe.wait_ge(edges, 4)
            with pe.Fori(0, TILES // 2) as i:
                for u in range(2):
                    pe.wait_ge(h_made, 2 * i + u + 1)
                    pe.wait_ge(hT_made, 2 * i)
                    for half in range(CH):
                        mm = pe.transpose(ps_h[u][:, half * P:(half + 1) * P], h[u][:, half * P:(half + 1) * P], keep.ident[:, :])
                    mm.then_inc(hT_mm, 1)
            pe.wait_ge(consts, 176)
            pe.wait_ge(hT_made, TILES)

            def turn_v(c, m):
                pe.wait_ge(act_got, STEPS * c + 4 + m + 1)
                for j in range(2):
                    pe.wait_ge(va_made, 4 * c + max(2 * m + j - 1, 0))
                    for i in range(4):
                        mm = pe.transpose(ps_v[j][:, i * P:(i + 1) * P], vT[m][:, (4 * j + i) * P:(4 * j + i + 1) * P],
                                          keep.ident[:, :])
                    mm.then_inc(vT_mm, 1)

            with pe.Fori(0, QBS) as c:
                for k in range(STEPS):
                    kind, m = divmod(k, 2)
                    pe.wait_ge(act_got, STEPS * c + max(k - 1, 0))
                    if k >= 2:
                        pe.wait_ge(lo_made, 4 * c + k - 1)
                    for half in range(QB // CHUNK):
                        for j in range(3 * CH):
                            tap, ch = divmod(j, CH)
                            mm = pe.matmul(ps_c[k % 2][:, half * CHUNK:(half + 1) * CHUNK], w[:, kind, tap, ch, m * P:(m + 1) * P],
                                           hT[:, ch, bass.ds(c * QB + half * CHUNK + tap, CHUNK)],
                                           start=(j == 0), stop=(j == 3 * CH - 1))
                    mm.then_inc(conv_mm, 1)
                for m in range(CH):
                    turn_v(c, m)

        @block.scalar
        def _(act):
            norm.act(act)
            with act.Fori(0, TILES // 2) as i:
                for u in range(2):
                    act.wait_ge(hT_mm, 2 * i + u + 1)
                    act.activation(hT[:, :, bass.ds(2 * i * P + u * P + 1, P)], ps_h[u][:, 0:C].rearrange("p (h n) -> p h n", h=CH),
                                   ACT.Copy).then_inc(hT_made, 1)
            act.wait_ge(consts, 176)
            with act.Fori(0, QBS) as c:
                for k in range(STEPS):
                    kind, m = divmod(k, 2)
                    act.wait_ge(conv_mm, STEPS * c + k + 1)
                    if kind < 2:
                        act.wait_ge(parts_out[k % 2], 96 * c + 48 * kind)
                        out = hi[k % 2][:, :]
                    else:
                        act.wait_ge(vT_mm, 4 * c)
                        out = vT[m][:, :]
                    act.activation(out, ps_c[k % 2][:, :], ACT.Identity, bias=wb[:, kind, m:m + 1]).then_inc(act_got, 1)

        @block.vector
        def _(dve):
            dve.wait_ge(x_in, 16)
            norm.dve(dve, x, 1e-5)
            dve.wait_ge(consts, 176)
            with dve.Fori(0, TILES // 2) as i:
                for u in range(2):
                    n = 2 * i + u
                    xt = x[:, bass.ds(n, 1), :].rearrange("p a n -> p (a n)")
                    dve.wait_ge(hT_mm, 2 * i)
                    dve.tensor_scalar(h[u][:, :], xt, norm.mean[:, bass.ds(n, 1)], norm.rstd[:, bass.ds(n, 1)],
                                      ALU.subtract, ALU.mult).then_inc(h_made, 1)
                    dve.wait_ge(h_made, n + 1)
                    t = Tally(dve, norm.chain, norm.steps + n)
                    t.link(dve.tensor_tensor(xt, xt, h[u][:, :], ALU.add))
                    dve.tensor_tensor(xt, xt, bo[:, :], ALU.add).then_inc(base_made, 1)
            with dve.Fori(0, QBS) as c:
                for k in range(4):
                    kind, m = divmod(k, 2)
                    dve.wait_ge(act_got, STEPS * c + k + 1)
                    dve.wait_ge(parts_out[k % 2], 96 * c + 48 * kind)
                    dve.scalar_tensor_tensor(out=lo[k % 2][:, :], in0=ps_c[k % 2][:, :], scalar=wb[:, kind, m:m + 1],
                                             in1=hi[k % 2][:, :].bitcast(F32), op0=ALU.add, op1=ALU.subtract)\
                        .then_inc(lo_made, 1)
                for m in range(CH):
                    dve.wait_ge(va_out[m], 16 * c)
                    for j in range(2):
                        dve.wait_ge(vT_mm, 4 * c + 2 * m + j + 1)
                        dve.tensor_copy(va[m][:, :, 4 * j:4 * j + 4, 0:HD].rearrange("p h k n -> p k h n"),
                                        ps_v[j][:, :].rearrange("p (k h n) -> p k h n", k=4, h=4)).then_inc(va_made, 1)


class Norm:

    def __init__(self, r, tiles):
        self.tiles = tiles
        self.stats = r.sb("stats", [P, tiles, 6])
        self.mean, self.diff, self.var, self.std, self.rstd = (r.sb(n, [P, tiles]) for n in ("mean", "diff", "var", "std", "rstd"))
        self.chain, self.var_made, self.std_made = r.sem("chain"), r.sem("var_made"), r.sem("std_made")
        self.steps = tiles + 6

    def dve(self, dve, x, eps):
        t = Tally(dve, self.chain)
        for i in range(self.tiles):
            t.inc(dve.bn_stats(self.stats[:, i, :], x[:, i, :]))
        dve.wait_ge(self.chain, self.tiles)
        even, odd = self.stats[:, :, 0:3], self.stats[:, :, 3:6]
        t.link(dve.tensor_tensor(self.diff[:, :], even[:, :, 1], odd[:, :, 1], ALU.subtract))
        t.link(dve.scalar_tensor_tensor(out=self.mean[:, :], in0=self.diff[:, :], scalar=0.5, in1=odd[:, :, 1],
                                        op0=ALU.mult, op1=ALU.add))
        t.link(dve.tensor_tensor(self.var[:, :], even[:, :, 2], odd[:, :, 2], ALU.add))
        t.link(dve.scalar_tensor_tensor(out=self.diff[:, :], in0=self.diff[:, :], scalar=float(C) / 4, in1=self.diff[:, :],
                                        op0=ALU.mult, op1=ALU.mult))
        t.link(dve.tensor_tensor(self.var[:, :], self.var[:, :], self.diff[:, :], ALU.add))
        dve.tensor_scalar(self.var[:, :], self.var[:, :], 1.0 / C, eps, ALU.mult, ALU.add).then_inc(self.var_made, 1)
        dve.wait_ge(self.std_made, 1)
        t.link(dve.reciprocal(self.rstd[:, :], self.std[:, :]))
        assert t.n == self.steps

    def act(self, act):
        act.wait_ge(self.var_made, 1)
        act.activation(self.std[:, :], self.var[:, :], ACT.Sqrt).then_inc(self.std_made, 1)


class Attention:

    def __init__(self, nc, stack, s, keep, b):
        r = Room(nc, stack, f"a{b}")
        self.s, self.keep, self.b = s, keep, b
        self.k = [r.sb(f"k{i}", [ROWS, N], F32R) for i in range(2)]
        self.q = [r.sb(f"q{i}", [ROWS, QB], F32R) for i in range(2)]
        self.v = [r.sb(f"v{i}", [P, N // P, 2 * HD]) for i in range(2)]
        self.p = [r.sb(f"p{i}", [P, QB]) for i in range(P_SLOTS)]
        self.chunk_max = r.sb("chunk_max", [P, QB // P, CHUNKS])
        self.row_max = r.sb("row_max", [P, QB // P])
        self.shift = r.sb("shift", [P, QB // P, 2], F32R)
        self.inv = r.sb("inv", [P, CHUNK])
        self.ctx = [r.sb(f"ctx{i}", [HD, QB]) for i in range(2)]
        self.k_in = [r.sem(f"k_in{i}") for i in range(2)]
        self.q_in = [r.sem(f"q_in{i}") for i in range(2)]
        self.ones, self.s_mm, self.exped, self.p_used = r.sem("ones"), r.sem("s_mm"), r.sem("exped"), r.sem("p_used")
        self.max_mm, self.max_got, self.shift_made, self.shift_in = (r.sem(n) for n in ("mmm", "mg", "sm", "si"))
        self.ctx_got, self.ctx_made = r.sem("cg"), r.sem("cm")
        self.ctx_out = [r.sem(f"ctx_out{i}") for i in range(2)]
        self.chain = r.sem("chain")
        

    def load_q(self, sp, n, u):
        sp.dma_start(self.q[u][0:3 * HD, :].bitcast(F32), self.s["q"][self.b, bass.ds(n, 1)].rearrange("a r n -> (a r) n"))\
            .then_inc(self.q_in[u], 16)

    def load_kv(self, sp, h, par):
        sp.dma_start(self.k[par][0:3 * HD, :].bitcast(F32), self.s["k"][self.b, bass.ds(h, 1)].rearrange("a r n -> (a r) n"))\
            .then_inc(self.k_in[par], 16)
        sp.dma_start(self.v[par][:, :, :].rearrange("p k n -> p (k n)"), self.s["v"][self.b, bass.ds(h, 1)]
                     .rearrange("a p n -> (a p) n")).then_inc(self.k_in[par], 16)

    def first_loads(self, sp):
        self.load_kv(sp, 0, 0)
        self.load_q(sp, 0, 0)
        self.load_q(sp, 1, 1)

    def kv_step(self, sp, h, n, par, last):
        sp.wait_ge(self.p_used, BLOCKS * n + P_SLOTS)
        self.load_kv(sp, h if last else h + 1, 1 - par)

    def sync_step(self, sp, h, n, j, last):
        u = j % 2
        sp.wait_ge(self.s_mm, BLOCKS * n + BLOCKS)
        self.load_q(sp, n if last and j >= 2 else n + 2, u)
        sp.wait_ge(self.ctx_made, n + 1)
        sp.dma_start(self.s["ctx"][self.b, bass.ds(h, 1), :, j * QB:(j + 1) * QB].rearrange("a r n -> (a r) n"),
                     self.ctx[u][:, :]).then_inc(self.ctx_out[u], 16)

    def end_sync(self, sp):
        for u in range(2):
            sp.wait_ge(self.ctx_out[u], 16 * STEPS_A // 2)
            sp.wait_ge(self.q_in[u], 16 * (STEPS_A // 2 + 1))
        sp.wait_ge(self.k_in[0], 32 * 5)
        sp.wait_ge(self.k_in[1], 32 * 4)

    def set_ones(self, pool):
        for k in self.k:
            pool.memset(k[3 * HD:ROWS, :].bitcast(F32), 1.0).then_inc(self.ones, 1)

    def pe_begin(self, pe):
        pe.wait_ge(self.ones, 2)
        pe.wait_ge(self.q_in[0], 16)
        pe.wait_ge(self.k_in[0], 32)
        pe.sem_inc(self.p_used, P_SLOTS)

    def max_chunks(self, pe, base, q, k, a, b):
        for c in range(a, b):
            t, j = divmod(c, CHUNKS)
            pe.wait_ge(self.max_got, base + c + 1)
            pe.matmul(self.ps_max[c % 2], q[0:3 * HD, t * P:(t + 1) * P], k[0:3 * HD, j * CHUNK:(j + 1) * CHUNK],
                      start=True, stop=True).then_inc(self.max_mm, 1)

    def turn_shift(self, pe, base, n):
        pe.wait_ge(self.shift_made, n + 1)
        for j in range(2):
            c = 64 + j
            pe.wait_ge(self.max_got, base + c + 1)
            for i in range(4):
                mm = pe.transpose(self.ps_max[j][0:2, i * P:(i + 1) * P], self.shift[:, 4 * j + i, :].bitcast(F32),
                                  self.keep.ident[:, :])
            mm.then_inc(self.max_mm, 1)

    def weigh(self, pe, n, k, q, v, kb):
        if kb == 0:
            pe.wait_ge(self.shift_in, n + 1)
        pe.wait_ge(self.exped, BLOCKS * n + kb + 1)
        for i in range(2):
            mm = pe.matmul(self.ps_s[kb % 2][:, i * CHUNK:(i + 1) * CHUNK], k[:, kb * P:(kb + 1) * P],
                           q[:, i * CHUNK:(i + 1) * CHUNK], start=True, stop=True)
        mm.then_inc(self.s_mm, 1)
        if kb >= LAG:
            self.sum_block(pe, n, v, kb - LAG)

    def sum_block(self, pe, n, v, kb):
        if kb == 0:
            pe.wait_ge(self.ctx_got, n)
        pe.wait_ge(self.exped, BLOCKS * n + kb + 3)
        for i in range(2):
            mm = pe.matmul(self.ps_ctx[i * 2 * HD:(i + 1) * 2 * HD, :], v[:, kb, :], self.p[kb % P_SLOTS][:, i * CHUNK:(i + 1) * CHUNK],
                           start=(kb == 0), stop=(kb == BLOCKS - 1))
        mm.then_inc(self.p_used, 1)

    def next_waits(self, pe, hp, par, j):
        pe.wait_ge(self.q_in[1 - j % 2], self.q_count(hp, par, j))
        if j == 3:
            pe.wait_ge(self.k_in[1 - par], 32 * hp + 32 * (1 + par))

    def q_count(self, hp, par, j):
        return 16 * (4 * hp + 2 * par + (j + 1) // 2 + 1)

    def act_begin(self, act):
        act.sem_inc(self.exped, 2)

    def exp_block(self, act, n, kb):
        act.wait_ge(self.s_mm, BLOCKS * n + kb + 1)
        act.wait_ge(self.p_used, BLOCKS * n + kb + 1)
        act.activation(self.p[kb % P_SLOTS][:, :], self.ps_s[kb % 2], ACT.Exp, scale=float(HD) ** -0.5).then_inc(self.exped, 1)

    def dve_begin(self, dve):
        dve.sem_inc(self.max_got, 2)

    def max_got_chunks(self, dve, base, a, b):
        for c in range(a, b):
            t, j = divmod(c, CHUNKS)
            dve.wait_ge(self.max_mm, base + c + 1)
            dve.tensor_reduce(self.chunk_max[:, t, j:j + 1], self.ps_max[c % 2], AX_X, ALU.max).then_inc(self.max_got, 1)

    def make_shift(self, dve, base, t):
        dve.wait_ge(self.max_got, base + 66)
        t.link(dve.tensor_reduce(self.row_max[:, :], self.chunk_max[:, :, :], AX_X, ALU.max))
        t.link(dve.tensor_scalar(self.shift[:, :, 0], self.row_max[:, :], -1.0, None, ALU.mult))
        dve.scalar_tensor_tensor(out=self.shift[:, :, 1], in0=self.row_max[:, :], scalar=-1.0,
                                 in1=self.shift[:, :, 0].bitcast(F32), op0=ALU.mult, op1=ALU.subtract).then_inc(self.shift_made, 1)

    def place_shift(self, dve, base, q):
        for j in range(2):
            dve.wait_ge(self.max_mm, base + 65 + j)
            dve.tensor_copy(q[3 * HD:ROWS, j * CHUNK:(j + 1) * CHUNK], self.ps_max[j][0:2, :]).then_inc(self.max_got, 1)
        dve.wait_ge(self.max_got, base + 68)
        dve.sem_inc(self.shift_in, 1)

    def normalize(self, dve, n, u, turns, t):
        dve.wait_ge(self.p_used, BLOCKS * n + BLOCKS + P_SLOTS)
        t.link(dve.reciprocal(self.inv[:, :], self.ps_ctx))
        dve.wait_ge(self.ctx_out[u], turns)
        for i in range(2):
            lo = 2 * HD * i
            t.inc(dve.tensor_tensor(self.ctx[u][:, i * CHUNK:(i + 1) * CHUNK], self.ps_ctx[lo:lo + HD, :],
                                    self.inv[lo + HD:lo + 2 * HD, :], ALU.mult))
        dve.wait_ge(self.chain, t.base + t.n)
        dve.sem_inc(self.ctx_got, 1)
        dve.sem_inc(self.ctx_made, 1)


def chunks_by(kb, sampling):
    if not sampling:
        return min(64, 64 * kb // 27)
    return min(64, 2 * (kb + sum(kb > slot for slot in (9, HALF + 9))))


def stage_attention(nc, d, s, keep, b, sample=None):
    with Stage(nc) as stack:
        at = Attention(nc, stack, s, keep, b)
        r = Room(nc, stack, f"at{b}")
        at.ps_s = [r.ps(f"s{i}", [P, QB])[:, :] for i in range(2)]
        at.ps_max = [r.ps(f"max{i}", [P, CHUNK])[:, :] for i in range(2)]
        at.ps_ctx = r.ps("ctx", [P, CHUNK])[:, :]
        sa = None
        if sample is not None:
            sa = Sampling(nc, stack, d, s, keep, sample)
            sa.ps_in_one_bank(r)
        block = stack.enter_context(nc.Block())
        PARTS = 12
        FIRST = HALF + 1
        LAST = TILES - 1

        def chunks(kb):
            return (chunks_by(kb - 1, sa is not None), chunks_by(kb, sa is not None)) if kb else (0, 0)

        @block.sync
        def _(sp):
            at.first_loads(sp)
            if sa:
                sa.load_constants(sp)
                for u in range(2):
                    sa.load_tile(sp, u, u)
                    sa.load_x(sp, u, u)

            def pair(hp, first, last):
                for par in range(2):
                    for j in range(4):
                        n, u = 8 * hp + 4 * par + j, j % 2
                        ends = last and par == 1
                        if j == 0:
                            at.kv_step(sp, 2 * hp + par, n, par, ends)
                        if sa and not (first and par == 0 and j == 0):
                            sa.store_tile(sp, n - 1, 1 - u)
                            if not (ends and j == 3):
                                sa.load_x(sp, n + 1, 1 - u)
                        if sa and not (ends and j >= 2):
                            sa.reload(sp, n, u)
                        at.sync_step(sp, 2 * hp + par, n, j, ends)

            pair(0, True, False)
            with sp.Fori(1, HEADS // 2 - 1) as hp:
                pair(hp, False, False)
            pair(HEADS // 2 - 1, False, True)
            at.end_sync(sp)
            if sa:
                sa.store_tile(sp, LAST, LAST % 2)
                sa.wait_stores(sp)

        @block.gpsimd
        def _(pool):
            at.set_ones(pool)
            if sa:
                with pool.Fori(0, TILES // 2) as i:
                    for u in range(2):
                        for g in range(G):
                            sa.gather(pool, 2 * i + u, i, u, g)

        @block.tensor
        def _(pe):
            at.pe_begin(pe)
            if sa:
                sa.pe_begin(pe)
            at.max_chunks(pe, 0, at.q[0], at.k[0], 0, 64)
            at.turn_shift(pe, 0, 0)

            def tile_parts(n, kb, first):
                if kb < PARTS and not first:
                    sa.sum_values(pe, n - 1, 1, kb, PARTS)
                if kb == PARTS + 1 and not first:
                    sa.project(pe, n - 1)
                if FIRST <= kb < FIRST + PARTS:
                    sa.sum_values(pe, n, 0, kb - FIRST, PARTS)

            def pair(hp, first):
                for par in range(2):
                    for j in range(4):
                        u, n = j % 2, 8 * hp + 4 * par + j
                        base = 66 * (n + 1)
                        nq, nk = at.q[1 - u], at.k[par if j < 3 else 1 - par]
                        for kb in range(BLOCKS):
                            if sa:
                                tile_parts(n, kb, first and par == 0 and j == 0)
                            at.weigh(pe, n, at.k[par], at.q[u], at.v[par], kb)
                            if kb == 1:
                                at.next_waits(pe, hp, par, j)
                            at.max_chunks(pe, base, nq, nk, *chunks(kb))
                        at.sum_block(pe, n, at.v[par], BLOCKS - 2)
                        at.turn_shift(pe, base, n + 1)
                        at.sum_block(pe, n, at.v[par], BLOCKS - 1)

            pair(0, True)
            with pe.Fori(1, HEADS // 2) as hp:
                pair(hp, False)
            if sa:
                for part in range(PARTS):
                    sa.sum_values(pe, LAST, 1, part, PARTS)
                sa.project(pe, LAST)

        @block.scalar
        def _(act):
            at.act_begin(act)

            def step(n, first):
                for kb in range(BLOCKS):
                    at.exp_block(act, n, kb)
                    if sa:
                        for half in range(2):
                            if kb == HALF * half + 10:
                                sa.exps(act, n, half)
                        if kb == PARTS and not first:
                            sa.copy_out(act, n - 1, 1)
                        if kb == FIRST + PARTS:
                            sa.copy_out(act, n, 0)

            step(0, True)
            with act.Fori(1, STEPS_A) as n:
                step(n, False)
            if sa:
                sa.copy_out(act, LAST, 1)

        @block.vector
        def _(dve):
            at.dve_begin(dve)
            if sa:
                sa.begin(dve)
            t = Tally(dve, at.chain)
            at.max_got_chunks(dve, 0, 0, 64)
            at.make_shift(dve, 0, t)
            at.place_shift(dve, 0, at.q[0])

            def step(i, u, n, first):
                base = 66 * (n + 1)
                t = Tally(dve, at.chain, 2 + 5 * n)
                ts = sa and sa.tally(dve, n)
                for kb in range(1, BLOCKS):
                    at.max_got_chunks(dve, base, *chunks(kb))
                    if sa:
                        sa.piece(dve, ts, n, i, u, kb - 1)
                        if kb == FIRST - 1 and not first:
                            sa.add_residual(dve, n - 1, i - 1 + u, 1 - u)
                    if chunks(kb)[0] < 64 == chunks(kb)[1]:
                        at.make_shift(dve, base, t)
                at.place_shift(dve, base, at.q[1 - u])
                at.normalize(dve, n, u, 16 * i, t)
                assert t.n == 5 and (not sa or ts.n == sa.STEPS), (t.n, ts.n)

            for u in range(2):
                step(0, u, u, u == 0)
            with dve.Fori(1, STEPS_A // 2) as i:
                for u in range(2):
                    step(i, u, 2 * i + u, False)
            if sa:
                sa.add_residual(dve, LAST, LAST // 2, LAST % 2)


def stage_mix(nc, d, s, keep, b):
    with Stage(nc) as stack:
        r = Room(nc, stack, f"x{b}")
        ctx = r.sb("ctx", [P, CH, N + 2])
        w = r.sb("w", [P, 3, CH, C])
        x = r.sb("x", [P, TILES, C])
        oT = [r.sb(f"oT{i}", [P, CH, CHUNK]) for i in range(2)]
        h = [r.sb(f"h{i}", [P, C]) for i in range(2)]
        hT = [r.sb(f"hT{i}", [P, CH, P]) for i in range(2)]
        gw = r.sb("gw", [P, CH, E])
        gb = r.sb("gb", [P, E])
        norm = Norm(r, TILES)
        ps_o = [r.ps(f"ps_o{i}", [P, 512]) for i in range(2)]
        ps_t = [r.ps(f"ps_t{i}", [P, 512]) for i in range(2)]
        ps_h = [r.ps(f"ps_h{i}", [P, 512]) for i in range(2)]
        ps_g = [r.ps(f"ps_g{i}", [P, 512]) for i in range(2)]
        ctx_in, consts, x_in, edges = r.sem("ctx_in"), r.sem("consts"), r.sem("x_in"), r.sem("edges")
        o_mm, oT_made, t_mm, t_made, t_out = (r.sem(n) for n in ("o_mm", "oT_made", "t_mm", "t_made", "t_out"))
        h_made, hT_mm, hT_made, g_mm, g_got = (r.sem(n) for n in ("h_made", "hT_mm", "hT_made", "g_mm", "g_got"))
        h_out = [r.sem(f"h_out{i}") for i in range(2)]
        block = stack.enter_context(nc.Block())
        PAIRS = TILES // 2

        @block.sync
        def _(sp):
            sp.dma_start(ctx[:, :, 1:N + 1], s["ctx"][b].rearrange("(a h) r n -> (h r) a n", a=CH)).then_inc(ctx_in, 16)
            sp.dma_start(x[:, :, :], s["base"][b].rearrange("t p n -> p t n")).then_inc(x_in, 16)
            for tap in range(3):
                sp.dma_start(w[:, tap, :, :], d["Wo"][tap].rearrange("(h p) n -> p h n", p=P)).then_inc(consts, 16)
            sp.dma_start(gw[:, :, :], d["gate_w"].rearrange("(h p) n -> p h n", p=P)).then_inc(consts, 16)
            sp.dma_start(gb[:, :], d["gate_b"].to_broadcast([P, E])).then_inc(consts, 16)
            sp.wait_ge(t_made, 2 * CHUNKS)
            sp.dma_start(s["t2"][b].rearrange("t p n -> p t n"), x[:, :, :]).then_inc(t_out, 16)
            with sp.Fori(0, PAIRS) as i:
                for u in range(2):
                    sp.wait_ge(h_made, 2 * i + u + 1)
                    sp.dma_start(s["h2"][b, bass.ds(2 * i + u, 1)].rearrange("a p n -> (a p) n"), h[u][:, :]).then_inc(h_out[u], 16)
            sp.wait_ge(t_out, 16)
            for u in range(2):
                sp.wait_ge(h_out[u], 16 * PAIRS)

        @block.gpsimd
        def _(pool):
            pool.memset(ctx[:, :, 0:1], 0.0).then_inc(edges, 1)
            pool.memset(ctx[:, :, N + 1:N + 2], 0.0).then_inc(edges, 1)

        @block.tensor
        def _(pe):
            pe.wait_ge(edges, 2)
            pe.wait_ge(consts, 80)
            pe.wait_ge(ctx_in, 16)
            with pe.Fori(0, CHUNKS // 2) as i:
                for u in range(2):
                    c = 2 * i + u
                    pe.wait_ge(oT_made, 2 * c)
                    for m in range(CH):
                        for j in range(3 * CH):
                            tap, ch = divmod(j, CH)
                            mm = pe.matmul(ps_o[m][:, :], w[:, tap, ch, m * P:(m + 1) * P],
                                           ctx[:, ch, bass.ds(2 * i * CHUNK + u * CHUNK + tap, CHUNK)],
                                           start=(j == 0), stop=(j == 3 * CH - 1))
                        mm.then_inc(o_mm, 1)
                    pe.wait_ge(oT_made, 2 * c + 2)
                    for half in range(2):
                        pe.wait_ge(t_made, 2 * c)
                        for k in range(2):
                            for m in range(CH):
                                at = (2 * half + k) * P
                                mm = pe.transpose(ps_t[half][:, k * C + m * P:k * C + (m + 1) * P], oT[u][:, m, at:at + P],
                                                  keep.ident[:, :])
                        mm.then_inc(t_mm, 1)

            with pe.Fori(0, PAIRS) as i:
                for u in range(2):
                    pe.wait_ge(h_made, 2 * i + u + 1)
                    pe.wait_ge(hT_made, 2 * i)
                    for m in range(CH):
                        mm = pe.transpose(ps_h[u][:, m * P:(m + 1) * P], h[u][:, m * P:(m + 1) * P], keep.ident[:, :])
                    mm.then_inc(hT_mm, 1)
                    pe.wait_ge(hT_made, 2 * i + u + 1)
                    pe.wait_ge(g_got, 2 * i)
                    for m in range(CH):
                        mm = pe.matmul(ps_g[u][:, 0:E], hT[u][:, m, :], gw[:, m, :], start=(m == 0), stop=(m == CH - 1))
                    mm.then_inc(g_mm, 1)

        @block.scalar
        def _(act):
            with act.Fori(0, CHUNKS // 2) as i:
                for u in range(2):
                    c = 2 * i + u
                    act.wait_ge(t_mm, 4 * i)
                    for m in range(CH):
                        act.wait_ge(o_mm, 2 * c + m + 1)
                        act.activation(oT[u][:, m, :], ps_o[m][:, :], ACT.Copy).then_inc(oT_made, 1)
            norm.act(act)
            with act.Fori(0, PAIRS) as i:
                for u in range(2):
                    act.wait_ge(hT_mm, 2 * i + u + 1)
                    act.wait_ge(g_mm, 2 * i)
                    act.activation(hT[u][:, :, :], ps_h[u][:, 0:C].rearrange("p (h n) -> p h n", h=CH), ACT.Copy)\
                        .then_inc(hT_made, 1)

        @block.vector
        def _(dve):
            dve.wait_ge(consts, 80)
            dve.wait_ge(x_in, 16)
            with dve.Fori(0, CHUNKS) as c:
                for half in range(2):
                    dve.wait_ge(t_mm, 2 * c + half + 1)
                    two = x[:, bass.ds(4 * c + 2 * half, 2), :].rearrange("p t n -> p (t n)")
                    dve.tensor_tensor(two, ps_t[half][:, :], two, ALU.add).then_inc(t_made, 1)
            dve.wait_ge(t_made, 2 * CHUNKS)
            norm.dve(dve, x, 1e-5)
            with dve.Fori(0, PAIRS) as i:
                for u in range(2):
                    n = 2 * i + u
                    dve.wait_ge(hT_mm, 2 * i)
                    dve.wait_ge(h_out[u], 16 * i)
                    dve.tensor_scalar(h[u][:, :], x[:, bass.ds(n, 1), :].rearrange("p a n -> p (a n)"),
                                      norm.mean[:, bass.ds(n, 1)], norm.rstd[:, bass.ds(n, 1)],
                                      ALU.subtract, ALU.mult).then_inc(h_made, 1)
                    dve.wait_ge(g_mm, n + 1)
                    dve.tensor_tensor(keep.gate[:, bass.ds(n + b * TILES, 1), :].rearrange("p a e -> p (a e)"),
                                      ps_g[u][:, 0:E], gb[:, :], ALU.add).then_inc(g_got, 1)


def stage_route(nc, d, s, keep):
    with Stage(nc) as stack:
        r = Room(nc, stack, "r")
        ALL = B * TILES
        h = r.sb("h", [P, ALL, C])
        upper, ones = r.sb("upper", [P, P]), r.sb("ones", [P, P])
        prio, first = r.sb("prio", [P, E]), r.sb("first", [P, E])
        top, total, prob, best, expert, place, kept, row = (
            r.sb(n, [P, ALL]) for n in ("top", "total", "prob", "best", "expert", "place", "kept", "row"))
        exps, hot, rank, each, before, work = (r.sb(n, [P, ALL, E]) for n in ("exps", "hot", "rank", "each", "before", "work"))
        to_row = r.sb("to_row", [P, ALL], U32)
        ps_rank, ps_each = r.ps("ps_rank", [P, 512]), r.ps("ps_each", [P, 512])
        consts, h_in, chain = r.sem("consts"), r.sem("h_in"), r.sem("chain")
        less, exped, hot_made, counted, rows_made, sent = (r.sem(n) for n in ("less", "exped", "hot", "counted", "rows", "sent"))
        block = stack.enter_context(nc.Block())

        @block.sync
        def _(sp):
            for tile, name in ((upper, "upper"), (ones, "ones"), (prio, "prio"), (first, "first")):
                sp.dma_start(tile[:, :], d[name]).then_inc(consts, 16)
            sp.dma_start(h[:, :, :], s["h2"].rearrange("b t p n -> p (b t) n")).then_inc(h_in, 16)
            sp.wait_ge(h_in, 16)

        @block.scalar
        def _(act):
            act.wait_ge(less, 1)
            act.activation(exps[:, :, :], exps[:, :, :], ACT.Exp).then_inc(exped, 1)

        @block.tensor
        def _(pe):
            pe.wait_ge(consts, 64)
            pe.wait_ge(hot_made, 1)
            flat = hot[:, :, :].rearrange("p t e -> p (t e)")
            pe.matmul(ps_rank[:, :], upper[:, :], flat, start=True, stop=True)
            pe.matmul(ps_each[:, :], ones[:, :], flat, start=True, stop=True).then_inc(counted, 1)

        @block.vector
        def _(dve):
            t = Tally(dve, chain)

            def tokens(v):
                return v[:, :].unsqueeze(2).to_broadcast([P, ALL, E])

            def experts(v):
                return v[:, :].unsqueeze(1).to_broadcast([P, ALL, E])

            def tt(out, a, b, op):
                t.link(dve.tensor_tensor(out, a, b, op))

            gate = keep.gate[:, :, :]
            dve.wait_ge(consts, 64)
            t.link(dve.tensor_reduce(top[:, :], gate, AX_X, ALU.max))
            tt(hot[:, :, :], gate, tokens(top), ALU.is_equal)
            tt(hot[:, :, :], hot[:, :, :], experts(prio), ALU.mult)
            t.link(dve.tensor_reduce(best[:, :], hot[:, :, :], AX_X, ALU.max))
            tt(rank[:, :, :], hot[:, :, :], tokens(best), ALU.is_equal)
            dve.tensor_copy(hot[:, :, :], rank[:, :, :]).then_inc(hot_made, 1)
            dve.tensor_tensor(exps[:, :, :], gate, tokens(top), ALU.subtract).then_inc(less, 1)
            dve.wait_ge(exped, 1)
            t.link(dve.tensor_reduce(total[:, :], exps[:, :, :], AX_X, ALU.add))
            t.link(dve.reciprocal(prob[:, :], total[:, :]))
            dve.wait_ge(counted, 1)
            flat = "p t e -> p (t e)"
            t.link(dve.tensor_copy(each[:, :, :].rearrange(flat), ps_each[:, :]))
            t.link(dve.tensor_copy(before[:, :, :], each[:, :, :]))
            step, src, dst = 1, before, work
            while step < ALL:
                t.inc(dve.tensor_copy(dst[:, 0:step, :], src[:, 0:step, :]))
                tt(dst[:, step:, :], src[:, step:, :], src[:, 0:ALL - step, :], ALU.add)
                step, src, dst = 2 * step, dst, src
            tt(src[:, :, :], src[:, :, :], each[:, :, :], ALU.subtract)
            tt(src[:, :, :].rearrange(flat), src[:, :, :].rearrange(flat), ps_rank[:, :], ALU.add)
            dve.wait_ge(hot_made, 1)
            tt(src[:, :, :], src[:, :, :], hot[:, :, :], ALU.mult)
            t.link(dve.tensor_reduce(place[:, :], src[:, :, :], AX_X, ALU.add))
            tt(hot[:, :, :], hot[:, :, :], experts(first), ALU.mult)
            t.link(dve.tensor_reduce(expert[:, :], hot[:, :, :], AX_X, ALU.add))
            t.link(dve.tensor_scalar(kept[:, :], place[:, :], float(CAP), None, ALU.is_lt))
            tt(keep.answer_w[:, :], prob[:, :], kept[:, :], ALU.mult)
            t.link(dve.tensor_scalar(work[:, :, 0], kept[:, :], -float(2 * E * CAP), float(2 * E * CAP), ALU.mult, ALU.add))
            t.link(dve.tensor_scalar(place[:, :], place[:, :], float(CAP - 1), None, ALU.min))
            tt(row[:, :], expert[:, :], place[:, :], ALU.add)
            t.link(dve.tensor_copy(keep.answer_row[:, :], row[:, :]))
            dve.tensor_tensor(to_row[:, :], row[:, :], work[:, :, 0], ALU.add).then_inc(rows_made, 1)

        @block.gpsimd
        def _(pool):
            pool.wait_ge(rows_made, 1)
            pool.wait_ge(h_in, 16)
            for t in range(ALL):
                pool.indirect_dma_start(
                    out=s["buf"], out_offset=bass.IndirectOffsetOnAxis(ap=to_row[:, t:t + 1], axis=0),
                    in_=h[:, t, :], in_offset=None, bounds_check=E * CAP - 1, oob_is_err=False).then_inc(sent, 16)
            pool.wait_ge(sent, 16 * ALL)


def stage_experts(nc, d, s, keep):
    with Stage(nc) as stack:
        r = Room(nc, stack, "e")
        RT = CAP // P
        FT = F // P
        PIECES = [(a, min(a + CHUNK, CAP)) for a in range(0, CAP, CHUNK)]
        x = [r.sb(f"x{i}", [P, RT, C]) for i in range(2)]
        w1 = [r.sb(f"w1{i}", [P, CH, F]) for i in range(2)]
        w2 = [r.sb(f"w2{i}", [P, FT, C]) for i in range(2)]
        b1 = [r.sb(f"b1{i}", [P, FT]) for i in range(2)]
        b2 = [r.sb(f"b2{i}", [P, C]) for i in range(2)]
        xT = r.sb("xT", [P, CH, CAP])
        mid = r.sb("mid", [P, FT, CAP])
        y = [r.sb(f"y{i}", [P, RT, C]) for i in range(2)]
        ps_x = [r.ps(f"ps_x{i}", [P, 512]) for i in range(2)]
        ps_m = [r.ps(f"ps_m{i}", [P, 512]) for i in range(4)]
        ps_y = [r.ps(f"ps_y{i}", [P, 512]) for i in range(2)]
        in_sem = [r.sem(f"in{i}") for i in range(2)]
        xT_mm, xT_made, m_mm, m_made, y_mm, y_made = (r.sem(n) for n in ("xT_mm", "xT_made", "m_mm", "m_made", "y_mm", "y_made"))
        y_out = [r.sem(f"y_out{i}") for i in range(2)]
        block = stack.enter_context(nc.Block())
        LOADS = 5 * 16
        XS, MS = RT, FT * len(PIECES)
        TWO = E // 2

        @block.sync
        def _(sp):
            def load(e, u):
                one = bass.ds(e, 1)
                sp.dma_start(x[u][:, :, :], s["buf"].rearrange("(e t p) n -> e p t n", e=E, p=P)[one]
                             .rearrange("a p t n -> p (a t) n")).then_inc(in_sem[u], 16)
                sp.dma_start(w1[u][:, :, :], d["w1"][one].rearrange("a (h p) n -> p (a h) n", p=P)).then_inc(in_sem[u], 16)
                sp.dma_start(w2[u][:, :, :], d["w2"][one].rearrange("a (h p) n -> p (a h) n", p=P)).then_inc(in_sem[u], 16)
                sp.dma_start(b1[u][:, :], d["b1"][one].rearrange("a p n -> (a p) n")).then_inc(in_sem[u], 16)
                sp.dma_start(b2[u][:, :], d["b2"][one].rearrange("a n -> a n").to_broadcast([P, C])).then_inc(in_sem[u], 16)

            def store(e, u):
                sp.wait_ge(y_made, RT * e + RT)
                sp.dma_start(s["y"].rearrange("(e t p) n -> e p t n", e=E, p=P)[bass.ds(e, 1)]
                             .rearrange("a p t n -> p (a t) n"), y[u][:, :, :]).then_inc(y_out[u], 16)

            for u in range(2):
                load(u, u)
            with sp.Fori(0, TWO - 1) as i:
                for u in range(2):
                    store(2 * i + u, u)
                    load(2 * i + u + 2, u)
            for u in range(2):
                store(E - 2 + u, u)
            for u in range(2):
                sp.wait_ge(y_out[u], 16 * TWO)

        @block.tensor
        def _(pe):
            with pe.Fori(0, TWO) as i:
                for u in range(2):
                    e = 2 * i + u
                    pe.wait_ge(in_sem[u], LOADS * (i + 1))
                    for k in range(XS):
                        pe.wait_ge(xT_made, XS * e + max(k - 1, 0))
                        for h in range(CH):
                            mm = pe.transpose(ps_x[k % 2][:, h * P:(h + 1) * P], x[u][:, k, h * P:(h + 1) * P], keep.ident[:, :])
                        mm.then_inc(xT_mm, 1)
                    pe.wait_ge(xT_made, XS * e + XS)
                    for k in range(MS):
                        m, (a, z) = k // len(PIECES), PIECES[k % len(PIECES)]
                        pe.wait_ge(m_made, MS * e + max(k - 3, 0))
                        for h in range(CH):
                            mm = pe.matmul(ps_m[k % 4][:, 0:z - a], w1[u][:, h, m * P:(m + 1) * P], xT[:, h, a:z],
                                           start=(h == 0), stop=(h == CH - 1))
                        mm.then_inc(m_mm, 1)
                    pe.wait_ge(m_made, MS * e + MS)
                    for k in range(RT):
                        pe.wait_ge(y_made, RT * e + max(k - 1, 0))
                        for m in range(FT):
                            mm = pe.matmul(ps_y[k % 2][:, 0:C], mid[:, m, k * P:(k + 1) * P], w2[u][:, m, :],
                                           start=(m == 0), stop=(m == FT - 1))
                        mm.then_inc(y_mm, 1)

        @block.scalar
        def _(act):
            with act.Fori(0, TWO) as i:
                for u in range(2):
                    e = 2 * i + u
                    act.wait_ge(in_sem[u], LOADS * (i + 1))
                    act.wait_ge(m_mm, MS * e)
                    for k in range(XS):
                        act.wait_ge(xT_mm, XS * e + k + 1)
                        act.activation(xT[:, :, k * P:(k + 1) * P], ps_x[k % 2][:, 0:C].rearrange("p (h n) -> p h n", h=CH),
                                       ACT.Copy).then_inc(xT_made, 1)
                    act.wait_ge(y_mm, RT * e)
                    for k in range(MS):
                        m, (a, z) = k // len(PIECES), PIECES[k % len(PIECES)]
                        act.wait_ge(m_mm, MS * e + k + 1)
                        act.activation(mid[:, m, a:z], ps_m[k % 4][:, 0:z - a], ACT.Relu, bias=b1[u][:, m:m + 1]).then_inc(m_made, 1)

        @block.vector
        def _(dve):
            with dve.Fori(0, TWO) as i:
                for u in range(2):
                    e = 2 * i + u
                    dve.wait_ge(in_sem[u], LOADS * (i + 1))
                    dve.wait_ge(y_out[u], 16 * i)
                    for k in range(RT):
                        dve.wait_ge(y_mm, RT * e + k + 1)
                        dve.tensor_tensor(y[u][:, k, :], ps_y[k % 2][:, 0:C], b2[u][:, :], ALU.add).then_inc(y_made, 1)


def stage_combine(nc, d, s, keep, out):
    with Stage(nc) as stack:
        r = Room(nc, stack, "c")
        GT = 8
        GROUPS = B * TILES // GT
        t2 = r.sb("t2", [P, B * TILES, C])
        y = r.sb("y", [P, B * TILES, C])
        good = [r.sb(f"good{i}", [P, GT * C], U32) for i in range(2)]
        big = [r.sb(f"big{i}", [P, GT * C]) for i in range(2)]
        neg = [r.sb(f"neg{i}", [P, GT * C]) for i in range(2)]
        got = [r.sem(f"got{i}") for i in range(GROUPS)]
        t2_in, scaled, summed, out_sem, chain = r.sem("t2_in"), r.sem("scaled"), r.sem("summed"), r.sem("out"), r.sem("chain")
        block = stack.enter_context(nc.Block())

        @block.sync
        def _(sp):
            sp.dma_start(t2[:, :, :], s["t2"].rearrange("b t p n -> p (b t) n")).then_inc(t2_in, 16)
            for g in range(GROUPS):
                sp.wait_ge(summed, g + 1)
                sp.dma_start(out.rearrange("b (t p) n -> p (b t) n", p=P)[:, g * GT:(g + 1) * GT, :],
                             t2[:, g * GT:(g + 1) * GT, :]).then_inc(out_sem, 16)
            sp.wait_ge(out_sem, 16 * GROUPS)

        @block.gpsimd
        def _(pool):
            for t in range(B * TILES):
                pool.indirect_dma_start(out=y[:, t, :], out_offset=None, in_=s["y"],
                                        in_offset=bass.IndirectOffsetOnAxis(ap=keep.answer_row[:, t:t + 1], axis=0))\
                    .then_inc(got[t // GT], 16)

        @block.scalar
        def _(act):
            for g in range(GROUPS):
                act.wait_ge(got[g], 16 * GT)
                for t in range(g * GT, (g + 1) * GT):
                    act.activation(y[:, t, :], y[:, t, :], ACT.Copy, scale=keep.answer_w[:, t:t + 1]).then_inc(scaled, 1)

        @block.vector
        def _(dve):
            t = Tally(dve, chain)
            dve.wait_ge(t2_in, 16)
            for g in range(GROUPS):
                u = g % 2
                dve.wait_ge(scaled, GT * (g + 1))
                v = y[:, g * GT:(g + 1) * GT, :].rearrange("p t n -> p (t n)")
                res = t2[:, g * GT:(g + 1) * GT, :].rearrange("p t n -> p (t n)")
                t.inc(dve.tensor_scalar(good[u][:, :], v, 0.0, 0.0, ALU.mult, ALU.is_equal))
                t.inc(dve.tensor_scalar(big[u][:, :], v, 0.0, 1e4, ALU.is_gt, ALU.mult))
                t.link(dve.tensor_scalar(neg[u][:, :], v, 0.0, -1e4, ALU.is_lt, ALU.mult))
                t.link(dve.tensor_tensor(big[u][:, :], big[u][:, :], neg[u][:, :], ALU.add))
                t.link(dve.copy_predicated(big[u][:, :], good[u][:, :], v))
                dve.tensor_tensor(res, res, big[u][:, :], ALU.add).then_inc(summed, 1)


class Keep:

    def __init__(self, nc, stack):
        r = Room(nc, stack, "keep")
        self.ident = r.sb("ident", [P, P])
        self.gate = r.sb("gate", [P, B * TILES, E])
        self.answer_w = r.sb("answer_w", [P, B * TILES])
        self.answer_row = r.sb("answer_row", [P, B * TILES], U32)


class OffsetWeights:

    def __init__(self, nc, stack):
        r = Room(nc, stack, "off")
        self.off_w = r.sb("w", [P, CH, OFFS])
        self.taps = r.sb("taps", [P, TAPS, OFFS])


def scratch(nc):
    def dram(name, shape, dt=F32):
        return nc.dram_tensor(f"s_{name}", shape, dt).ap()

    return {
        "dwq": dram("dwq", [B, 4, P, (H + 2) * W]),
        "dwkv": dram("dwkv", [B, 2 * CH, P, KVPAD]),
        "rec": dram("rec", [B, TILES, P, REC]),
        "qpix": dram("qpix", [B, TILES, P, C]),
        "base": dram("base", [B, TILES, P, C]),
        "q": dram("q", [B, STEPS_A, 3 * HD, QB]),
        "k": dram("k", [B, HEADS, 3 * HD, N]),
        "v": dram("v", [B, HEADS, P, N // P * 2 * HD]),
        "ctx": dram("ctx", [B, HEADS, HD, N]),
        "t2": dram("t2", [B, TILES, P, C]),
        "h2": dram("h2", [B, TILES, P, C]),
        "buf": dram("buf", [E * CAP, C]),
        "y": dram("y", [E * CAP, C]),
        "x1": dram("x1", [B, TILES, P, C]),
        "table": dram("table", [B, TILES, P, G * 4 * 2 * HC]),
    }


def build(nc, d, out, upto=None, s=None):
    s = s or scratch(nc)
    with ExitStack() as stack:
        keep = Keep(nc, stack)
        stages = {
            "sample0": lambda: stage_sample(nc, d, s, keep, 0),
            "project0": lambda: stage_project(nc, d, s, keep, 0),
            "attention0": lambda: stage_attention(nc, d, s, keep, 0, sample=1),
            "project1": lambda: stage_project(nc, d, s, keep, 1),
            "attention1": lambda: stage_attention(nc, d, s, keep, 1),
            "mix0": lambda: stage_mix(nc, d, s, keep, 0),
            "mix1": lambda: stage_mix(nc, d, s, keep, 1),
            "route": lambda: stage_route(nc, d, s, keep),
            "experts": lambda: stage_experts(nc, d, s, keep),
            "combine": lambda: stage_combine(nc, d, s, keep, out),
        }
        with ExitStack() as early:
            offset_w = OffsetWeights(nc, early)
            first = {
                "weights": lambda: stage_weights(nc, d, s, keep, offset_w),
                "maps": lambda: stage_maps(nc, d, s),
                "tables": lambda: stage_tables(nc, d, s, keep, offset_w),
            }
            for st in first:
                if upto is None or st in upto:
                    first[st]()
        for st in stages:
            if upto is None or st in upto:
                stages[st]()
    return s


def lay_out(inputs):
    import numpy as np

    a = {k: np.asarray(v) for k, v in inputs.items()}
    f = np.float32
    gx, gy = np.meshgrid(np.arange(W), np.arange(H), indexing="xy")
    pts = np.array([[i - 1, j - 1] for i in range(3) for j in range(3)])
    base = np.stack([pts * (2 * g + 1) for g in range(G)]).reshape(1, SAMPLES, 2)
    grid = np.stack([gx.reshape(-1), gy.reshape(-1)], -1)[:, None, :] + base
    io = {
        "x": a["x"].reshape(B, N, C),
        "xT": a["x"].reshape(B, N, C).transpose(0, 2, 1),
        "qkv_w": a["L0_conv_qkv_w"],
        "qkv_b": a["L0_conv_qkv_b"].reshape(MT, P).T,
        "dw_w": a["L0_conv_dw_w"].reshape(TAPS, MT, P).transpose(2, 1, 0),
        "dw_b": a["L0_conv_dw_b"].reshape(MT, P).T,
        "pconv": np.concatenate([a["L0_conv_off_pconv_w"], a["L0_conv_mask_pconv_w"][None]])
        .reshape(G + 1, CQ, CQ, TAPS).transpose(1, 0, 3, 2),
        "off_wT": np.concatenate([a["L0_conv_off_w"].reshape(2 * SAMPLES, C), a["L0_conv_mask_w"]]).T,
        "off_b": np.concatenate([a["L0_conv_off_b"].reshape(-1), a["L0_conv_mask_b"]]).reshape(1, OFFS),
        "grid": grid.reshape(TILES, P, 2 * SAMPLES).transpose(1, 0, 2).astype(f),
        "gcol": np.tile((N * G * np.arange(B))[:, None] + np.repeat(np.arange(G), K), (P, 1, 1)).astype(f),
        "proj_w": a["L0_conv_proj_w"],
        "proj_b": a["L0_conv_proj_b"].reshape(1, C),
        "Wq": a["L1_attn_Wq"],
        "Wk": a["L1_attn_Wk"],
        "Wv": a["L1_attn_Wv"],
        "Wo": a["L1_attn_Wo"],
        "bqkv": np.stack([a[f"L1_attn_b{n}"] for n in "qkv"]).reshape(3, CH, P).transpose(2, 0, 1),
        "bo": a["L1_attn_bo"].reshape(1, C),
        "gate_w": a["L1_ffn_gate_w"],
        "gate_b": a["L1_ffn_gate_b"].reshape(1, E),
        "w1": a["L1_ffn_w1"],
        "b1": a["L1_ffn_b1"].reshape(E, F // P, P).transpose(0, 2, 1),
        "w2": a["L1_ffn_w2"],
        "b2": a["L1_ffn_b2"],
        "upper": np.triu(np.ones((P, P), f), 1),
        "ones": np.ones((P, P), f),
        "prio": np.tile(E - np.arange(E), (P, 1)).astype(f),
        "first": np.tile(CAP * np.arange(E), (P, 1)).astype(f),
        "ident": np.eye(P, dtype=f),
        "grp": (np.kron(np.eye(P // 8), np.ones((8, 8))) / 8).astype(f),
    }
    return {k: np.ascontiguousarray(v) for k, v in io.items()}


def kernel(**inputs):
    import numpy as np
    import concourse.bacc as bacc
    from concourse import mybir as mb
    from concourse.bass_utils import run_bass_kernel_spmd

    nc = bacc.Bacc("TRN2", target_bir_lowering=False, num_devices=1)
    arrays, d = {}, {}
    for name, a in lay_out(inputs).items():
        arrays[f"in_{name}"] = a
        d[name] = nc.dram_tensor(f"in_{name}", a.shape, mb.dt.from_np(a.dtype), kind="ExternalInput").ap()
    out = nc.dram_tensor("out", [B, N, C], F32, kind="ExternalOutput").ap()
    build(nc, d, out)
    r = run_bass_kernel_spmd(nc, [arrays], core_ids=[0])
    return np.asarray(r.results[0]["out"]).reshape(B, H, W, C)
```

```python
from contextlib import ExitStack

import concourse.bass as bass
from concourse import mybir

F32 = mybir.dt.float32
F32R = mybir.dt.float32r
U32 = mybir.dt.uint32
ALU = mybir.AluOpType
ACT = mybir.ActivationFunctionType
AX_X = mybir.AxisListType.X

P = 128
B, H, W, C = 2, 64, 64, 256
N = H * W
CH = C // P
TILES = N // P
G, K, HC = 8, 9, C // 8
CQ = C // 4
TAPS = 9
SAMPLES = G * K
OFFS = 2 * SAMPLES + K
PW = W + 2
PADDED = (H + 2) * PW
KVPAD = N + P
KVWIN = P + W + 1
MT = 3 * C // P
CHUNK = 512
CHUNKS = N // CHUNK
HEADS, HD = 8, 32
QB = 1024
QBS = N // QB
BLOCKS = N // P
ROWS = 3 * HD + 2
STEPS_A = HEADS * QBS
NORM = 5
P_SLOTS, LAG = 3, 2
E, F, CAP = 8, 4 * C, 5 * B * N // (4 * 8)
ROUND = float(2 ** 23)
HALF = 15
REC = 5 * SAMPLES


class Tally:

    def __init__(self, engine, sem, base=0):
        self.engine, self.sem, self.base, self.n = engine, sem, base, 0

    def inc(self, ins):
        ins.then_inc(self.sem, 1)
        self.n += 1

    def link(self, ins):
        self.inc(ins)
        self.engine.wait_ge(self.sem, self.base + self.n)


class Stage(ExitStack):

    def __init__(self, nc):
        super().__init__()
        self.nc, self.sems = nc, []

    def __exit__(self, *error):
        super().__exit__(*error)
        if error[0] is None:
            self.nc.clear_and_free_semaphores(self.sems)
            self.nc.all_engine_barrier()


class Room:

    def __init__(self, nc, stack, stage):
        self.nc, self.stack, self.stage = nc, stack, stage

    def sb(self, name, shape, dt=F32):
        return self.stack.enter_context(self.nc.sbuf_tensor(f"{self.stage}_{name}", shape, dt))

    def ps(self, name, shape, dt=F32):
        return self.stack.enter_context(self.nc.psum_tensor(f"{self.stage}_{name}", shape, dt))

    def sem(self, name):
        sem = self.nc.alloc_semaphore(name=f"{self.stage}_{name}")
        self.stack.sems.append(sem)
        return sem


def prepare_weights(nc, stack, block, d, s, keep, offset_w):
    r = Room(nc, stack, "w")
    pconv = r.sb("pconv", [CQ, G + 1, TAPS, CQ])
    banks = [r.ps(f"ps{i}", [P, 512]) for i in range(2)]
    FILLS = 16
    zeros = r.sb("zeros", [P, E * CAP // P * C // FILLS])
    loaded, zeroed, made, copied = (r.sem(x) for x in ("loaded", "zeroed", "made", "copied"))
    blank, blanked = r.sem("blank"), r.sem("blanked")

    @block.sync
    def _(sp):
        sp.dma_start(pconv[:, :, :, :], d["pconv"]).then_inc(loaded, 16)
        sp.dma_start(offset_w.off_w[:, :, :], d["off_wT"].rearrange("(h p) n -> p h n", p=P)).then_inc(loaded, 16)

    @block.gpsimd
    def _(pool):
        pool.memset(offset_w.taps[:, :, :], 0.0).then_inc(zeroed, 1)
        pool.memset(zeros[:, :], 0.0).then_inc(blank, 1)
        pool.wait_ge(blank, 1)
        for i in range(FILLS):
            pool.dma_start(s["buf"].rearrange("(i p r) n -> i p (r n)", i=FILLS, p=P)[i], zeros[:, :]).then_inc(blanked, 16)

    @block.tensor
    def _(pe):
        pe.wait_ge(loaded, 32)
        for tap in range(TAPS):
            if tap >= 2:
                pe.wait_ge(copied, tap - 1)
            for g in range(G + 1):
                a, b = 2 * K * g, min(2 * K * (g + 1), OFFS)
                mm = pe.matmul(banks[tap % 2][0:CQ, a:b], pconv[:, g, tap, :], offset_w.off_w[0:CQ, 0, a:b],
                               start=True, stop=True)
            mm.then_inc(made, 1)
        pe.wait_ge(copied, TAPS)

    @block.vector
    def _(dve):
        dve.wait_ge(zeroed, 1)
        for tap in range(TAPS):
            dve.wait_ge(made, tap + 1)
            dve.tensor_copy(offset_w.taps[0:CQ, tap, :], banks[tap % 2][0:CQ, 0:OFFS]).then_inc(copied, 1)
        dve.wait_ge(loaded, 32)
        dve.tensor_copy(offset_w.taps[CQ:P, TAPS // 2, :], offset_w.off_w[CQ:P, 0, :]).then_inc(copied, 1)

    def end(pool):
        pool.wait_ge(blanked, 16 * FILLS)

    return banks, end


def stage_maps(nc, d, s, keep, offset_w):
    with Stage(nc) as stack:
        r = Room(nc, stack, "m")
        xt = r.sb("xt", [P, CH, N])
        w = r.sb("w", [P, CH, 3 * C])
        wb = r.sb("wb", [P, MT])
        dw = r.sb("dw", [P, MT, TAPS])
        dwb = r.sb("dwb", [P, MT])
        grp = r.sb("grp", [P, P])
        pad = [r.sb(f"pad{i}", [P, H + 2, PW]) for i in range(2)]
        outq = [r.sb(f"outq{i}", [P, H + 2, PW]) for i in range(2)]
        outkv = [r.sb(f"outkv{i}", [P, KVPAD]) for i in range(2)]
        stats = r.sb("stats", [P, CH, CHUNKS, 6])
        mv = r.sb("mv", [P, CH, 2])
        gmean = r.sb("gmean", [P, CH])
        dev = r.sb("dev", [P, CH])
        var = r.sb("var", [P, CH])
        veps = r.sb("veps", [P, CH])
        std = r.sb("std", [P, CH])
        rstd = r.sb("rstd", [P, CH])
        ps_g = r.ps("g", [P, 512])
        ps = [r.ps(f"ps{i}", [P, 512]) for i in range(4)]
        wts, xt_in = r.sem("wts"), r.sem("xt_in")
        chan_mean, chan_var, grp_mean, grp_var = (r.sem(x) for x in ("cm", "cv", "gm", "gv"))
        var_ready, std_ready, xn_ready = r.sem("var"), r.sem("std"), r.sem("xn")
        qkv_ready, pad_full, pad_free, conv_done = r.sem("qkv"), r.sem("padfull"), r.sem("padfree"), r.sem("conv")
        edges = r.sem("edges")
        q_out = [r.sem(f"qout{i}") for i in range(2)]
        kv_out = [r.sem(f"kvout{i}") for i in range(2)]
        chain = r.sem("chain")
        conv_mm, conv_got, diag_made, ident_in = (r.sem(x) for x in ("conv_mm", "conv_got", "diag", "ident_in"))
        diag = r.sb("diag", [P, MT, TAPS, P])
        block = stack.enter_context(nc.Block())
        ps_d, end_of_weights = prepare_weights(nc, stack, block, d, s, keep, offset_w)
        Q_COPIES = (3, 1)
        LEFT = 2
        ROWS_V = H - LEFT * CHUNK // W
        PER = MT * CHUNKS
        DVE_STEPS = CH * CHUNKS + 7 + MT * (TAPS - 1)

        @block.sync
        def _(sp):
            for h in range(CH):
                sp.dma_start(xt[:, h, :], d["xT"][0, h * P:(h + 1) * P, :]).then_inc(xt_in, 16)
            sp.dma_start(w[:, :, :], d["qkv_w"].rearrange("(h p) n -> p h n", p=P)).then_inc(wts, 16)
            sp.dma_start(wb[:, :], d["qkv_b"]).then_inc(wts, 16)
            sp.dma_start(dw[:, :, :], d["dw_w"]).then_inc(wts, 16)
            sp.dma_start(dwb[:, :], d["dw_b"]).then_inc(wts, 16)
            sp.dma_start(grp[:, :], d["grp"]).then_inc(wts, 16)
            sp.dma_start(keep.ident[:, :], d["ident"]).then_inc(ident_in, 16)

            def load_image(b):
                for h in range(CH):
                    sp.dma_start(xt[:, h, :], d["xT"][b, h * P:(h + 1) * P, :]).then_inc(xt_in, 16)

            for b in range(B):
                for m in range(MT):
                    if m == MT - 1 and b < B - 1:
                        sp.wait_ge(qkv_ready, PER * (b + 1))
                        load_image(b + 1)
                    sp.wait_ge(conv_done, MT * b + m + 1)
                    sp.wait_ge(conv_got, LEFT * (MT * b + m + 1))
                    if m < CH:
                        for dx in range(3) if m == 0 else (1,):
                            sp.dma_start(s["dwq"][b, dx if m == 0 else 3].rearrange("p (r c) -> p r c", c=W),
                                         outq[m][:, :, dx:dx + W]).then_inc(q_out[m], 16)
                    else:
                        sp.dma_start(s["dwkv"][b, m - CH],
                                     outkv[m % 2][:, :]).then_inc(kv_out[m % 2], 16)
            for i in range(2):
                sp.wait_ge(q_out[i], 16 * Q_COPIES[i] * B)
                sp.wait_ge(kv_out[i], 32 * B)

        @block.gpsimd
        def _(pool):
            for t in pad:
                pool.memset(t[:, :, :], 0.0).then_inc(pad_free, 1)
            for t in outq:
                pool.memset(t[:, :, :], 0.0).then_inc(edges, 1)
            for t in outkv:
                pool.memset(t[:, :], 0.0).then_inc(edges, 1)
            end_of_weights(pool)

        @block.tensor
        def _(pe):
            pe.wait_ge(wts, 80)
            pe.wait_ge(diag_made, MT * TAPS)
            with pe.Fori(0, B) as b:
                pe.wait_ge(chan_mean, b + 1)
                pe.matmul(ps_g[:, 0:CH], grp[:, :], mv[:, :, 0], start=True, stop=True).then_inc(grp_mean, 1)
                pe.wait_ge(chan_var, b + 1)
                pe.matmul(ps_g[:, CH:2 * CH], grp[:, :], var[:, :], start=True, stop=True).then_inc(grp_var, 1)
                pe.wait_ge(xn_ready, b + 1)

                def depthwise(m):
                    pe.wait_ge(pad_full, PER * b + CHUNKS * (m + 1))
                    for c in range(LEFT):
                        pe.wait_ge(conv_got, LEFT * (MT * b + m))
                        for tap in range(TAPS):
                            dy, dx = divmod(tap, 3)
                            row = ROWS_V + c * CHUNK // W + dy
                            mm = pe.matmul(ps_d[c][:, :], diag[:, m, tap, :], pad[m % 2][:, row:row + CHUNK // W, dx:dx + W],
                                           start=(tap == 0), stop=(tap == TAPS - 1))
                        mm.then_inc(conv_mm, 1)

                for i in range(PER):
                    m, c = divmod(i, CHUNKS)
                    if c == 0 and m >= 2:
                        depthwise(m - 2)
                    pe.wait_ge(pad_full, PER * b + max(i - 3, 0))
                    for h in range(CH):
                        mm = pe.matmul(ps[i % 4][:, :], w[:, h, m * P:(m + 1) * P],
                                       xt[:, h, c * CHUNK:(c + 1) * CHUNK], start=(h == 0), stop=(h == CH - 1))
                    mm.then_inc(qkv_ready, 1)
                for m in range(MT - 2, MT):
                    depthwise(m)

        @block.scalar
        def _(act):
            act.wait_ge(wts, 80)
            act.wait_ge(ident_in, 16)
            for m in range(MT):
                for tap in range(TAPS):
                    act.activation(diag[:, m, tap, :], keep.ident[:, :], ACT.Copy, scale=dw[:, m, tap:tap + 1]).then_inc(diag_made, 1)
            act.wait_ge(edges, 4)
            with act.Fori(0, B) as b:
                act.wait_ge(var_ready, b + 1)
                act.activation(std[:, :], veps[:, :], ACT.Sqrt).then_inc(std_ready, 1)

                def depthwise(m):
                    if m < CH:
                        act.wait_ge(q_out[m], 16 * Q_COPIES[m] * b)
                        acc = outq[m][:, 1:1 + H, 1:1 + W]
                    else:
                        act.wait_ge(kv_out[m % 2], 32 * b + 16 * ((m - CH) // 2))
                        acc = outkv[m % 2][:, 0:N].rearrange("p (r c) -> p r c", c=W)
                    for c in range(LEFT):
                        row = ROWS_V + c * CHUNK // W
                        act.wait_ge(conv_mm, LEFT * (MT * b + m) + c + 1)
                        act.activation(acc[:, row:row + CHUNK // W, :], ps_d[c][:, :].rearrange("p (r c) -> p r c", c=W),
                                       ACT.Identity, bias=dwb[:, m:m + 1]).then_inc(conv_got, 1)

                for i in range(PER):
                    m, c = divmod(i, CHUNKS)
                    if c == 0 and m >= 2:
                        depthwise(m - 2)
                    if c == 0:
                        act.wait_ge(pad_free, MT * b + m + 1)
                    act.wait_ge(qkv_ready, PER * b + i + 1)
                    rows = CHUNK // W
                    act.activation(pad[m % 2][:, 1 + c * rows:1 + (c + 1) * rows, 1:1 + W],
                                   ps[i % 4][:, :].rearrange("p (r c) -> p r c", c=W), ACT.Identity,
                                   bias=wb[:, m:m + 1]).then_inc(pad_full, 1)
                for m in range(MT - 2, MT):
                    depthwise(m)

        @block.vector
        def _(dve):
            dve.wait_ge(wts, 80)
            dve.wait_ge(edges, 4)
            with dve.Fori(0, B) as b:
                t = Tally(dve, chain, DVE_STEPS * b)
                dve.wait_ge(xt_in, 16 * CH * b + 16 * CH)
                for h in range(CH):
                    for c in range(CHUNKS):
                        t.inc(dve.bn_stats(stats[:, h, c, :], xt[:, h, c * CHUNK:(c + 1) * CHUNK]))
                dve.wait_ge(chain, t.base + t.n)
                dve.memset(veps[:, :], 0.0)
                t.inc(dve.bn_aggr(mv[:, 0, :], stats[:, 0, :, :].rearrange("p c s -> p (c s)")))
                dve.bn_aggr(mv[:, 1, :], stats[:, 1, :, :].rearrange("p c s -> p (c s)")).then_inc(chan_mean, 1)
                dve.wait_ge(grp_mean, b + 1)
                t.link(dve.tensor_copy(gmean[:, :], ps_g[:, 0:CH]))
                t.link(dve.tensor_tensor(dev[:, :], mv[:, :, 0], gmean[:, :], ALU.subtract))
                t.link(dve.tensor_tensor(dev[:, :], dev[:, :], dev[:, :], ALU.mult))
                dve.tensor_tensor(var[:, :], dev[:, :], mv[:, :, 1], ALU.add).then_inc(chan_var, 1)
                dve.wait_ge(grp_var, b + 1)
                dve.tensor_scalar(veps[:, :], ps_g[:, CH:2 * CH], 1e-5, None, ALU.add).then_inc(var_ready, 1)
                dve.wait_ge(std_ready, b + 1)
                t.link(dve.reciprocal(rstd[:, :], std[:, :]))
                for h in range(CH):
                    t.inc(dve.tensor_scalar(xt[:, h, :], xt[:, h, :], gmean[:, h:h + 1], rstd[:, h:h + 1],
                                            ALU.subtract, ALU.mult))
                dve.wait_ge(chain, t.base + t.n)
                dve.tensor_copy(dev[:, :], rstd[:, :]).then_inc(xn_ready, 1)
                for m in range(MT):
                    dve.wait_ge(pad_full, PER * b + CHUNKS * (m + 1))
                    if m < CH:
                        dve.wait_ge(q_out[m], 16 * Q_COPIES[m] * b)
                        acc = outq[m][:, 1:1 + ROWS_V, 1:1 + W]
                    else:
                        dve.wait_ge(kv_out[m % 2], 32 * b + 16 * ((m - CH) // 2))
                        acc = outkv[m % 2][:, 0:ROWS_V * W].rearrange("p (r c) -> p r c", c=W)
                    for tap in range(TAPS):
                        dy, dx = divmod(tap, 3)
                        win = pad[m % 2][:, dy:dy + ROWS_V, dx:dx + W]
                        wt = dw[:, m, tap:tap + 1]
                        if tap == 0:
                            t.link(dve.tensor_scalar(acc, win, wt, dwb[:, m:m + 1], ALU.mult, ALU.add))
                        elif tap < TAPS - 1:
                            t.link(dve.scalar_tensor_tensor(out=acc, in0=win, scalar=wt, in1=acc, op0=ALU.mult, op1=ALU.add))
                        else:
                            dve.scalar_tensor_tensor(out=acc, in0=win, scalar=wt, in1=acc, op0=ALU.mult,
                                                     op1=ALU.add).then_inc(conv_done, 1)
                    dve.wait_ge(conv_done, MT * b + m + 1)
                    dve.tensor_copy(dev[:, 0:1], rstd[:, 0:1]).then_inc(pad_free, 1)
                assert t.n == DVE_STEPS, t.n


class Tables:

    def __init__(self, nc, stack, d, s, keep, offset_w, b):
        r = Room(nc, stack, f"t{b}")
        self.d, self.s, self.keep, self.offset_w, self.b = d, s, keep, offset_w, b
        self.qwin = [r.sb(f"qwin{i}", [P, 4, 4 * W]) for i in range(2)]
        self.kvwin = [r.sb(f"kvwin{i}", [P, 2 * CH, KVWIN]) for i in range(2)]
        self.qpix = [r.sb(f"qpix{i}", [P, C]) for i in range(2)]
        self.rows = [r.sb(f"rows{i}", [P, G, 4, 2, HC]) for i in range(2)]
        self.bias = r.sb("bias", [P, OFFS])
        self.grid = r.sb("grid", [P, TILES, 2 * SAMPLES])
        self.gcol = r.sb("gcol", [P, SAMPLES])
        self.off = r.sb("off", [P, 2, OFFS])
        self.pos = r.sb("pos", [P, 2, 2 * SAMPLES])
        self.low = r.sb("low", [P, 2, 2 * SAMPLES])
        self.tmp = r.sb("tmp", [P, 2, 2 * SAMPLES])
        self.rec = r.sb("rec", [P, 2, REC])
        self.ps_off = [r.ps(f"off{i}", [P, 512]) for i in range(2)]
        self.ps_q = r.ps("q", [P, 512])
        self.ps_kv = [r.ps(f"kv{i}", [P, 512]) for i in range(4)]
        self.consts = r.sem("consts")
        self.qwin_in = [r.sem(f"qwin_in{i}") for i in range(2)]
        self.kvwin_in = [r.sem(f"kvwin_in{i}") for i in range(2)]
        self.off_mm, self.q_mm, self.kv_mm = r.sem("off_mm"), r.sem("q_mm"), r.sem("kv_mm")
        self.off_got, self.q_got, self.kv_act, self.kv_dve = (r.sem(x) for x in ("off_got", "q_got", "kv_act", "kv_dve"))
        self.q_out = [r.sem(f"q_out{i}") for i in range(2)]
        self.rows_out = [r.sem(f"rows_out{i}") for i in range(2)]
        self.chain, self.rec_ready, self.rec_out = r.sem("chain"), r.sem("rec_ready"), r.sem("rec_out")

    def load_constants(self, sp):
        sp.dma_start(self.bias[:, :], self.d["off_b"].to_broadcast([P, OFFS])).then_inc(self.consts, 16)
        sp.dma_start(self.grid[:, :, :], self.d["grid"]).then_inc(self.consts, 16)
        sp.dma_start(self.gcol[:, :], self.d["gcol"]).then_inc(self.consts, 16)

    def load(self, sp, t, u):
        sp.dma_start(self.qwin[u][:, :, :], self.s["dwq"][self.b, :, :, bass.ds(t * P, 4 * W)].rearrange("h p n -> p h n"))\
            .then_inc(self.qwin_in[u], 16)
        sp.dma_start(self.kvwin[u][:, :, :], self.s["dwkv"][self.b, :, :, bass.ds(t * P, KVWIN)].rearrange("h p n -> p h n"))\
            .then_inc(self.kvwin_in[u], 16)

    def reload(self, sp, t, u):
        sp.wait_ge(self.kv_mm, 4 * t + 4)
        self.load(sp, t + 2, u)

    def store(self, sp, i):
        sp.wait_ge(self.rec_ready, i + 1)
        sp.dma_start(self.s["rec"][self.b, bass.ds(2 * i, 2)].rearrange("t p n -> p t n"), self.rec[:, :, :]).then_inc(self.rec_out, 16)

    def end_sync(self, sp):
        sp.wait_ge(self.rec_out, 16 * TILES // 2)

    def multiply(self, pe, i, u):
        pe.wait_ge(self.qwin_in[u], 16 * i + 16)
        pe.wait_ge(self.off_got, 2 * i)
        for tap in range(TAPS):
            dy, dx = divmod(tap, 3)
            pe.matmul(self.ps_off[u][:, 0:OFFS], self.qwin[u][:, dx, dy * W:dy * W + P], self.offset_w.taps[:, tap, :],
                      start=(tap == 0), stop=False)
        pe.matmul(self.ps_off[u][:, 0:OFFS], self.qwin[u][:, 3, W:W + P], self.offset_w.off_w[:, 1, :],
                  start=False, stop=True).then_inc(self.off_mm, 1)
        pe.wait_ge(self.q_got, 2 * i + u)
        for h in range(CH):
            mm = pe.transpose(self.ps_q[:, h * P:(h + 1) * P], self.qwin[u][:, 1 + 2 * h, W:W + P], self.keep.ident[:, :])
        mm.then_inc(self.q_mm, 1)
        pe.wait_ge(self.kvwin_in[u], 16 * i + 16)
        for c in range(4):
            pe.wait_ge(self.kv_act if c < 2 else self.kv_dve, 4 * i + (2 * u if u else 0))
            at = (c // 2) * W + c % 2
            for m in range(2 * CH):
                mm = pe.transpose(self.ps_kv[c][:, m * P:(m + 1) * P], self.kvwin[u][:, m, at:at + P], self.keep.ident[:, :])
            mm.then_inc(self.kv_mm, 1)

    def corner(self, u, c):
        return (self.rows[u][:, :, c, :, :].rearrange("p g a c -> p a g c"),
                self.ps_kv[c][:, :].rearrange("p (a g c) -> p a g c", a=2, g=G))

    def copy_out(self, act, i, u):
        act.wait_ge(self.q_mm, 2 * i + u + 1)
        act.wait_ge(self.q_out[u], 16 * i)
        act.activation(self.qpix[u][:, :], self.ps_q[:, 0:C], ACT.Copy).then_inc(self.q_got, 1)
        act.wait_ge(self.q_got, 2 * i + u + 1)
        act.dma_start(self.s["qpix"][self.b, bass.ds(2 * i + u, 1)].rearrange("t p n -> (t p) n"),
                      self.qpix[u][:, :]).then_inc(self.q_out[u], 16)
        act.wait_ge(self.rows_out[u], 16 * i)
        for c in range(2):
            act.wait_ge(self.kv_mm, 8 * i + 4 * u + c + 1)
            out, src = self.corner(u, c)
            act.activation(out, src, ACT.Copy).then_inc(self.kv_act, 1)
        act.wait_ge(self.kv_act, 4 * i + 2 * u + 2)
        act.wait_ge(self.kv_dve, 4 * i + 2 * u + 2)
        act.dma_start(self.s["table"][self.b][bass.ds(2 * i + u, 1)].rearrange("t p n -> (t p) n"),
                      self.rows[u][:, :, :, :, :].rearrange("p g c a n -> p (g c a n)")).then_inc(self.rows_out[u], 16)

    def end_scalar(self, act):
        for u in range(2):
            act.wait_ge(self.q_out[u], 16 * TILES // 2)
            act.wait_ge(self.rows_out[u], 16 * TILES // 2)

    def begin(self, dve):
        dve.wait_ge(self.consts, 48)

    def add_bias(self, dve, i, u):
        dve.wait_ge(self.off_mm, 2 * i + u + 1)
        dve.tensor_tensor(self.off[:, u, :],
                          self.ps_off[u][:, 0:OFFS], self.bias[:, :], ALU.add).then_inc(self.off_got, 1)
        dve.wait_ge(self.rows_out[u], 16 * i)
        for c in range(2, 4):
            dve.wait_ge(self.kv_mm, 8 * i + 4 * u + c + 1)
            out, src = self.corner(u, c)
            dve.tensor_copy(out, src).then_inc(self.kv_dve, 1)

    def records(self, dve, i):
        CALC = 9
        t = Tally(dve, self.chain, CALC * i)
        dve.wait_ge(self.off_got, 2 * i + 2)
        dve.wait_ge(self.rec_out, 16 * i)
        t.link(dve.tensor_tensor(self.pos[:, :, :], self.off[:, :, 0:2 * SAMPLES], self.grid[:, bass.ds(2 * i, 2), :], ALU.add))
        t.link(dve.tensor_scalar(self.pos[:, :, :], self.pos[:, :, :], 0.0, float(W - 1), ALU.max, ALU.min))
        t.link(dve.tensor_scalar(self.low[:, :, :], self.pos[:, :, :], ROUND, -ROUND, ALU.add, ALU.add))
        t.link(dve.tensor_tensor(self.tmp[:, :, :], self.low[:, :, :], self.pos[:, :, :], ALU.is_gt))
        t.link(dve.tensor_tensor(self.low[:, :, :], self.low[:, :, :], self.tmp[:, :, :], ALU.subtract))
        t.link(dve.tensor_tensor(self.pos[:, :, :], self.pos[:, :, :], self.low[:, :, :], ALU.subtract))
        pix = self.tmp[:, :, 0:SAMPLES]
        wx = self.pos[:, :, :].rearrange("p t (g k c) -> p t g k c", g=G, c=2)
        mask = self.off[:, :, 2 * SAMPLES:OFFS].unsqueeze(2).to_broadcast([P, 2, G, K])
        xw = self.rec[:, :, SAMPLES:3 * SAMPLES].rearrange("p t (g k c) -> p t g k c", g=G, c=2)
        yw = self.rec[:, :, 3 * SAMPLES:5 * SAMPLES].rearrange("p t (k c) -> p t k c", c=2)
        wy = self.pos[:, :, :].rearrange("p t (k c) -> p t k c", c=2)
        low2 = self.low[:, :, :].rearrange("p t (k c) -> p t k c", c=2)
        t.link(dve.scalar_tensor_tensor(out=pix, in0=low2[:, :, :, 1], scalar=float(W), in1=low2[:, :, :, 0],
                                        op0=ALU.mult, op1=ALU.add))
        dve.scalar_tensor_tensor(out=self.rec[:, :, 0:SAMPLES].bitcast(U32), in0=pix, scalar=float(G),
                                 in1=self.gcol[:, :].unsqueeze(1).to_broadcast([P, 2, SAMPLES]),
                                 op0=ALU.mult, op1=ALU.add)
        t.link(dve.tensor_tensor(xw[:, :, :, :, 1], wx[:, :, :, :, 0], mask, ALU.mult))
        dve.tensor_tensor(xw[:, :, :, :, 0], mask, xw[:, :, :, :, 1], ALU.subtract)
        dve.tensor_copy(yw[:, :, :, 1], wy[:, :, :, 1])
        t.link(dve.tensor_scalar(yw[:, :, :, 0], wy[:, :, :, 1], -1.0, 1.0, ALU.mult, ALU.add))
        dve.tensor_copy(self.tmp[:, 0, 0:1], self.pos[:, 0, 0:1]).then_inc(self.rec_ready, 1)
        assert t.n == CALC, t.n


def stage_tables(nc, d, s, keep, offset_w, b):
    with Stage(nc) as stack:
        ta = Tables(nc, stack, d, s, keep, offset_w, b)
        block = stack.enter_context(nc.Block())
        TURNS = TILES // 2

        @block.sync
        def _(sp):
            ta.load_constants(sp)
            for u in range(2):
                ta.load(sp, u, u)
            with sp.Fori(0, TURNS - 1) as i:
                for u in range(2):
                    ta.reload(sp, 2 * i + u, u)
                ta.store(sp, i)
            ta.store(sp, TURNS - 1)
            ta.end_sync(sp)

        @block.tensor
        def _(pe):
            with pe.Fori(0, TURNS) as i:
                for u in range(2):
                    ta.multiply(pe, i, u)

        @block.scalar
        def _(act):
            with act.Fori(0, TURNS) as i:
                for u in range(2):
                    ta.copy_out(act, i, u)
            ta.end_scalar(act)

        @block.vector
        def _(dve):
            ta.begin(dve)
            with dve.Fori(0, TURNS) as i:
                for u in range(2):
                    ta.add_bias(dve, i, u)
                ta.records(dve, i)


class Sampling:

    def __init__(self, nc, stack, d, s, keep, b, vals=2):
        r = Room(nc, stack, f"s{b}")
        self.one_vals = vals == 1
        self.nc, self.d, self.s, self.keep, self.b = nc, d, s, keep, b
        self.rec = [r.sb(f"rec{i}", [P, REC]) for i in range(2)]
        self.q = [r.sb(f"q{i}", [P, C]) for i in range(2)]
        self.x = [r.sb(f"x{i}", [P, C]) for i in range(2)]
        self.x1 = [r.sb(f"x1{i}", [P, C]) for i in range(2)]
        self.slot = [r.sb(f"slot{g}", [P, K, 4, 2, HC]) for g in range(G)]
        own = [r.sb(f"vals{i}", [P, 4 * K, P]) for i in range(vals)]
        self.vals = [own[0], own[-1]]
        self.proj_w = r.sb("proj_w", [P, CH, C])
        self.proj_b = r.sb("proj_b", [P, C])
        self.outT = r.sb("outT", [P, CH, P])
        self.dots = [r.sb(f"dots{i}", [P, 4, K, 4]) for i in range(2)]
        self.corner = [r.sb(f"corner{i}", [P, 4 * K, 2, 2]) for i in range(2)]
        self.logit = [r.sb(f"logit{i}", [P, 4, K]) for i in range(2)]
        self.top = [r.sb(f"top{i}", [P, 4]) for i in range(2)]
        self.prob = [r.sb(f"prob{i}", [P, 4, K]) for i in range(2)]
        self.total = [r.sb(f"total{i}", [P, 4]) for i in range(2)]
        self.share = [r.sb(f"share{i}", [P, 4]) for i in range(2)]
        self.const_in = r.sem("const_in")
        self.slots_free = r.sem("slots_free")
        self.gathered = [r.sem(f"gathered{g}") for g in range(G)]
        self.values_made = r.sem("values_made")
        self.values_summed = r.sem("values_summed")
        self.logits_made = r.sem("logits_made")
        self.probs_made = r.sem("probs_made")
        self.outT_made = r.sem("outT_made")
        self.projected = r.sem("projected")
        self.x1_made = r.sem("x1_made")
        self.x1_out = [r.sem(f"x1_out{i}") for i in range(2)]
        self.chain = r.sem("chain")
        self.tile_in = [r.sem(f"tile_in{i}") for i in range(2)]
        self.x_in = [r.sem(f"x_in{i}") for i in range(2)]
        self.biased = r.sem("biased")
        self.STEPS = 2 + 2 * G + 2 * 7

    def ps_in_one_bank(self, r):
        ps = r.ps("sums", [P, 512])
        self.ps_sum = [ps[:, i * P:(i + 1) * P] for i in range(2)]
        self.ps_proj = ps[:, C:2 * C]

    def load_constants(self, sp):
        sp.dma_start(self.proj_w[:, :, :], self.d["proj_w"].rearrange("(h p) n -> p h n", p=P)).then_inc(self.const_in, 16)
        sp.dma_start(self.proj_b[:, :], self.d["proj_b"].to_broadcast([P, C])).then_inc(self.const_in, 16)

    def load_tile(self, sp, n, u):
        b = self.b
        flat = "a p n -> (a p) n"
        sp.dma_start(self.rec[u][:, :], self.s["rec"][b, bass.ds(n, 1)].rearrange(flat)).then_inc(self.tile_in[u], 16)
        sp.dma_start(self.q[u][:, :], self.s["qpix"][b, bass.ds(n, 1)].rearrange(flat)).then_inc(self.tile_in[u], 16)

    def load_x(self, sp, n, u):
        sp.dma_start(self.x[u][:, :], self.d["x"][self.b].rearrange("(t p) n -> t p n", p=P)[bass.ds(n, 1)]
                     .rearrange("a p n -> (a p) n"))\
            .then_inc(self.x_in[u], 16)

    def reload(self, sp, n, u):
        sp.wait_ge(self.values_made, G * n + G + 5)
        self.load_tile(sp, n + 2, u)

    def store_tile(self, sp, n, u):
        sp.wait_ge(self.x1_made, n + 1)
        sp.dma_start(self.s["x1"][self.b, bass.ds(n, 1)].rearrange("a p n -> (a p) n"), self.x1[u][:, :])\
            .then_inc(self.x1_out[u], 16)

    def wait_stores(self, sp):
        for u in range(2):
            sp.wait_ge(self.x1_out[u], 16 * TILES // 2)

    def gather(self, pool, n, turn, u, g):
        if g == 0:
            pool.wait_ge(self.tile_in[u], 32 * turn + 32)
        pool.wait_ge(self.values_made, G * n + g + 1)
        pool.sem_inc(self.slots_free, 1)
        for k in range(K):
            pool.indirect_dma_start(
                out=self.slot[g][:, k, :, :, :].rearrange("p c a n -> p (c a n)"), out_offset=None,
                in_=self.s["table"][self.b].rearrange("t p (g n) -> (t p g) n", g=G),
                in_offset=bass.IndirectOffsetOnAxis(ap=self.rec[u][:, g * K + k:g * K + k + 1].bitcast(U32), axis=0),
            ).then_inc(self.gathered[g], 16)

    def begin(self, dve):
        dve.wait_ge(self.const_in, 32)
        dve.sem_inc(self.values_made, G)

    def tally(self, dve, n):
        return Tally(dve, self.chain, self.STEPS * n)

    def tile_start(self, dve, t, n, turn, u):
        dve.wait_ge(self.tile_in[u], 32 * turn + 32)
        for i in range(2):
            w = self.rec[u][:, SAMPLES + i * SAMPLES:SAMPLES + (i + 1) * SAMPLES].rearrange("p (k x) -> p k x", x=2)
            v = self.rec[u][:, (3 + i) * SAMPLES:(4 + i) * SAMPLES].rearrange("p (k y) -> p k y", y=2)
            t.inc(dve.tensor_tensor(self.corner[i][:, :, :, :], v.unsqueeze(3).to_broadcast([P, 4 * K, 2, 2]),
                                    w.unsqueeze(2).to_broadcast([P, 4 * K, 2, 2]), ALU.mult))

    def q_times_k(self, dve, t, n, u, g):
        dve.wait_ge(self.gathered[g], 16 * K * n + 16 * K)
        k = self.slot[g][:, :, :, 0, :].rearrange("p k c n -> p (k c) n")
        q = self.q[u][:, g * HC:(g + 1) * HC].unsqueeze(1).to_broadcast([P, 4 * K, HC])
        t.inc(dve.tensor_tensor(k, k, q, ALU.mult))

    def scores(self, dve, t, n, g):
        k = self.slot[g][:, :, :, 0, :].rearrange("p k c n -> p (k c) n")
        dve.wait_ge(self.chain, t.base + t.n)
        t.inc(dve.tensor_reduce(self.dots[g // 4][:, g % 4, :, :].rearrange("p k c -> p (k c)"), k, AX_X, ALU.add))

    def logits(self, dve, t, n, i):
        dots = self.dots[i][:, :, :, :].rearrange("p g k c -> p (g k) c")
        dve.wait_ge(self.chain, t.base + t.n)
        t.link(dve.tensor_tensor(dots, dots, self.corner[i][:, :, :, :].rearrange("p k y x -> p k (y x)"), ALU.mult))
        t.link(dve.tensor_reduce(self.logit[i][:, :, :].rearrange("p g k -> p (g k)"), dots, AX_X, ALU.add))
        t.link(dve.tensor_reduce(self.top[i][:, :], self.logit[i][:, :, :], AX_X, ALU.max))
        dve.tensor_tensor(self.logit[i][:, :, :], self.logit[i][:, :, :],
                          self.top[i][:, :].unsqueeze(2).to_broadcast([P, 4, K]), ALU.subtract).then_inc(self.logits_made, 1)

    def weights(self, dve, t, n, i):
        dve.wait_ge(self.probs_made, 2 * n + i + 1)
        t.link(dve.tensor_reduce(self.total[i][:, :], self.prob[i][:, :, :], AX_X, ALU.add))
        t.link(dve.reciprocal(self.share[i][:, :], self.total[i][:, :]))
        t.link(dve.tensor_tensor(self.prob[i][:, :, :], self.prob[i][:, :, :],
                                 self.share[i][:, :].unsqueeze(2).to_broadcast([P, 4, K]), ALU.mult))
        c = self.corner[i][:, :, :, :].rearrange("p k y x -> p k (y x)")
        p = self.prob[i][:, :, :].rearrange("p g k -> p (g k)").unsqueeze(2).to_broadcast([P, 4 * K, 4])
        t.link(dve.tensor_tensor(c, c, p, ALU.mult))

    def piece(self, dve, t, n, turn, u, slot):
        i, m = divmod(slot, HALF)
        if i > 1:
            return
        if slot == 0:
            self.tile_start(dve, t, n, turn, u)
        if m < 8 and m % 2 == 0:
            self.q_times_k(dve, t, n, u, 4 * i + m // 2)
        elif m < 8:
            self.scores(dve, t, n, 4 * i + m // 2)
        elif m == 8:
            self.logits(dve, t, n, i)
        elif m == 10:
            self.weights(dve, t, n, i)
        elif m > 10:
            self.values(dve, n, 4 * i + m - 11)

    def values(self, dve, n, g):
        i, j = divmod(g, 4)
        if j == 0:
            dve.wait_ge(self.values_summed, 2 * n + i + int(self.one_vals))
        v = self.slot[g][:, :, :, 1, :].rearrange("p k c n -> p (k c) n")
        w = self.corner[i][:, j * K:(j + 1) * K, :, :].rearrange("p k y x -> p (k y x)").unsqueeze(2)
        dve.tensor_tensor(self.vals[i][:, :, j * HC:(j + 1) * HC], v, w.to_broadcast([P, 4 * K, HC]), ALU.mult)\
            .then_inc(self.values_made, 1)

    def add_residual(self, dve, n, turn, u):
        dve.wait_ge(self.x_in[u], 16 * turn + 16)
        dve.tensor_tensor(self.x[u][:, :], self.x[u][:, :], self.proj_b[:, :], ALU.add).then_inc(self.biased, 1)
        dve.wait_ge(self.biased, n + 1)
        dve.wait_ge(self.projected, n + 1)
        dve.wait_ge(self.x1_out[u], 16 * turn)
        dve.tensor_tensor(self.x1[u][:, :], self.ps_proj, self.x[u][:, :], ALU.add).then_inc(self.x1_made, 1)

    def exps(self, act, n, i):
        act.wait_ge(self.logits_made, 2 * n + i + 1)
        act.activation(self.prob[i][:, :, :], self.logit[i][:, :, :], ACT.Exp, scale=float(HC) ** -0.5)\
            .then_inc(self.probs_made, 1)

    def copy_out(self, act, n, i):
        act.wait_ge(self.values_summed, 2 * n + i + 2)
        if i == 0:
            act.wait_ge(self.projected, n)
        act.activation(self.outT[:, i, :], self.ps_sum[i], ACT.Copy).then_inc(self.outT_made, 1)

    def pe_begin(self, pe):
        pe.wait_ge(self.const_in, 32)
        pe.sem_inc(self.values_summed, 1)

    def sum_values(self, pe, n, i, part, parts):
        if part == 0:
            pe.wait_ge(self.values_made, G * n + 4 * i + 4 + G)
            if i == 0:
                pe.wait_ge(self.x1_made, n)
            else:
                pe.wait_ge(self.outT_made, 2 * n + 1)
        step = 4 * K // parts
        for j in range(part * step, (part + 1) * step):
            mm = pe.matmul(self.ps_sum[i], self.vals[i][:, j, :], self.keep.ident[:, :],
                           start=(j == 0), stop=(j == 4 * K - 1))
        if part == parts - 1:
            mm.then_inc(self.values_summed, 1)

    def project(self, pe, n):
        pe.wait_ge(self.outT_made, 2 * n + 2)
        for i in range(CH):
            mm = pe.matmul(self.ps_proj, self.outT[:, i, :], self.proj_w[:, i, :], start=(i == 0), stop=(i == CH - 1))
        mm.then_inc(self.projected, 1)


def stage_sample(nc, d, s, keep, offset_w, b, tables):
    with Stage(nc) as stack:
        sa = Sampling(nc, stack, d, s, keep, b, vals=1)
        ta = Tables(nc, stack, d, s, keep, offset_w, tables)
        sa.ps_in_one_bank(Room(nc, stack, f"sp{b}"))
        block = stack.enter_context(nc.Block())
        PAIRS = TILES // 2

        @block.sync
        def _(sp):
            ta.load_constants(sp)
            sa.load_constants(sp)
            for u in range(2):
                sa.load_tile(sp, u, u)
                sa.load_x(sp, u, u)
                ta.load(sp, u, u)
            with sp.Fori(0, PAIRS - 1) as i:
                for u in range(2):
                    n = 2 * i + u
                    ta.reload(sp, n, u)
                    if u == 1:
                        ta.store(sp, i)
                    sa.reload(sp, n, u)
                    sa.store_tile(sp, n, u)
                    sa.load_x(sp, n + 2, u)
            ta.store(sp, PAIRS - 1)
            for u in range(2):
                sa.store_tile(sp, TILES - 2 + u, u)
            ta.end_sync(sp)
            sa.wait_stores(sp)

        @block.gpsimd
        def _(pool):
            with pool.Fori(0, PAIRS) as i:
                for u in range(2):
                    for g in range(G):
                        sa.gather(pool, 2 * i + u, i, u, g)

        @block.vector
        def _(dve):
            ta.begin(dve)
            sa.begin(dve)
            with dve.Fori(0, PAIRS) as i:
                for u in range(2):
                    n = 2 * i + u
                    ta.add_bias(dve, i, u)
                    if u == 1:
                        ta.records(dve, i)
                    t = sa.tally(dve, n)
                    for slot in range(2 * HALF):
                        sa.piece(dve, t, n, i, u, slot)
                    sa.add_residual(dve, n, i, u)
                    assert t.n == sa.STEPS, t.n

        @block.scalar
        def _(act):
            with act.Fori(0, PAIRS) as i:
                for u in range(2):
                    n = 2 * i + u
                    ta.copy_out(act, i, u)
                    for half in range(2):
                        sa.exps(act, n, half)
                        sa.copy_out(act, n, half)
            ta.end_scalar(act)

        @block.tensor
        def _(pe):
            sa.pe_begin(pe)
            with pe.Fori(0, PAIRS) as i:
                for u in range(2):
                    n = 2 * i + u
                    ta.multiply(pe, i, u)
                    for half in range(2):
                        sa.sum_values(pe, n, half, 0, 1)
                    sa.project(pe, n)


def stage_project(nc, d, s, keep, b):
    with Stage(nc) as stack:
        r = Room(nc, stack, f"p{b}")
        x = r.sb("x", [P, TILES, C])
        hT = r.sb("hT", [P, CH, N + 2])
        w = r.sb("w", [P, 3, 3, CH, C])
        wb = r.sb("wb", [P, 3, CH])
        bo = r.sb("bo", [P, C])
        h = [r.sb(f"h{i}", [P, C]) for i in range(2)]
        hi = [r.sb(f"hi{i}", [P, QB], F32R) for i in range(2)]
        lo = [r.sb(f"lo{i}", [P, QB], F32R) for i in range(2)]
        vT = [r.sb(f"vT{i}", [P, QB]) for i in range(2)]
        va = [r.sb(f"va{i}", [P, 4, QB // P, 2 * HD]) for i in range(2)]
        norm = Norm(r, TILES)
        ps_c = [r.ps(f"c{i}", [P, QB]) for i in range(2)]
        ps_h = [r.ps(f"ps_h{i}", [P, 512]) for i in range(2)]
        ps_v = [r.ps(f"ps_v{i}", [P, 512]) for i in range(2)]
        consts, x_in, edges = r.sem("consts"), r.sem("x_in"), r.sem("edges")
        h_made, hT_mm, hT_made, base_made, base_out = (r.sem(n) for n in ("hm", "hTmm", "hTm", "bm", "bo"))
        conv_mm, act_got, lo_made, vT_mm, va_made = (r.sem(n) for n in ("cmm", "ag", "lm", "vmm", "vam"))
        parts_out = [r.sem(f"parts_out{i}") for i in range(2)]
        va_out = [r.sem(f"va_out{i}") for i in range(2)]
        block = stack.enter_context(nc.Block())
        names = ("Wq", "Wk", "Wv")
        STEPS = 6

        @block.sync
        def _(sp):
            sp.dma_start(x[:, :, :], s["x1"][b].rearrange("t p n -> p t n")).then_inc(x_in, 16)
            for i, name in enumerate(names):
                for tap in range(3):
                    sp.dma_start(w[:, i, tap, :, :], d[name][tap].rearrange("(h p) n -> p h n", p=P)).then_inc(consts, 16)
            sp.dma_start(wb[:, :, :], d["bqkv"]).then_inc(consts, 16)
            sp.dma_start(bo[:, :], d["bo"].to_broadcast([P, C])).then_inc(consts, 16)
            sp.wait_ge(base_made, TILES)
            sp.dma_start(s["base"][b].rearrange("t p n -> p t n"), x[:, :, :]).then_inc(base_out, 16)
            with sp.Fori(0, QBS) as c:
                for k in range(4):
                    sp.wait_ge(lo_made, 4 * c + k + 1)
                    u, m = k % 2, k % 2
                    if k < 2:
                        dst = s["q"][b].rearrange("(h q) r n -> h q r n", q=QBS)[4 * m:4 * m + 4, bass.ds(c, 1)]\
                            .rearrange("h q r n -> (h q) r n")
                        order = (hi, hi, lo)
                    else:
                        dst = s["k"][b, 4 * m:4 * m + 4, :, bass.ds(c * QB, QB)]
                        order = (hi, lo, hi)
                    for j, part in enumerate(order):
                        sp.dma_start(dst[:, j * HD:(j + 1) * HD, :], part[u][:, :].bitcast(F32)).then_inc(parts_out[u], 16)
                for m in range(CH):
                    sp.wait_ge(va_made, 4 * c + 2 * m + 2)
                    sp.dma_start(s["v"][b, 4 * m:4 * m + 4, :, bass.ds(c * QB // P * 2 * HD, QB // P * 2 * HD)]
                                 .rearrange("h p n -> p h n"), va[m][:, :, :, :].rearrange("p h k n -> p h (k n)"))\
                        .then_inc(va_out[m], 16)
            sp.wait_ge(base_out, 16)
            for u in range(2):
                sp.wait_ge(parts_out[u], 96 * QBS)
                sp.wait_ge(va_out[u], 16 * QBS)

        @block.gpsimd
        def _(pool):
            pool.memset(hT[:, :, 0:1], 0.0).then_inc(edges, 1)
            pool.memset(hT[:, :, N + 1:N + 2], 0.0).then_inc(edges, 1)
            for t in va:
                pool.memset(t[:, :, :, :], 1.0).then_inc(edges, 1)

        @block.tensor
        def _(pe):
            pe.wait_ge(edges, 4)
            with pe.Fori(0, TILES // 2) as i:
                for u in range(2):
                    pe.wait_ge(h_made, 2 * i + u + 1)
                    pe.wait_ge(hT_made, 2 * i)
                    for half in range(CH):
                        mm = pe.transpose(ps_h[u][:, half * P:(half + 1) * P], h[u][:, half * P:(half + 1) * P], keep.ident[:, :])
                    mm.then_inc(hT_mm, 1)
            pe.wait_ge(consts, 176)
            pe.wait_ge(hT_made, TILES)

            def turn_v(c, m):
                pe.wait_ge(act_got, STEPS * c + 4 + m + 1)
                for j in range(2):
                    pe.wait_ge(va_made, 4 * c + max(2 * m + j - 1, 0))
                    for i in range(4):
                        mm = pe.transpose(ps_v[j][:, i * P:(i + 1) * P], vT[m][:, (4 * j + i) * P:(4 * j + i + 1) * P],
                                          keep.ident[:, :])
                    mm.then_inc(vT_mm, 1)

            with pe.Fori(0, QBS) as c:
                for k in range(STEPS):
                    kind, m = divmod(k, 2)
                    pe.wait_ge(act_got, STEPS * c + max(k - 1, 0))
                    if k >= 2:
                        pe.wait_ge(lo_made, 4 * c + k - 1)
                    for half in range(QB // CHUNK):
                        for j in range(3 * CH):
                            tap, ch = divmod(j, CH)
                            mm = pe.matmul(ps_c[k % 2][:, half * CHUNK:(half + 1) * CHUNK], w[:, kind, tap, ch, m * P:(m + 1) * P],
                                           hT[:, ch, bass.ds(c * QB + half * CHUNK + tap, CHUNK)],
                                           start=(j == 0), stop=(j == 3 * CH - 1))
                    mm.then_inc(conv_mm, 1)
                for m in range(CH):
                    turn_v(c, m)

        @block.scalar
        def _(act):
            norm.act(act)
            with act.Fori(0, TILES // 2) as i:
                for u in range(2):
                    act.wait_ge(hT_mm, 2 * i + u + 1)
                    act.activation(hT[:, :, bass.ds(2 * i * P + u * P + 1, P)], ps_h[u][:, 0:C].rearrange("p (h n) -> p h n", h=CH),
                                   ACT.Copy).then_inc(hT_made, 1)
            act.wait_ge(consts, 176)
            with act.Fori(0, QBS) as c:
                for k in range(STEPS):
                    kind, m = divmod(k, 2)
                    act.wait_ge(conv_mm, STEPS * c + k + 1)
                    if kind < 2:
                        act.wait_ge(parts_out[k % 2], 96 * c + 48 * kind)
                        out = hi[k % 2][:, :]
                    else:
                        act.wait_ge(vT_mm, 4 * c)
                        out = vT[m][:, :]
                    act.activation(out, ps_c[k % 2][:, :], ACT.Identity, bias=wb[:, kind, m:m + 1]).then_inc(act_got, 1)

        @block.vector
        def _(dve):
            dve.wait_ge(x_in, 16)
            norm.dve(dve, x, 1e-5)
            dve.wait_ge(consts, 176)
            with dve.Fori(0, TILES // 2) as i:
                for u in range(2):
                    n = 2 * i + u
                    xt = x[:, bass.ds(n, 1), :].rearrange("p a n -> p (a n)")
                    dve.wait_ge(hT_mm, 2 * i)
                    dve.tensor_scalar(h[u][:, :], xt, norm.mean[:, bass.ds(n, 1)], norm.rstd[:, bass.ds(n, 1)],
                                      ALU.subtract, ALU.mult).then_inc(h_made, 1)
                    dve.wait_ge(h_made, n + 1)
                    t = Tally(dve, norm.chain, norm.steps + n)
                    t.link(dve.tensor_tensor(xt, xt, h[u][:, :], ALU.add))
                    dve.tensor_tensor(xt, xt, bo[:, :], ALU.add).then_inc(base_made, 1)
            with dve.Fori(0, QBS) as c:
                for k in range(4):
                    kind, m = divmod(k, 2)
                    dve.wait_ge(act_got, STEPS * c + k + 1)
                    dve.wait_ge(parts_out[k % 2], 96 * c + 48 * kind)
                    dve.scalar_tensor_tensor(out=lo[k % 2][:, :], in0=ps_c[k % 2][:, :], scalar=wb[:, kind, m:m + 1],
                                             in1=hi[k % 2][:, :].bitcast(F32), op0=ALU.add, op1=ALU.subtract)\
                        .then_inc(lo_made, 1)
                for m in range(CH):
                    dve.wait_ge(va_out[m], 16 * c)
                    for j in range(2):
                        dve.wait_ge(vT_mm, 4 * c + 2 * m + j + 1)
                        dve.tensor_copy(va[m][:, :, 4 * j:4 * j + 4, 0:HD].rearrange("p h k n -> p k h n"),
                                        ps_v[j][:, :].rearrange("p (k h n) -> p k h n", k=4, h=4)).then_inc(va_made, 1)


class Norm:

    def __init__(self, r, tiles):
        self.tiles = tiles
        self.stats = r.sb("stats", [P, tiles, 6])
        self.mean, self.diff, self.var, self.std, self.rstd = (r.sb(n, [P, tiles]) for n in ("mean", "diff", "var", "std", "rstd"))
        self.chain, self.var_made, self.std_made = r.sem("chain"), r.sem("var_made"), r.sem("std_made")
        self.steps = tiles + 6

    def dve(self, dve, x, eps):
        t = Tally(dve, self.chain)
        for i in range(self.tiles):
            t.inc(dve.bn_stats(self.stats[:, i, :], x[:, i, :]))
        dve.wait_ge(self.chain, self.tiles)
        even, odd = self.stats[:, :, 0:3], self.stats[:, :, 3:6]
        t.link(dve.tensor_tensor(self.diff[:, :], even[:, :, 1], odd[:, :, 1], ALU.subtract))
        t.link(dve.scalar_tensor_tensor(out=self.mean[:, :], in0=self.diff[:, :], scalar=0.5, in1=odd[:, :, 1],
                                        op0=ALU.mult, op1=ALU.add))
        t.link(dve.tensor_tensor(self.var[:, :], even[:, :, 2], odd[:, :, 2], ALU.add))
        t.link(dve.scalar_tensor_tensor(out=self.diff[:, :], in0=self.diff[:, :], scalar=float(C) / 4, in1=self.diff[:, :],
                                        op0=ALU.mult, op1=ALU.mult))
        t.link(dve.tensor_tensor(self.var[:, :], self.var[:, :], self.diff[:, :], ALU.add))
        dve.tensor_scalar(self.var[:, :], self.var[:, :], 1.0 / C, eps, ALU.mult, ALU.add).then_inc(self.var_made, 1)
        dve.wait_ge(self.std_made, 1)
        t.link(dve.reciprocal(self.rstd[:, :], self.std[:, :]))
        assert t.n == self.steps

    def act(self, act):
        act.wait_ge(self.var_made, 1)
        act.activation(self.std[:, :], self.var[:, :], ACT.Sqrt).then_inc(self.std_made, 1)


class Attention:

    def __init__(self, nc, stack, s, keep, b):
        r = Room(nc, stack, f"a{b}")
        self.s, self.keep, self.b = s, keep, b
        self.k = [r.sb(f"k{i}", [ROWS, N], F32R) for i in range(2)]
        self.q = [r.sb(f"q{i}", [ROWS, QB], F32R) for i in range(2)]
        self.v = [r.sb(f"v{i}", [P, N // P, 2 * HD]) for i in range(2)]
        self.p = [r.sb(f"p{i}", [P, QB]) for i in range(P_SLOTS)]
        self.chunk_max = r.sb("chunk_max", [P, QB // P, CHUNKS])
        self.row_max = r.sb("row_max", [P, QB // P])
        self.shift = r.sb("shift", [P, QB // P, 2], F32R)
        self.sums = r.sb("sums", [P, CHUNK])
        self.inv = r.sb("inv", [P, CHUNK])
        self.ctx = [r.sb(f"ctx{i}", [HD, QB]) for i in range(2)]
        self.k_in = [r.sem(f"k_in{i}") for i in range(2)]
        self.q_in = [r.sem(f"q_in{i}") for i in range(2)]
        self.ones, self.s_mm, self.exped, self.p_used = r.sem("ones"), r.sem("s_mm"), r.sem("exped"), r.sem("p_used")
        self.max_mm, self.max_got, self.shift_made, self.shift_in = (r.sem(n) for n in ("mmm", "mg", "sm", "si"))
        self.ctx_got, self.ctx_made = r.sem("cg"), r.sem("cm")
        self.ctx_out = [r.sem(f"ctx_out{i}") for i in range(2)]
        self.chain = r.sem("chain")
        

    def max_bank(self, c):
        return self.ps_max[c % len(self.ps_max)]

    def load_q(self, sp, n, u):
        sp.dma_start(self.q[u][0:3 * HD, :].bitcast(F32), self.s["q"][self.b, bass.ds(n, 1)].rearrange("a r n -> (a r) n"))\
            .then_inc(self.q_in[u], 16)

    def load_kv(self, sp, h, par):
        sp.dma_start(self.k[par][0:3 * HD, :].bitcast(F32), self.s["k"][self.b, bass.ds(h, 1)].rearrange("a r n -> (a r) n"))\
            .then_inc(self.k_in[par], 16)
        sp.dma_start(self.v[par][:, :, :].rearrange("p k n -> p (k n)"), self.s["v"][self.b, bass.ds(h, 1)]
                     .rearrange("a p n -> (a p) n")).then_inc(self.k_in[par], 16)

    def first_loads(self, sp):
        self.load_kv(sp, 0, 0)
        self.load_q(sp, 0, 0)
        self.load_q(sp, 1, 1)

    def kv_step(self, sp, h, n, par, last):
        sp.wait_ge(self.p_used, BLOCKS * n + P_SLOTS)
        self.load_kv(sp, h if last else h + 1, 1 - par)

    def sync_step(self, sp, h, n, j, last):
        u = j % 2
        sp.wait_ge(self.s_mm, BLOCKS * n + BLOCKS)
        self.load_q(sp, n if last and j >= 2 else n + 2, u)
        sp.wait_ge(self.ctx_made, n + 1)
        sp.dma_start(self.s["ctx"][self.b, bass.ds(h, 1), :, j * QB:(j + 1) * QB].rearrange("a r n -> (a r) n"),
                     self.ctx[u][:, :]).then_inc(self.ctx_out[u], 16)

    def end_sync(self, sp):
        for u in range(2):
            sp.wait_ge(self.ctx_out[u], 16 * STEPS_A // 2)
            sp.wait_ge(self.q_in[u], 16 * (STEPS_A // 2 + 1))
        sp.wait_ge(self.k_in[0], 32 * 5)
        sp.wait_ge(self.k_in[1], 32 * 4)

    def set_ones(self, pool):
        for k in self.k:
            pool.memset(k[3 * HD:ROWS, :].bitcast(F32), 1.0).then_inc(self.ones, 1)

    def pe_begin(self, pe):
        pe.wait_ge(self.ones, 2)
        pe.wait_ge(self.q_in[0], 16)
        pe.wait_ge(self.k_in[0], 32)
        pe.sem_inc(self.p_used, P_SLOTS)

    def max_chunks(self, pe, base, q, k, a, b):
        for c in range(a, b):
            t, j = divmod(c, CHUNKS)
            pe.wait_ge(self.max_got, base + c + 1)
            pe.matmul(self.max_bank(c), q[0:3 * HD, t * P:(t + 1) * P], k[0:3 * HD, j * CHUNK:(j + 1) * CHUNK],
                      start=True, stop=True).then_inc(self.max_mm, 1)

    def turn_shift(self, pe, base, n):
        pe.wait_ge(self.shift_made, n + 1)
        for j in range(2):
            c = 64 + j
            pe.wait_ge(self.max_got, base + c + 1)
            for i in range(4):
                mm = pe.transpose(self.max_bank(c)[0:2, i * P:(i + 1) * P], self.shift[:, 4 * j + i, :].bitcast(F32),
                                  self.keep.ident[:, :])
            mm.then_inc(self.max_mm, 1)

    def weigh(self, pe, n, k, q, kb):
        if kb == 0:
            pe.wait_ge(self.shift_in, n + 1)
        pe.wait_ge(self.exped, BLOCKS * n + kb + 1)
        for i in range(2):
            mm = pe.matmul(self.ps_s[kb % 2][:, i * CHUNK:(i + 1) * CHUNK], k[:, kb * P:(kb + 1) * P],
                           q[:, i * CHUNK:(i + 1) * CHUNK], start=True, stop=True)
        mm.then_inc(self.s_mm, 1)

    def sum_block(self, pe, n, v, kb):
        if kb == 0:
            pe.wait_ge(self.ctx_got, n)
        pe.wait_ge(self.exped, BLOCKS * n + kb + 3)
        for i in range(2):
            mm = pe.matmul(self.ps_ctx[i * 2 * HD:(i + 1) * 2 * HD, :], v[:, kb, :], self.p[kb % P_SLOTS][:, i * CHUNK:(i + 1) * CHUNK],
                           start=(kb == 0), stop=(kb == BLOCKS - 1))
        mm.then_inc(self.p_used, 1)

    def next_waits(self, pe, hp, par, j):
        pe.wait_ge(self.q_in[1 - j % 2], self.q_count(hp, par, j))
        if j == 3:
            pe.wait_ge(self.k_in[1 - par], 32 * hp + 32 * (1 + par))

    def q_count(self, hp, par, j):
        return 16 * (4 * hp + 2 * par + (j + 1) // 2 + 1)

    def act_begin(self, act):
        act.sem_inc(self.exped, 2)

    def exp_block(self, act, n, kb):
        act.wait_ge(self.s_mm, BLOCKS * n + kb + 1)
        act.wait_ge(self.p_used, BLOCKS * n + kb + 1)
        act.activation(self.p[kb % P_SLOTS][:, :], self.ps_s[kb % 2], ACT.Exp, scale=float(HD) ** -0.5).then_inc(self.exped, 1)

    def copy_sums(self, act, n):
        act.wait_ge(self.p_used, BLOCKS * n + BLOCKS + P_SLOTS)
        act.wait_ge(self.ctx_made, n)
        act.activation(self.sums[:, :], self.ps_ctx, ACT.Copy).then_inc(self.ctx_got, 1)

    def dve_begin(self, dve):
        dve.sem_inc(self.max_got, len(self.ps_max))

    def max_got_chunks(self, dve, base, a, b):
        for c in range(a, b):
            t, j = divmod(c, CHUNKS)
            dve.wait_ge(self.max_mm, base + c + 1)
            dve.tensor_reduce(self.chunk_max[:, t, j:j + 1], self.max_bank(c), AX_X, ALU.max).then_inc(self.max_got, 1)

    def make_shift(self, dve, base, t):
        dve.wait_ge(self.max_got, base + 64 + len(self.ps_max))
        t.link(dve.tensor_reduce(self.row_max[:, :], self.chunk_max[:, :, :], AX_X, ALU.max))
        t.link(dve.tensor_scalar(self.shift[:, :, 0], self.row_max[:, :], -1.0, None, ALU.mult))
        dve.scalar_tensor_tensor(out=self.shift[:, :, 1], in0=self.row_max[:, :], scalar=-1.0,
                                 in1=self.shift[:, :, 0].bitcast(F32), op0=ALU.mult, op1=ALU.subtract).then_inc(self.shift_made, 1)

    def place_shift(self, dve, base, q):
        for j in range(2):
            dve.wait_ge(self.max_mm, base + 65 + j)
            dve.tensor_copy(q[3 * HD:ROWS, j * CHUNK:(j + 1) * CHUNK], self.max_bank(64 + j)[0:2, :]).then_inc(self.max_got, 1)
        dve.wait_ge(self.max_got, base + 66 + len(self.ps_max))
        dve.sem_inc(self.shift_in, 1)

    def normalize_piece(self, dve, n, u, turns, piece, t):
        step = CHUNK // (NORM - 1)
        if piece == 0:
            dve.wait_ge(self.ctx_got, n + 1)
        if piece < NORM - 1:
            at = slice(piece * step, (piece + 1) * step)
            t.inc(dve.reciprocal(self.inv[:, at], self.sums[:, at]))
            return
        dve.wait_ge(self.chain, t.base + t.n)
        dve.wait_ge(self.ctx_out[u], turns)
        for i in range(2):
            lo = 2 * HD * i
            t.link(dve.tensor_tensor(self.ctx[u][:, i * CHUNK:(i + 1) * CHUNK], self.sums[lo:lo + HD, :],
                                    self.inv[lo + HD:lo + 2 * HD, :], ALU.mult))
        dve.sem_inc(self.ctx_made, 1)


def chunks_by(kb, sampling):
    if not sampling:
        return 2 * kb if kb <= NORM else min(64, 2 * NORM + (64 - 2 * NORM) * (kb - NORM) // (28 - NORM))
    return min(64, 2 * (kb + sum(kb > slot for slot in (9, HALF + 9))))


def stage_attention(nc, d, s, keep, b, sample=None):
    with Stage(nc) as stack:
        at = Attention(nc, stack, s, keep, b)
        r = Room(nc, stack, f"at{b}")
        at.ps_s = [r.ps(f"s{i}", [P, QB])[:, :] for i in range(2)]
        at.ps_max = [r.ps(f"max{i}", [P, CHUNK])[:, :] for i in range(3 if sample is None else 2)]
        at.ps_ctx = r.ps("ctx", [P, CHUNK])[:, :]
        sa = None
        if sample is not None:
            sa = Sampling(nc, stack, d, s, keep, sample)
            sa.ps_in_one_bank(r)
        block = stack.enter_context(nc.Block())
        PARTS = 12
        FIRST = HALF + 1
        LAST = TILES - 1
        TURN = BLOCKS if sa else 29
        LINKS = NORM + 3

        def chunks(kb):
            return (chunks_by(kb - 1, sa is not None), chunks_by(kb, sa is not None)) if kb else (0, 0)

        @block.sync
        def _(sp):
            at.first_loads(sp)
            if sa:
                sa.load_constants(sp)
                for u in range(2):
                    sa.load_tile(sp, u, u)
                    sa.load_x(sp, u, u)

            def pair(hp, first, last):
                for par in range(2):
                    for j in range(4):
                        n, u = 8 * hp + 4 * par + j, j % 2
                        ends = last and par == 1
                        if j == 0:
                            at.kv_step(sp, 2 * hp + par, n, par, ends)
                        if sa and not (first and par == 0 and j == 0):
                            sa.store_tile(sp, n - 1, 1 - u)
                            if not (ends and j == 3):
                                sa.load_x(sp, n + 1, 1 - u)
                        if sa and not (ends and j >= 2):
                            sa.reload(sp, n, u)
                        at.sync_step(sp, 2 * hp + par, n, j, ends)

            pair(0, True, False)
            with sp.Fori(1, HEADS // 2 - 1) as hp:
                pair(hp, False, False)
            pair(HEADS // 2 - 1, False, True)
            at.end_sync(sp)
            if sa:
                sa.store_tile(sp, LAST, LAST % 2)
                sa.wait_stores(sp)

        @block.gpsimd
        def _(pool):
            at.set_ones(pool)
            if sa:
                with pool.Fori(0, TILES // 2) as i:
                    for u in range(2):
                        for g in range(G):
                            sa.gather(pool, 2 * i + u, i, u, g)

        @block.tensor
        def _(pe):
            at.pe_begin(pe)
            if sa:
                sa.pe_begin(pe)
            at.max_chunks(pe, 0, at.q[0], at.k[0], 0, 64)
            at.turn_shift(pe, 0, 0)

            def tile_parts(n, kb, first):
                if kb < PARTS and not first:
                    sa.sum_values(pe, n - 1, 1, kb, PARTS)
                if kb == PARTS + 1 and not first:
                    sa.project(pe, n - 1)
                if FIRST <= kb < FIRST + PARTS:
                    sa.sum_values(pe, n, 0, kb - FIRST, PARTS)

            def pair(hp, first):
                for par in range(2):
                    for j in range(4):
                        u, n = j % 2, 8 * hp + 4 * par + j
                        base = 66 * (n + 1)
                        nq, nk = at.q[1 - u], at.k[par if j < 3 else 1 - par]
                        for kb in range(BLOCKS):
                            done, upto = chunks(kb)
                            if kb == 1:
                                at.next_waits(pe, hp, par, j)
                            at.weigh(pe, n, at.k[par], at.q[u], kb)
                            at.max_chunks(pe, base, nq, nk, done, min(done + 1, upto))
                            if kb >= LAG:
                                at.sum_block(pe, n, at.v[par], kb - LAG)
                            at.max_chunks(pe, base, nq, nk, min(done + 1, upto), min(done + 2, upto))
                            if sa:
                                tile_parts(n, kb, first and par == 0 and j == 0)
                            at.max_chunks(pe, base, nq, nk, min(done + 2, upto), upto)
                            if kb == TURN:
                                at.turn_shift(pe, base, n + 1)
                        at.sum_block(pe, n, at.v[par], BLOCKS - 2)
                        if TURN == BLOCKS:
                            at.turn_shift(pe, base, n + 1)
                        at.sum_block(pe, n, at.v[par], BLOCKS - 1)

            pair(0, True)
            with pe.Fori(1, HEADS // 2) as hp:
                pair(hp, False)
            if sa:
                for part in range(PARTS):
                    sa.sum_values(pe, LAST, 1, part, PARTS)
                sa.project(pe, LAST)

        @block.scalar
        def _(act):
            at.act_begin(act)

            def step(n, first):
                for kb in range(BLOCKS):
                    at.exp_block(act, n, kb)
                    if kb == 0 and not first:
                        at.copy_sums(act, n - 1)
                    if sa:
                        for half in range(2):
                            if kb == HALF * half + 10:
                                sa.exps(act, n, half)
                        if kb == PARTS and not first:
                            sa.copy_out(act, n - 1, 1)
                        if kb == FIRST + PARTS:
                            sa.copy_out(act, n, 0)

            step(0, True)
            with act.Fori(1, STEPS_A) as n:
                step(n, False)
            at.copy_sums(act, STEPS_A - 1)
            if sa:
                sa.copy_out(act, LAST, 1)

        @block.vector
        def _(dve):
            at.dve_begin(dve)
            if sa:
                sa.begin(dve)
            t = Tally(dve, at.chain)
            at.max_got_chunks(dve, 0, 0, 64)
            at.make_shift(dve, 0, t)
            at.place_shift(dve, 0, at.q[0])

            def step(i, u, n, first):
                base = 66 * (n + 1)
                t = Tally(dve, at.chain, 2 + LINKS * n)
                ts = sa and sa.tally(dve, n)
                for kb in range(1, BLOCKS):
                    at.max_got_chunks(dve, base, *chunks(kb))
                    if kb <= NORM and not first:
                        at.normalize_piece(dve, n - 1, 1 - u, 16 * (i - 1 + u), kb - 1, t)
                    if sa:
                        sa.piece(dve, ts, n, i, u, kb - 1)
                        if kb == FIRST - 1 and not first:
                            sa.add_residual(dve, n - 1, i - 1 + u, 1 - u)
                    if chunks(kb)[0] < 64 == chunks(kb)[1]:
                        at.make_shift(dve, base, t)
                at.place_shift(dve, base, at.q[1 - u])
                if first:
                    for _ in range(LINKS - 2):
                        dve.sem_inc(at.chain, 1)
                        t.n += 1
                assert t.n == LINKS and (not sa or ts.n == sa.STEPS), (t.n, ts.n)

            for u in range(2):
                step(0, u, u, u == 0)
            with dve.Fori(1, STEPS_A // 2) as i:
                for u in range(2):
                    step(i, u, 2 * i + u, False)
            t = Tally(dve, at.chain, 2 + LINKS * STEPS_A)
            for piece in range(NORM):
                at.normalize_piece(dve, STEPS_A - 1, 1, 16 * (STEPS_A // 2 - 1), piece, t)
            if sa:
                sa.add_residual(dve, LAST, LAST // 2, LAST % 2)


def stage_mix(nc, d, s, keep, b):
    with Stage(nc) as stack:
        r = Room(nc, stack, f"x{b}")
        SLOTS = 4
        ctx = r.sb("ctx", [P, CH, N + 2])
        w = r.sb("w", [P, 3, CH, C])
        x = r.sb("x", [P, TILES, C])
        oT = [r.sb(f"oT{i}", [P, CH, CHUNK]) for i in range(2)]
        h = [r.sb(f"h{i}", [P, C]) for i in range(SLOTS)]
        hT = [r.sb(f"hT{i}", [P, CH, P]) for i in range(2)]
        gw = r.sb("gw", [P, CH, E])
        gb = r.sb("gb", [P, E])
        norm = Norm(r, TILES)
        ps_o = [r.ps(f"ps_o{i}", [P, 512]) for i in range(2)]
        ps_t = [r.ps(f"ps_t{i}", [P, 512]) for i in range(2)]
        ps_h = [r.ps(f"ps_h{i}", [P, 512]) for i in range(2)]
        ps_g = r.ps("ps_g", [P, TILES * E])
        ctx_in, consts, x_in, edges = r.sem("ctx_in"), r.sem("consts"), r.sem("x_in"), r.sem("edges")
        o_mm, oT_made, t_mm, t_made, t_out = (r.sem(n) for n in ("o_mm", "oT_made", "t_mm", "t_made", "t_out"))
        h_made, hT_mm, hT_made, g_mm = (r.sem(n) for n in ("h_made", "hT_mm", "hT_made", "g_mm"))
        h_out = [r.sem(f"h_out{i}") for i in range(SLOTS)]
        block = stack.enter_context(nc.Block())
        TURNS = TILES // SLOTS

        @block.sync
        def _(sp):
            sp.dma_start(ctx[:, :, 1:N + 1], s["ctx"][b].rearrange("(a h) r n -> (h r) a n", a=CH)).then_inc(ctx_in, 16)
            sp.dma_start(x[:, :, :], s["base"][b].rearrange("t p n -> p t n")).then_inc(x_in, 16)
            for tap in range(3):
                sp.dma_start(w[:, tap, :, :], d["Wo"][tap].rearrange("(h p) n -> p h n", p=P)).then_inc(consts, 16)
            sp.dma_start(gw[:, :, :], d["gate_w"].rearrange("(h p) n -> p h n", p=P)).then_inc(consts, 16)
            sp.dma_start(gb[:, :], d["gate_b"].to_broadcast([P, E])).then_inc(consts, 16)
            sp.wait_ge(t_made, 2 * CHUNKS)
            sp.dma_start(s["t2"][b].rearrange("t p n -> p t n"), x[:, :, :]).then_inc(t_out, 16)
            with sp.Fori(0, TURNS) as i:
                for u in range(SLOTS):
                    sp.wait_ge(h_made, SLOTS * i + u + 1)
                    sp.dma_start(s["h2"][b, bass.ds(SLOTS * i + u, 1)].rearrange("a p n -> (a p) n"), h[u][:, :])\
                        .then_inc(h_out[u], 16)
            sp.wait_ge(t_out, 16)
            for u in range(SLOTS):
                sp.wait_ge(h_out[u], 16 * TURNS)

        @block.gpsimd
        def _(pool):
            pool.memset(ctx[:, :, 0:1], 0.0).then_inc(edges, 1)
            pool.memset(ctx[:, :, N + 1:N + 2], 0.0).then_inc(edges, 1)

        @block.tensor
        def _(pe):
            pe.wait_ge(edges, 2)
            pe.wait_ge(consts, 80)
            pe.wait_ge(ctx_in, 16)
            with pe.Fori(0, CHUNKS // 2) as i:
                for u in range(2):
                    c = 2 * i + u
                    pe.wait_ge(oT_made, 2 * c)
                    for m in range(CH):
                        for j in range(3 * CH):
                            tap, ch = divmod(j, CH)
                            mm = pe.matmul(ps_o[m][:, :], w[:, tap, ch, m * P:(m + 1) * P],
                                           ctx[:, ch, bass.ds(2 * i * CHUNK + u * CHUNK + tap, CHUNK)],
                                           start=(j == 0), stop=(j == 3 * CH - 1))
                        mm.then_inc(o_mm, 1)
                    pe.wait_ge(oT_made, 2 * c + 2)
                    for half in range(2):
                        pe.wait_ge(t_made, 2 * c)
                        for k in range(2):
                            for m in range(CH):
                                at = (2 * half + k) * P
                                mm = pe.transpose(ps_t[half][:, k * C + m * P:k * C + (m + 1) * P], oT[u][:, m, at:at + P],
                                                  keep.ident[:, :])
                        mm.then_inc(t_mm, 1)

            def turn(n, u):
                pe.wait_ge(h_made, n + 1)
                for m in range(CH):
                    mm = pe.transpose(ps_h[u % 2][:, m * P:(m + 1) * P], h[u][:, m * P:(m + 1) * P], keep.ident[:, :])
                mm.then_inc(hT_mm, 1)

            def gate(n, u):
                pe.wait_ge(hT_made, n + 1)
                for m in range(CH):
                    mm = pe.matmul(ps_g[:, bass.ds(n * E, E)], hT[u % 2][:, m, :], gw[:, m, :], start=(m == 0), stop=(m == CH - 1))
                mm.then_inc(g_mm, 1)

            with pe.Fori(0, TURNS) as i:
                for u in range(0, SLOTS, 2):
                    for half in range(2):
                        turn(SLOTS * i + u + half, u + half)
                    for half in range(2):
                        gate(SLOTS * i + u + half, u + half)

        @block.scalar
        def _(act):
            with act.Fori(0, CHUNKS // 2) as i:
                for u in range(2):
                    c = 2 * i + u
                    act.wait_ge(t_mm, 4 * i)
                    for m in range(CH):
                        act.wait_ge(o_mm, 2 * c + m + 1)
                        act.activation(oT[u][:, m, :], ps_o[m][:, :], ACT.Copy).then_inc(oT_made, 1)
            norm.act(act)
            with act.Fori(0, TURNS) as i:
                for u in range(SLOTS):
                    act.wait_ge(hT_mm, SLOTS * i + u + 1)
                    act.wait_ge(g_mm, SLOTS * i + u // 2 * 2)
                    act.activation(hT[u % 2][:, :, :], ps_h[u % 2][:, 0:C].rearrange("p (h n) -> p h n", h=CH), ACT.Copy)\
                        .then_inc(hT_made, 1)

        @block.vector
        def _(dve):
            dve.wait_ge(consts, 80)
            dve.wait_ge(x_in, 16)
            with dve.Fori(0, CHUNKS) as c:
                for half in range(2):
                    dve.wait_ge(t_mm, 2 * c + half + 1)
                    two = x[:, bass.ds(4 * c + 2 * half, 2), :].rearrange("p t n -> p (t n)")
                    dve.tensor_tensor(two, ps_t[half][:, :], two, ALU.add).then_inc(t_made, 1)
            dve.wait_ge(t_made, 2 * CHUNKS)
            norm.dve(dve, x, 1e-5)
            with dve.Fori(0, TURNS) as i:
                for u in range(SLOTS):
                    n = SLOTS * i + u
                    dve.wait_ge(h_out[u], 16 * i)
                    dve.wait_ge(hT_mm, SLOTS * i)
                    dve.tensor_scalar(h[u][:, :], x[:, bass.ds(n, 1), :].rearrange("p a n -> p (a n)"),
                                      norm.mean[:, bass.ds(n, 1)], norm.rstd[:, bass.ds(n, 1)],
                                      ALU.subtract, ALU.mult).then_inc(h_made, 1)
            dve.wait_ge(g_mm, TILES)
            dve.tensor_tensor(keep.gate[:, b * TILES:(b + 1) * TILES, :], ps_g[:, :].rearrange("p (t e) -> p t e", e=E),
                              gb[:, :].unsqueeze(1).to_broadcast([P, TILES, E]), ALU.add)


def stage_route(nc, d, s, keep):
    with Stage(nc) as stack:
        r = Room(nc, stack, "r")
        ALL = B * TILES
        h = r.sb("h", [P, ALL, C])
        upper, ones = r.sb("upper", [P, P]), r.sb("ones", [P, P])
        prio, first = r.sb("prio", [P, E]), r.sb("first", [P, E])
        top, total, prob, best, expert, place, kept, row = (
            r.sb(n, [P, ALL]) for n in ("top", "total", "prob", "best", "expert", "place", "kept", "row"))
        exps, hot, rank, each, before, work = (r.sb(n, [P, ALL, E]) for n in ("exps", "hot", "rank", "each", "before", "work"))
        to_row = r.sb("to_row", [P, ALL], U32)
        ps_rank, ps_each = r.ps("ps_rank", [P, 512]), r.ps("ps_each", [P, 512])
        consts, h_in, chain = r.sem("consts"), r.sem("h_in"), r.sem("chain")
        less, exped, hot_made, counted, rows_made, sent = (r.sem(n) for n in ("less", "exped", "hot", "counted", "rows", "sent"))
        block = stack.enter_context(nc.Block())

        @block.sync
        def _(sp):
            for tile, name in ((upper, "upper"), (ones, "ones"), (prio, "prio"), (first, "first")):
                sp.dma_start(tile[:, :], d[name]).then_inc(consts, 16)
            sp.dma_start(h[:, :, :], s["h2"].rearrange("b t p n -> p (b t) n")).then_inc(h_in, 16)
            sp.wait_ge(h_in, 16)

        @block.scalar
        def _(act):
            act.wait_ge(less, 1)
            act.activation(exps[:, :, :], exps[:, :, :], ACT.Exp).then_inc(exped, 1)

        @block.tensor
        def _(pe):
            pe.wait_ge(consts, 64)
            pe.wait_ge(hot_made, 1)
            flat = hot[:, :, :].rearrange("p t e -> p (t e)")
            pe.matmul(ps_rank[:, :], upper[:, :], flat, start=True, stop=True)
            pe.matmul(ps_each[:, :], ones[:, :], flat, start=True, stop=True).then_inc(counted, 1)

        @block.vector
        def _(dve):
            t = Tally(dve, chain)

            def tokens(v):
                return v[:, :].unsqueeze(2).to_broadcast([P, ALL, E])

            def experts(v):
                return v[:, :].unsqueeze(1).to_broadcast([P, ALL, E])

            def tt(out, a, b, op):
                t.link(dve.tensor_tensor(out, a, b, op))

            gate = keep.gate[:, :, :]
            dve.wait_ge(consts, 64)
            t.link(dve.tensor_reduce(top[:, :], gate, AX_X, ALU.max))
            tt(hot[:, :, :], gate, tokens(top), ALU.is_equal)
            tt(hot[:, :, :], hot[:, :, :], experts(prio), ALU.mult)
            t.link(dve.tensor_reduce(best[:, :], hot[:, :, :], AX_X, ALU.max))
            tt(rank[:, :, :], hot[:, :, :], tokens(best), ALU.is_equal)
            dve.tensor_copy(hot[:, :, :], rank[:, :, :]).then_inc(hot_made, 1)
            dve.tensor_tensor(exps[:, :, :], gate, tokens(top), ALU.subtract).then_inc(less, 1)
            dve.wait_ge(exped, 1)
            t.link(dve.tensor_reduce(total[:, :], exps[:, :, :], AX_X, ALU.add))
            t.link(dve.reciprocal(prob[:, :], total[:, :]))
            dve.wait_ge(counted, 1)
            flat = "p t e -> p (t e)"
            t.link(dve.tensor_copy(each[:, :, :].rearrange(flat), ps_each[:, :]))
            t.link(dve.tensor_copy(before[:, :, :], each[:, :, :]))
            step, src, dst = 1, before, work
            while step < ALL:
                t.inc(dve.tensor_copy(dst[:, 0:step, :], src[:, 0:step, :]))
                tt(dst[:, step:, :], src[:, step:, :], src[:, 0:ALL - step, :], ALU.add)
                step, src, dst = 2 * step, dst, src
            tt(src[:, :, :], src[:, :, :], each[:, :, :], ALU.subtract)
            tt(src[:, :, :].rearrange(flat), src[:, :, :].rearrange(flat), ps_rank[:, :], ALU.add)
            dve.wait_ge(hot_made, 1)
            tt(src[:, :, :], src[:, :, :], hot[:, :, :], ALU.mult)
            t.link(dve.tensor_reduce(place[:, :], src[:, :, :], AX_X, ALU.add))
            tt(hot[:, :, :], hot[:, :, :], experts(first), ALU.mult)
            t.link(dve.tensor_reduce(expert[:, :], hot[:, :, :], AX_X, ALU.add))
            t.link(dve.tensor_scalar(kept[:, :], place[:, :], float(CAP), None, ALU.is_lt))
            tt(keep.answer_w[:, :], prob[:, :], kept[:, :], ALU.mult)
            t.link(dve.tensor_scalar(work[:, :, 0], kept[:, :], -float(2 * E * CAP), float(2 * E * CAP), ALU.mult, ALU.add))
            t.link(dve.tensor_scalar(place[:, :], place[:, :], float(CAP - 1), None, ALU.min))
            tt(row[:, :], expert[:, :], place[:, :], ALU.add)
            t.link(dve.tensor_copy(keep.answer_row[:, :], row[:, :]))
            dve.tensor_tensor(to_row[:, :], row[:, :], work[:, :, 0], ALU.add).then_inc(rows_made, 1)

        @block.gpsimd
        def _(pool):
            pool.wait_ge(rows_made, 1)
            pool.wait_ge(h_in, 16)
            for t in range(ALL):
                pool.indirect_dma_start(
                    out=s["buf"], out_offset=bass.IndirectOffsetOnAxis(ap=to_row[:, t:t + 1], axis=0),
                    in_=h[:, t, :], in_offset=None, bounds_check=E * CAP - 1, oob_is_err=False).then_inc(sent, 16)
            pool.wait_ge(sent, 16 * ALL)


def stage_experts(nc, d, s, keep):
    with Stage(nc) as stack:
        r = Room(nc, stack, "e")
        RT = CAP // P
        FT = F // P
        PIECES = [(a, min(a + CHUNK, CAP)) for a in range(0, CAP, CHUNK)]
        x = [r.sb(f"x{i}", [P, RT, C]) for i in range(2)]
        w1 = [r.sb(f"w1{i}", [P, CH, F]) for i in range(2)]
        w2 = [r.sb(f"w2{i}", [P, FT, C]) for i in range(2)]
        b1 = [r.sb(f"b1{i}", [P, FT]) for i in range(2)]
        b2 = [r.sb(f"b2{i}", [P, C]) for i in range(2)]
        xT = r.sb("xT", [P, CH, CAP])
        mid = r.sb("mid", [P, FT, CAP])
        y = [r.sb(f"y{i}", [P, RT, C]) for i in range(2)]
        ps_x = [r.ps(f"ps_x{i}", [P, 512]) for i in range(2)]
        ps_m = [r.ps(f"ps_m{i}", [P, 512]) for i in range(4)]
        ps_y = [r.ps(f"ps_y{i}", [P, 512]) for i in range(2)]
        in_sem = [r.sem(f"in{i}") for i in range(2)]
        xT_mm, xT_made, m_mm, m_made, y_mm, y_made = (r.sem(n) for n in ("xT_mm", "xT_made", "m_mm", "m_made", "y_mm", "y_made"))
        y_out = [r.sem(f"y_out{i}") for i in range(2)]
        block = stack.enter_context(nc.Block())
        LOADS = 5 * 16
        XS, MS = RT, FT * len(PIECES)
        TWO = E // 2

        @block.sync
        def _(sp):
            def load(e, u):
                one = bass.ds(e, 1)
                sp.dma_start(x[u][:, :, :], s["buf"].rearrange("(e t p) n -> e p t n", e=E, p=P)[one]
                             .rearrange("a p t n -> p (a t) n")).then_inc(in_sem[u], 16)
                sp.dma_start(w1[u][:, :, :], d["w1"][one].rearrange("a (h p) n -> p (a h) n", p=P)).then_inc(in_sem[u], 16)
                sp.dma_start(w2[u][:, :, :], d["w2"][one].rearrange("a (h p) n -> p (a h) n", p=P)).then_inc(in_sem[u], 16)
                sp.dma_start(b1[u][:, :], d["b1"][one].rearrange("a p n -> (a p) n")).then_inc(in_sem[u], 16)
                sp.dma_start(b2[u][:, :], d["b2"][one].rearrange("a n -> a n").to_broadcast([P, C])).then_inc(in_sem[u], 16)

            def store(e, u):
                sp.wait_ge(y_made, RT * e + RT)
                sp.dma_start(s["y"].rearrange("(e t p) n -> e p t n", e=E, p=P)[bass.ds(e, 1)]
                             .rearrange("a p t n -> p (a t) n"), y[u][:, :, :]).then_inc(y_out[u], 16)

            for u in range(2):
                load(u, u)
            with sp.Fori(0, TWO - 1) as i:
                for u in range(2):
                    store(2 * i + u, u)
                    load(2 * i + u + 2, u)
            for u in range(2):
                store(E - 2 + u, u)
            for u in range(2):
                sp.wait_ge(y_out[u], 16 * TWO)

        @block.tensor
        def _(pe):
            with pe.Fori(0, TWO) as i:
                for u in range(2):
                    e = 2 * i + u
                    pe.wait_ge(in_sem[u], LOADS * (i + 1))
                    for k in range(XS):
                        pe.wait_ge(xT_made, XS * e + max(k - 1, 0))
                        for h in range(CH):
                            mm = pe.transpose(ps_x[k % 2][:, h * P:(h + 1) * P], x[u][:, k, h * P:(h + 1) * P], keep.ident[:, :])
                        mm.then_inc(xT_mm, 1)
                    pe.wait_ge(xT_made, XS * e + XS)
                    for k in range(MS):
                        m, (a, z) = k // len(PIECES), PIECES[k % len(PIECES)]
                        pe.wait_ge(m_made, MS * e + max(k - 3, 0))
                        for h in range(CH):
                            mm = pe.matmul(ps_m[k % 4][:, 0:z - a], w1[u][:, h, m * P:(m + 1) * P], xT[:, h, a:z],
                                           start=(h == 0), stop=(h == CH - 1))
                        mm.then_inc(m_mm, 1)
                    pe.wait_ge(m_made, MS * e + MS)
                    for k in range(RT):
                        pe.wait_ge(y_made, RT * e + max(k - 1, 0))
                        for m in range(FT):
                            mm = pe.matmul(ps_y[k % 2][:, 0:C], mid[:, m, k * P:(k + 1) * P], w2[u][:, m, :],
                                           start=(m == 0), stop=(m == FT - 1))
                        mm.then_inc(y_mm, 1)

        @block.scalar
        def _(act):
            with act.Fori(0, TWO) as i:
                for u in range(2):
                    e = 2 * i + u
                    act.wait_ge(in_sem[u], LOADS * (i + 1))
                    act.wait_ge(m_mm, MS * e)
                    for k in range(XS):
                        act.wait_ge(xT_mm, XS * e + k + 1)
                        act.activation(xT[:, :, k * P:(k + 1) * P], ps_x[k % 2][:, 0:C].rearrange("p (h n) -> p h n", h=CH),
                                       ACT.Copy).then_inc(xT_made, 1)
                    act.wait_ge(y_mm, RT * e)
                    for k in range(MS):
                        m, (a, z) = k // len(PIECES), PIECES[k % len(PIECES)]
                        act.wait_ge(m_mm, MS * e + k + 1)
                        act.activation(mid[:, m, a:z], ps_m[k % 4][:, 0:z - a], ACT.Relu, bias=b1[u][:, m:m + 1]).then_inc(m_made, 1)

        @block.vector
        def _(dve):
            with dve.Fori(0, TWO) as i:
                for u in range(2):
                    e = 2 * i + u
                    dve.wait_ge(in_sem[u], LOADS * (i + 1))
                    dve.wait_ge(y_out[u], 16 * i)
                    for k in range(RT):
                        dve.wait_ge(y_mm, RT * e + k + 1)
                        dve.tensor_tensor(y[u][:, k, :], ps_y[k % 2][:, 0:C], b2[u][:, :], ALU.add).then_inc(y_made, 1)


def stage_combine(nc, d, s, keep, out):
    with Stage(nc) as stack:
        r = Room(nc, stack, "c")
        GT = 8
        GROUPS = B * TILES // GT
        t2 = r.sb("t2", [P, B * TILES, C])
        y = r.sb("y", [P, B * TILES, C])
        good = [r.sb(f"good{i}", [P, GT * C], U32) for i in range(2)]
        big = [r.sb(f"big{i}", [P, GT * C]) for i in range(2)]
        neg = [r.sb(f"neg{i}", [P, GT * C]) for i in range(2)]
        got = [r.sem(f"got{i}") for i in range(GROUPS)]
        t2_in, scaled, summed, out_sem, chain = r.sem("t2_in"), r.sem("scaled"), r.sem("summed"), r.sem("out"), r.sem("chain")
        block = stack.enter_context(nc.Block())

        @block.sync
        def _(sp):
            sp.dma_start(t2[:, :, :], s["t2"].rearrange("b t p n -> p (b t) n")).then_inc(t2_in, 16)
            for g in range(GROUPS):
                sp.wait_ge(summed, g + 1)
                sp.dma_start(out.rearrange("b (t p) n -> p (b t) n", p=P)[:, g * GT:(g + 1) * GT, :],
                             t2[:, g * GT:(g + 1) * GT, :]).then_inc(out_sem, 16)
            sp.wait_ge(out_sem, 16 * GROUPS)

        @block.gpsimd
        def _(pool):
            for t in range(B * TILES):
                pool.indirect_dma_start(out=y[:, t, :], out_offset=None, in_=s["y"],
                                        in_offset=bass.IndirectOffsetOnAxis(ap=keep.answer_row[:, t:t + 1], axis=0))\
                    .then_inc(got[t // GT], 16)

        @block.scalar
        def _(act):
            for g in range(GROUPS):
                act.wait_ge(got[g], 16 * GT)
                for t in range(g * GT, (g + 1) * GT):
                    act.activation(y[:, t, :], y[:, t, :], ACT.Copy, scale=keep.answer_w[:, t:t + 1]).then_inc(scaled, 1)

        @block.vector
        def _(dve):
            t = Tally(dve, chain)
            dve.wait_ge(t2_in, 16)
            for g in range(GROUPS):
                u = g % 2
                dve.wait_ge(scaled, GT * (g + 1))
                v = y[:, g * GT:(g + 1) * GT, :].rearrange("p t n -> p (t n)")
                res = t2[:, g * GT:(g + 1) * GT, :].rearrange("p t n -> p (t n)")
                t.inc(dve.tensor_scalar(good[u][:, :], v, 0.0, 0.0, ALU.mult, ALU.is_equal))
                t.inc(dve.tensor_scalar(big[u][:, :], v, 0.0, 1e4, ALU.is_gt, ALU.mult))
                t.link(dve.tensor_scalar(neg[u][:, :], v, 0.0, -1e4, ALU.is_lt, ALU.mult))
                t.link(dve.tensor_tensor(big[u][:, :], big[u][:, :], neg[u][:, :], ALU.add))
                t.link(dve.copy_predicated(big[u][:, :], good[u][:, :], v))
                dve.tensor_tensor(res, res, big[u][:, :], ALU.add).then_inc(summed, 1)


class Keep:

    def __init__(self, nc, stack):
        r = Room(nc, stack, "keep")
        self.ident = r.sb("ident", [P, P])
        self.gate = r.sb("gate", [P, B * TILES, E])
        self.answer_w = r.sb("answer_w", [P, B * TILES])
        self.answer_row = r.sb("answer_row", [P, B * TILES], U32)


class OffsetWeights:

    def __init__(self, nc, stack):
        r = Room(nc, stack, "off")
        self.off_w = r.sb("w", [P, CH, OFFS])
        self.taps = r.sb("taps", [P, TAPS, OFFS])


def scratch(nc):
    def dram(name, shape, dt=F32):
        return nc.dram_tensor(f"s_{name}", shape, dt).ap()

    return {
        "dwq": dram("dwq", [B, 4, P, (H + 2) * W]),
        "dwkv": dram("dwkv", [B, 2 * CH, P, KVPAD]),
        "rec": dram("rec", [B, TILES, P, REC]),
        "qpix": dram("qpix", [B, TILES, P, C]),
        "base": dram("base", [B, TILES, P, C]),
        "q": dram("q", [B, STEPS_A, 3 * HD, QB]),
        "k": dram("k", [B, HEADS, 3 * HD, N]),
        "v": dram("v", [B, HEADS, P, N // P * 2 * HD]),
        "ctx": dram("ctx", [B, HEADS, HD, N]),
        "t2": dram("t2", [B, TILES, P, C]),
        "h2": dram("h2", [B, TILES, P, C]),
        "buf": dram("buf", [E * CAP, C]),
        "y": dram("y", [E * CAP, C]),
        "x1": dram("x1", [B, TILES, P, C]),
        "table": [dram(f"table{b}", [TILES, P, G * 4 * 2 * HC]) for b in range(B)],
    }


def build(nc, d, out, upto=None, s=None):
    s = s or scratch(nc)
    with ExitStack() as stack:
        keep = Keep(nc, stack)
        stages = {
            "project0": lambda: stage_project(nc, d, s, keep, 0),
            "attention0": lambda: stage_attention(nc, d, s, keep, 0, sample=1),
            "project1": lambda: stage_project(nc, d, s, keep, 1),
            "attention1": lambda: stage_attention(nc, d, s, keep, 1),
            "mix0": lambda: stage_mix(nc, d, s, keep, 0),
            "mix1": lambda: stage_mix(nc, d, s, keep, 1),
            "route": lambda: stage_route(nc, d, s, keep),
            "experts": lambda: stage_experts(nc, d, s, keep),
            "combine": lambda: stage_combine(nc, d, s, keep, out),
        }
        with ExitStack() as early:
            offset_w = OffsetWeights(nc, early)
            first = {
                "maps": lambda: stage_maps(nc, d, s, keep, offset_w),
                "tables0": lambda: stage_tables(nc, d, s, keep, offset_w, 0),
                "sample0": lambda: stage_sample(nc, d, s, keep, offset_w, 0, tables=1),
            }
            for st in first:
                if upto is None or st in upto:
                    first[st]()
        for st in stages:
            if upto is None or st in upto:
                stages[st]()
    return s


def lay_out(inputs):
    import numpy as np

    a = {k: np.asarray(v) for k, v in inputs.items()}
    f = np.float32
    gx, gy = np.meshgrid(np.arange(W), np.arange(H), indexing="xy")
    pts = np.array([[i - 1, j - 1] for i in range(3) for j in range(3)])
    base = np.stack([pts * (2 * g + 1) for g in range(G)]).reshape(1, SAMPLES, 2)
    grid = np.stack([gx.reshape(-1), gy.reshape(-1)], -1)[:, None, :] + base
    io = {
        "x": a["x"].reshape(B, N, C),
        "xT": a["x"].reshape(B, N, C).transpose(0, 2, 1),
        "qkv_w": a["L0_conv_qkv_w"],
        "qkv_b": a["L0_conv_qkv_b"].reshape(MT, P).T,
        "dw_w": a["L0_conv_dw_w"].reshape(TAPS, MT, P).transpose(2, 1, 0),
        "dw_b": a["L0_conv_dw_b"].reshape(MT, P).T,
        "pconv": np.concatenate([a["L0_conv_off_pconv_w"], a["L0_conv_mask_pconv_w"][None]])
        .reshape(G + 1, CQ, CQ, TAPS).transpose(1, 0, 3, 2),
        "off_wT": np.concatenate([a["L0_conv_off_w"].reshape(2 * SAMPLES, C), a["L0_conv_mask_w"]]).T,
        "off_b": np.concatenate([a["L0_conv_off_b"].reshape(-1), a["L0_conv_mask_b"]]).reshape(1, OFFS),
        "grid": grid.reshape(TILES, P, 2 * SAMPLES).transpose(1, 0, 2).astype(f),
        "gcol": np.tile(np.repeat(np.arange(G), K), (P, 1)).astype(f),
        "proj_w": a["L0_conv_proj_w"],
        "proj_b": a["L0_conv_proj_b"].reshape(1, C),
        "Wq": a["L1_attn_Wq"],
        "Wk": a["L1_attn_Wk"],
        "Wv": a["L1_attn_Wv"],
        "Wo": a["L1_attn_Wo"],
        "bqkv": np.stack([a[f"L1_attn_b{n}"] for n in "qkv"]).reshape(3, CH, P).transpose(2, 0, 1),
        "bo": a["L1_attn_bo"].reshape(1, C),
        "gate_w": a["L1_ffn_gate_w"],
        "gate_b": a["L1_ffn_gate_b"].reshape(1, E),
        "w1": a["L1_ffn_w1"],
        "b1": a["L1_ffn_b1"].reshape(E, F // P, P).transpose(0, 2, 1),
        "w2": a["L1_ffn_w2"],
        "b2": a["L1_ffn_b2"],
        "upper": np.triu(np.ones((P, P), f), 1),
        "ones": np.ones((P, P), f),
        "prio": np.tile(E - np.arange(E), (P, 1)).astype(f),
        "first": np.tile(CAP * np.arange(E), (P, 1)).astype(f),
        "ident": np.eye(P, dtype=f),
        "grp": (np.kron(np.eye(P // 8), np.ones((8, 8))) / 8).astype(f),
    }
    return {k: np.ascontiguousarray(v) for k, v in io.items()}


def kernel(**inputs):
    import numpy as np
    import concourse.bacc as bacc
    from concourse import mybir as mb
    from concourse.bass_utils import run_bass_kernel_spmd

    nc = bacc.Bacc("TRN2", target_bir_lowering=False, num_devices=1)
    arrays, d = {}, {}
    for name, a in lay_out(inputs).items():
        arrays[f"in_{name}"] = a
        d[name] = nc.dram_tensor(f"in_{name}", a.shape, mb.dt.from_np(a.dtype), kind="ExternalInput").ap()
    out = nc.dram_tensor("out", [B, N, C], F32, kind="ExternalOutput").ap()
    build(nc, d, out)
    r = run_bass_kernel_spmd(nc, [arrays], core_ids=[0])
    return np.asarray(r.results[0]["out"]).reshape(B, H, W, C)
```
